# Optimizing a Trainium2 kernel written in Bass

```python
import numpy as np
import jax
import jax.numpy as jnp

def _softmax(x, axis=-1):
    return jax.nn.softmax(x, axis=axis)

def _gelu(x):
    return jax.nn.gelu(x, approximate=True)

def _silu(x):
    return jax.nn.silu(x)

def _sigmoid(x):
    return jax.nn.sigmoid(x)

def _layernorm(x, axis=-1, eps=1e-05):
    m = jnp.mean(x, axis=axis, keepdims=True)
    v = jnp.var(x, axis=axis, keepdims=True)
    return (x - m) / jnp.sqrt(v + eps)

def _scatter_add(tgt, idx, src, axis=0):
    return tgt.at[idx].add(src)

def _segment_sum(src, seg, n):
    return jax.ops.segment_sum(src, seg, n)
kernel_name = 'mk_flamingo_gated_d2_seqx_r8_51db41'

def setup_inputs(seed: int=0):
    np.random.seed(seed)
    _w = jnp.asarray

    def _rec_inputs():
        import jax
        import jax.numpy as jnp
        _rk = jax.random.key(seed)
        x = 4.136e-05 + 0.9999 * jax.random.normal(jax.random.fold_in(_rk, 1), (4, 256, 256), jnp.float32)
        _lenS = 256 - jax.random.randint(jax.random.fold_in(_rk, 7), (4,), 0, max(1, 256 // 4) + 1, jnp.int32)
        _lenS2 = 256 - jax.random.randint(jax.random.fold_in(_rk, 8), (4,), 0, max(1, 256 // 4) + 1, jnp.int32)
        _ctx_1024P = jax.random.normal(jax.random.fold_in(_rk, 11), (4, 16, 128), jnp.float32)
        _ctx_1024c = jax.random.dirichlet(jax.random.fold_in(_rk, 511), 0.3 * jnp.ones((16,), jnp.float32), (4, 256))
        _ctx_1024t = jnp.einsum('bsk,bkd->bsd', _ctx_1024c, _ctx_1024P)
        _ctx_1024t = _ctx_1024t * jax.lax.rsqrt(jnp.mean(jnp.square(_ctx_1024t)) + 1e-12) * 0.953939
        ctx_1024 = -0.000292821 + 1.00034 * (_ctx_1024t + 0.3 * jax.random.normal(jax.random.fold_in(_rk, 611), (4, 256, 128), jnp.float32))
        _g = jax.random.normal(jax.random.fold_in(_rk, 9001), (2, 2), jnp.float32)
        _g = jnp.sign(_g) * jnp.maximum(jnp.abs(_g), 1.0) + (_g == 0) * 1.0
        g_xattn = _g[0]
        g_ffn = _g[1]
        return (x, ctx_1024, g_xattn, g_ffn)
    x, ctx_1024, g_xattn, g_ffn = _rec_inputs()

    def _L0_xattn_setup():
        import jax, jax.numpy as jnp
        import numpy as np
        import math
        B, L, DM = (2, 256, 128)
        DS, DC, EXP = (16, 4, 2)
        DI = EXP * DM
        DR = math.ceil(DM / 16)
        DT_MIN, DT_MAX, DT_FLOOR = (0.001, 0.1, 0.0001)

        def _ssm_forward(hidden_states, z, in_proj_w, conv_w, conv_b, x_proj_w, dt_proj_w, dt_proj_b, A_log, D):
            b = hidden_states.shape[0]
            x = jnp.einsum('ed,bld->bel', in_proj_w, hidden_states)
            xp = jnp.pad(x, ((0, 0), (0, 0), (DC - 1, 0)))
            xc = jax.lax.conv_general_dilated(xp, conv_w[:, None, :], window_strides=(1,), padding='VALID', dimension_numbers=('NCH', 'OIH', 'NCH'), feature_group_count=DI)
            u = jax.nn.silu(xc + conv_b[None, :, None])
            x_dbl = jnp.einsum('ke,bel->bkl', x_proj_w, u)
            dt_lo = x_dbl[:, :DR]
            Bm = x_dbl[:, DR:DR + DS]
            Cm = x_dbl[:, DR + DS:]
            delta = jax.nn.softplus(jnp.einsum('er,brl->bel', dt_proj_w, dt_lo) + dt_proj_b[None, :, None])
            A = -jnp.exp(A_log)

            def step(state, xs):
                d_t, B_t, C_t, u_t = xs
                dA = jnp.exp(d_t[..., None] * A)
                state = state * dA + (d_t * u_t)[..., None] * B_t[:, None, :]
                y_t = jnp.einsum('ben,bn->be', state, C_t)
                return (state, y_t)
            xs = (jnp.moveaxis(delta, -1, 0), jnp.moveaxis(Bm, -1, 0), jnp.moveaxis(Cm, -1, 0), jnp.moveaxis(u, -1, 0))
            state0 = jnp.zeros((b, DI, DS), delta.dtype)
            _, ys = jax.lax.scan(step, state0, xs)
            y = jnp.moveaxis(ys, 0, -1)
            y = y + D[None, :, None] * u
            y = y * jax.nn.silu(z)
            return jnp.swapaxes(y, 1, 2)
        key = jax.random.key(seed)
        ks = jax.random.split(key, 8)
        hidden_states = jax.random.normal(ks[0], (B, L, DM), jnp.float32)
        z = jax.random.normal(ks[1], (B, DI, L), jnp.float32)
        in_proj_w = jax.random.normal(ks[2], (DI, DM), jnp.float32) * DM ** (-0.5)
        conv_w = jax.random.normal(ks[3], (DI, DC), jnp.float32) * DC ** (-0.5)
        conv_b = jnp.zeros((DI,), jnp.float32)
        x_proj_w = jax.random.normal(ks[4], (DR + 2 * DS, DI), jnp.float32) * DI ** (-0.5)
        dt_std = DR ** (-0.5)
        dt_proj_w = jax.random.uniform(ks[5], (DI, DR), jnp.float32, -dt_std, dt_std)
        dt = jnp.exp(jax.random.uniform(ks[6], (DI,), jnp.float32) * (math.log(DT_MAX) - math.log(DT_MIN)) + math.log(DT_MIN))
        dt = jnp.clip(dt, DT_FLOOR)
        dt_proj_b = dt + jnp.log(-jnp.expm1(-dt))
        A_log = jnp.log(jnp.broadcast_to(jnp.arange(1, DS + 1, dtype=jnp.float32), (DI, DS)))
        D = jnp.ones((DI,), jnp.float32)
        return dict(hidden_states=hidden_states, z=z, in_proj_w=in_proj_w, conv_w=conv_w, conv_b=conv_b, x_proj_w=x_proj_w, dt_proj_w=dt_proj_w, dt_proj_b=dt_proj_b, A_log=A_log, D=D)
    _L0_xattn_all = _L0_xattn_setup()
    _L0_xattn_in = {k: v for k, v in _L0_xattn_all.items() if k in ('in_proj_w', 'conv_w', 'conv_b', 'x_proj_w', 'dt_proj_w', 'dt_proj_b', 'A_log', 'D')}
    del _L0_xattn_all

    def _L0_ffn_setup():
        import jax, jax.numpy as jnp
        import numpy as np
        D_MODEL = 256
        D_HIDDEN = 176
        NUM_SHARED = 2
        NUM_ROUTED = 32
        TOP_K = 6

        def _expert_apply(xf, w1, b1, w2, b2):
            return jnp.maximum(xf @ w1 + b1, 0.0) @ w2 + b2
        key = jax.random.key(seed)
        ks = jax.random.split(key, 11)
        d, h = (D_MODEL, D_HIDDEN)
        s1 = 1.0 / np.sqrt(d)
        s2 = 1.0 / np.sqrt(h)
        x = jax.random.normal(ks[0], (2, 256, d), dtype=jnp.float32)
        sw1 = jax.random.uniform(ks[1], (NUM_SHARED, d, h), jnp.float32, -s1, s1)
        sb1 = jax.random.uniform(ks[2], (NUM_SHARED, h), jnp.float32, -s1, s1)
        sw2 = jax.random.uniform(ks[3], (NUM_SHARED, h, d), jnp.float32, -s2, s2)
        sb2 = jax.random.uniform(ks[4], (NUM_SHARED, d), jnp.float32, -s2, s2)
        rw1 = jax.random.uniform(ks[5], (NUM_ROUTED, d, h), jnp.float32, -s1, s1)
        rb1 = jax.random.uniform(ks[6], (NUM_ROUTED, h), jnp.float32, -s1, s1)
        rw2 = jax.random.uniform(ks[7], (NUM_ROUTED, h, d), jnp.float32, -s2, s2)
        rb2 = jax.random.uniform(ks[8], (NUM_ROUTED, d), jnp.float32, -s2, s2)
        router_w = jax.random.uniform(ks[9], (d, NUM_ROUTED), jnp.float32, -s1, s1)
        router_b = jax.random.uniform(ks[10], (NUM_ROUTED,), jnp.float32, -s1, s1)
        return {'x': x, 'sw1': sw1, 'sb1': sb1, 'sw2': sw2, 'sb2': sb2, 'rw1': rw1, 'rb1': rb1, 'rw2': rw2, 'rb2': rb2, 'router_w': router_w, 'router_b': router_b}
    _L0_ffn_all = _L0_ffn_setup()
    _L0_ffn_in = {k: v for k, v in _L0_ffn_all.items() if k in ('sw1', 'sb1', 'sw2', 'sb2', 'rw1', 'rb1', 'rw2', 'rb2', 'router_w', 'router_b')}
    del _L0_ffn_all

    def _L1_xattn_setup():
        import jax, jax.numpy as jnp
        import numpy as np
        key = jax.random.key(seed)
        ks = jax.random.split(key, 6)
        B, L, N, C, D = (8, 64, 256, 128, 128)
        return {'teacher_logits': jax.random.normal(ks[0], (B, L, N), dtype=jnp.float32), 'teacher_features': jax.random.normal(ks[1], (B, N, C), dtype=jnp.float32), 'Wq': jax.random.normal(ks[2], (D, C), dtype=jnp.float32) * (1.0 / np.sqrt(C)), 'bq': jnp.zeros((D,), dtype=jnp.float32), 'Wk': jax.random.normal(ks[3], (D, C), dtype=jnp.float32) * (1.0 / np.sqrt(C)), 'bk': jnp.zeros((D,), dtype=jnp.float32)}
    _L1_xattn_all = _L1_xattn_setup()
    _L1_xattn_in = {k: v for k, v in _L1_xattn_all.items() if k in ('Wq', 'bq', 'Wk', 'bk')}
    del _L1_xattn_all

    def _L1_ffn_setup():
        import jax, jax.numpy as jnp
        import numpy as np
        TOPK = 2
        NORM_TOPK = True
        SCALE = 1.0
        EPS = 1e-09
        key = jax.random.key(seed)
        ks = jax.random.split(key, 9)
        h, i, E = (256, 128, 16)
        std = 0.02
        return {'x': jax.random.normal(ks[0], (1, 256, h), jnp.float32), 'Wr': jax.random.normal(ks[1], (E, h), jnp.float32) * std, 'bias': jnp.zeros((E,), jnp.float32), 'Wg': jax.random.normal(ks[2], (E, h, i), jnp.float32) * std, 'Wu': jax.random.normal(ks[3], (E, h, i), jnp.float32) * std, 'Wd': jax.random.normal(ks[4], (E, i, h), jnp.float32) * std, 'sWg': jax.random.normal(ks[5], (h, i), jnp.float32) * std, 'sWu': jax.random.normal(ks[6], (h, i), jnp.float32) * std, 'sWd': jax.random.normal(ks[7], (i, h), jnp.float32) * std}
    _L1_ffn_all = _L1_ffn_setup()
    _L1_ffn_in = {k: v for k, v in _L1_ffn_all.items() if k in ('Wr', 'bias', 'Wg', 'Wu', 'Wd', 'sWg', 'sWu', 'sWd')}
    del _L1_ffn_all
    return {'x': x, 'ctx_1024': ctx_1024, 'g_xattn': g_xattn, 'g_ffn': g_ffn, 'L0_xattn_in_proj_w': _L0_xattn_in['in_proj_w'], 'L0_xattn_conv_w': _L0_xattn_in['conv_w'], 'L0_xattn_conv_b': _L0_xattn_in['conv_b'], 'L0_xattn_x_proj_w': _L0_xattn_in['x_proj_w'], 'L0_xattn_dt_proj_w': _L0_xattn_in['dt_proj_w'], 'L0_xattn_dt_proj_b': _L0_xattn_in['dt_proj_b'], 'L0_xattn_A_log': _L0_xattn_in['A_log'], 'L0_xattn_D': _L0_xattn_in['D'], 'L0_ffn_sw1': _L0_ffn_in['sw1'], 'L0_ffn_sb1': _L0_ffn_in['sb1'], 'L0_ffn_sw2': _L0_ffn_in['sw2'], 'L0_ffn_sb2': _L0_ffn_in['sb2'], 'L0_ffn_rw1': _L0_ffn_in['rw1'], 'L0_ffn_rb1': _L0_ffn_in['rb1'], 'L0_ffn_rw2': _L0_ffn_in['rw2'], 'L0_ffn_rb2': _L0_ffn_in['rb2'], 'L0_ffn_router_w': _L0_ffn_in['router_w'], 'L0_ffn_router_b': _L0_ffn_in['router_b'], 'L1_xattn_Wq': _L1_xattn_in['Wq'], 'L1_xattn_bq': _L1_xattn_in['bq'], 'L1_xattn_Wk': _L1_xattn_in['Wk'], 'L1_xattn_bk': _L1_xattn_in['bk'], 'L1_ffn_Wr': _L1_ffn_in['Wr'], 'L1_ffn_bias': _L1_ffn_in['bias'], 'L1_ffn_Wg': _L1_ffn_in['Wg'], 'L1_ffn_Wu': _L1_ffn_in['Wu'], 'L1_ffn_Wd': _L1_ffn_in['Wd'], 'L1_ffn_sWg': _L1_ffn_in['sWg'], 'L1_ffn_sWu': _L1_ffn_in['sWu'], 'L1_ffn_sWd': _L1_ffn_in['sWd']}

def reference(x, ctx_1024, g_xattn, g_ffn, L0_xattn_in_proj_w, L0_xattn_conv_w, L0_xattn_conv_b, L0_xattn_x_proj_w, L0_xattn_dt_proj_w, L0_xattn_dt_proj_b, L0_xattn_A_log, L0_xattn_D, L0_ffn_sw1, L0_ffn_sb1, L0_ffn_sw2, L0_ffn_sb2, L0_ffn_rw1, L0_ffn_rb1, L0_ffn_rw2, L0_ffn_rb2, L0_ffn_router_w, L0_ffn_router_b, L1_xattn_Wq, L1_xattn_bq, L1_xattn_Wk, L1_xattn_bk, L1_ffn_Wr, L1_ffn_bias, L1_ffn_Wg, L1_ffn_Wu, L1_ffn_Wd, L1_ffn_sWg, L1_ffn_sWu, L1_ffn_sWd):
    import jax
    import jax.numpy as jnp

    def _L0_xattn_ref(hidden_states, z, in_proj_w, conv_w, conv_b, x_proj_w, dt_proj_w, dt_proj_b, A_log, D):
        import jax, jax.numpy as jnp
        import numpy as np
        import math
        B, L, DM = (2, 256, 128)
        DS, DC, EXP = (16, 4, 2)
        DI = EXP * DM
        DR = math.ceil(DM / 16)
        DT_MIN, DT_MAX, DT_FLOOR = (0.001, 0.1, 0.0001)

        def _ssm_forward(hidden_states, z, in_proj_w, conv_w, conv_b, x_proj_w, dt_proj_w, dt_proj_b, A_log, D):
            b = hidden_states.shape[0]
            x = jnp.einsum('ed,bld->bel', in_proj_w, hidden_states)
            xp = jnp.pad(x, ((0, 0), (0, 0), (DC - 1, 0)))
            xc = jax.lax.conv_general_dilated(xp, conv_w[:, None, :], window_strides=(1,), padding='VALID', dimension_numbers=('NCH', 'OIH', 'NCH'), feature_group_count=DI)
            u = jax.nn.silu(xc + conv_b[None, :, None])
            x_dbl = jnp.einsum('ke,bel->bkl', x_proj_w, u)
            dt_lo = x_dbl[:, :DR]
            Bm = x_dbl[:, DR:DR + DS]
            Cm = x_dbl[:, DR + DS:]
            delta = jax.nn.softplus(jnp.einsum('er,brl->bel', dt_proj_w, dt_lo) + dt_proj_b[None, :, None])
            A = -jnp.exp(A_log)

            def step(state, xs):
                d_t, B_t, C_t, u_t = xs
                dA = jnp.exp(d_t[..., None] * A)
                state = state * dA + (d_t * u_t)[..., None] * B_t[:, None, :]
                y_t = jnp.einsum('ben,bn->be', state, C_t)
                return (state, y_t)
            xs = (jnp.moveaxis(delta, -1, 0), jnp.moveaxis(Bm, -1, 0), jnp.moveaxis(Cm, -1, 0), jnp.moveaxis(u, -1, 0))
            state0 = jnp.zeros((b, DI, DS), delta.dtype)
            _, ys = jax.lax.scan(step, state0, xs)
            y = jnp.moveaxis(ys, 0, -1)
            y = y + D[None, :, None] * u
            y = y * jax.nn.silu(z)
            return jnp.swapaxes(y, 1, 2)
        return _ssm_forward(hidden_states, z, in_proj_w, conv_w, conv_b, x_proj_w, dt_proj_w, dt_proj_b, A_log, D)

    def _L0_ffn_ref(x, sw1, sb1, sw2, sb2, rw1, rb1, rw2, rb2, router_w, router_b):
        import jax, jax.numpy as jnp
        import numpy as np
        D_MODEL = 256
        D_HIDDEN = 176
        NUM_SHARED = 2
        NUM_ROUTED = 32
        TOP_K = 6

        def _expert_apply(xf, w1, b1, w2, b2):
            return jnp.maximum(xf @ w1 + b1, 0.0) @ w2 + b2
        B, S, d = x.shape
        flat = x.reshape(-1, d)
        T = flat.shape[0]

        def sh_body(acc, p):
            w1, b1, w2, b2 = p
            return (acc + _expert_apply(flat, w1, b1, w2, b2), None)
        shared_out, _ = jax.lax.scan(sh_body, jnp.zeros_like(flat), (sw1, sb1, sw2, sb2))
        shared_out = shared_out / NUM_SHARED
        logits = flat @ router_w + router_b
        probs = jax.nn.softmax(logits, axis=-1)
        topk_p, topk_i = jax.lax.top_k(probs, TOP_K)
        topk_p = topk_p / jnp.sum(topk_p, axis=-1, keepdims=True)
        gates = jnp.zeros((T, NUM_ROUTED), dtype=flat.dtype)
        gates = gates.at[jnp.arange(T)[:, None], topk_i].add(topk_p)

        def r_body(acc, p):
            w1, b1, w2, b2, g = p
            return (acc + g[:, None] * _expert_apply(flat, w1, b1, w2, b2), None)
        routed_out, _ = jax.lax.scan(r_body, jnp.zeros_like(flat), (rw1, rb1, rw2, rb2, gates.T))
        return (shared_out + routed_out).reshape(B, S, d)

    def _L1_xattn_ref(teacher_logits, teacher_features, Wq, bq, Wk, bk):
        import jax, jax.numpy as jnp
        import numpy as np
        query = jnp.einsum('bnc,dc->bnd', teacher_features, Wq) + bq
        key = jnp.einsum('bnc,dc->bnd', teacher_features, Wk) + bk
        energy = jnp.einsum('bnd,bmd->bnm', query, key)
        attention = jax.nn.softmax(energy, axis=-1)
        x_m = jnp.einsum('bln,bmn->blm', teacher_logits, attention)
        return x_m

    def _L1_ffn_ref(x, Wr, bias, Wg, Wu, Wd, sWg, sWu, sWd):
        import jax, jax.numpy as jnp
        import numpy as np
        TOPK = 2
        NORM_TOPK = True
        SCALE = 1.0
        EPS = 1e-09
        b, s, h = x.shape
        E = Wr.shape[0]
        xt = x.reshape(b * s, h)
        logits = xt @ Wr.T + bias
        probs = jax.nn.softmax(logits, axis=-1)
        topk_val, topk_idx = jax.lax.top_k(probs, TOPK)
        if NORM_TOPK:
            w = topk_val / (jnp.sum(topk_val, axis=-1, keepdims=True) + EPS)
        else:
            w = topk_val
        w = w * SCALE
        g = jnp.einsum('th,ehi->tei', xt, Wg)
        u = jnp.einsum('th,ehi->tei', xt, Wu)
        y = jnp.einsum('tei,eih->teh', jax.nn.silu(g) * u, Wd)
        oh = jax.nn.one_hot(topk_idx, E, dtype=x.dtype)
        routed = jnp.einsum('tke,tk,teh->th', oh, w, y)
        shared = jax.nn.silu(xt @ sWg) * (xt @ sWu) @ sWd
        return (routed + shared).reshape(b, s, h)
    x = x + jnp.tanh(g_xattn[0]) * _L0_xattn_ref(ctx_1024, _layernorm(x, axis=-1), L0_xattn_in_proj_w, L0_xattn_conv_w, L0_xattn_conv_b, L0_xattn_x_proj_w, L0_xattn_dt_proj_w, L0_xattn_dt_proj_b, L0_xattn_A_log, L0_xattn_D)
    x = x + jnp.tanh(g_ffn[0]) * _L0_ffn_ref(_layernorm(x, axis=-1), L0_ffn_sw1, L0_ffn_sb1, L0_ffn_sw2, L0_ffn_sb2, L0_ffn_rw1, L0_ffn_rb1, L0_ffn_rw2, L0_ffn_rb2, L0_ffn_router_w, L0_ffn_router_b)
    x = x + jnp.tanh(g_xattn[1]) * _L1_xattn_ref(_layernorm(x, axis=-1), ctx_1024, L1_xattn_Wq, L1_xattn_bq, L1_xattn_Wk, L1_xattn_bk)
    x = x + jnp.tanh(g_ffn[1]) * _L1_ffn_ref(_layernorm(x, axis=-1), L1_ffn_Wr, L1_ffn_bias, L1_ffn_Wg, L1_ffn_Wu, L1_ffn_Wd, L1_ffn_sWg, L1_ffn_sWu, L1_ffn_sWd)
    return x

_drawn_inputs = setup_inputs


def setup_inputs(seed=0):
    import zlib

    import numpy as np

    out = dict(_drawn_inputs(seed))
    spreads = {'g_ffn': (-1.0, 0.6),
     'L0_xattn_conv_b': (0.0, 0.1),
     'L0_xattn_D': (1.0, 0.2),
     'L1_xattn_bq': (0.0, 0.1),
     'L1_xattn_bk': (0.0, 0.8),
     'L1_ffn_bias': (0.0, 0.8)}
    factors = {'L0_xattn_dt_proj_w': 7.021,
     'L0_xattn_dt_proj_b': 3.192,
     'L0_xattn_A_log': 2.806,
     'L0_ffn_sb1': 6.989,
     'L0_ffn_sb2': 2.87,
     'L0_ffn_rb1': 8.0,
     'L0_ffn_rb2': 4.27,
     'L0_ffn_router_b': 3.901,
     'L1_ffn_Wr': 8.0,
     'L1_ffn_Wg': 8.0,
     'L1_ffn_Wu': 8.0,
     'L1_ffn_Wd': 8.0,
     'L1_ffn_sWg': 7.723,
     'L1_ffn_sWu': 7.66,
     'L1_ffn_sWd': 7.624}
    for name, (base, spread) in spreads.items():
        noise = np.random.default_rng([zlib.crc32(name.encode()), seed]).standard_normal(out[name].shape)
        drawn = base * np.exp(spread * noise) if base else spread * noise
        out[name] = jnp.asarray(drawn.astype(out[name].dtype))
    for name, factor in factors.items():
        out[name] = (out[name] * factor).astype(out[name].dtype)
    return out
```

```python
from contextlib import ExitStack

import concourse.bass as bass
from concourse import mybir
from concourse.alu_op_type import AluOpType as ALU

F32 = mybir.dt.float32
BF16 = mybir.dt.bfloat16
F16 = mybir.dt.float16
I32 = mybir.dt.int32
U32 = mybir.dt.uint32
ACT = mybir.ActivationFunctionType
AX = mybir.AxisListType

P = 128
EPS_LN = 1e-5


class MambaSemaphores:

    def __init__(self, new):
        self.consts = new("consts")
        self.ctx_in = new("ctx_in")
        self.mamba_in = new("mamba_in")
        self.gates_in = new("gates_in")
        self.x_in = new("x_in")
        self.att_in = new("att_in")
        self.l0_in = new("l0_in")
        self.l1_in = new("l1_in")
        self.w1_in = new("w1_in")
        self.w2_in = new("w2_in")
        self.b1_in = new("b1_in")
        self.gates_made = new("gates_made")
        self.hcb_made = new("hcb_made")
        self.wcv_made = new("wcv_made")
        self.dg_made = new("dg_made")
        self.var_made = new("var_made")
        self.rstd_made = new("rstd_made")
        self.dve_step = new("dve_step")
        self.pool_step = new("pool_step")
        self.ctxT_psum = new("ctxT_psum")
        self.ctxT_made = new("ctxT_made")
        self.wcT_psum = new("wcT_psum")
        self.wcT_made = new("wcT_made")
        self.xw_psum = new("xw_psum")
        self.xw_made = new("xw_made")
        self.a_made = new("a_made")
        self.conv_psum = new("conv_psum")
        self.th_made = new("th_made")
        self.u_made = new("u_made")
        self.bc_psum = new("bc_psum")
        self.dt_psum = new("dt_psum")
        self.hi_made = new("hi_made")
        self.dtl_made = new("dtl_made")
        self.parts_made = new("parts_made")
        self.dpre_psum = new("dpre_psum")
        self.abs_made = new("abs_made")
        self.exp_made = new("exp_made")
        self.ln_made = new("ln_made")
        self.w_made_1 = new("w_made_1")
        self.low_made = new("low_made")
        self.delta_made = new("delta_made")
        self.du_made = new("du_made")
        self.z_normed = new("z_normed")
        self.z_th = new("z_th")
        self.z_made = new("z_made")
        self.region_free = new("region_free")
        self.b_bcast = new("b_bcast")
        self.c_bcast = new("c_bcast")
        self.b_copied = new("b_copied")
        self.decay_made = new("decay_made")
        self.inflow_made = new("inflow_made")
        self.scanned = new("scanned")
        self.prod_made = new("prod_made")
        self.y_init = new("y_init")
        self.y_summed = new("y_summed")
        self.gated = new("gated")
        self.mix_psum = new("mix_psum")
        self.x1_made = new("x1_made")


class LayerSemaphores:

    def __init__(self, new, i):
        self.xn_made = new(f"xn_made_l{i}")
        self.xn_out = new(f"xn_out_l{i}")
        self.xnT_psum = new(f"xnT_psum_l{i}")
        self.xnT_a = new(f"xnT_a_l{i}")
        self.xnT_v = new(f"xnT_v_l{i}")
        self.logits_psum = new(f"logits_psum_l{i}")
        self.shifted = new(f"shifted_l{i}")
        self.exped = new(f"exped_l{i}")
        self.chosen_made = new(f"chosen_made_l{i}")
        self.rank_psum = new(f"rank_psum_l{i}")
        self.hot_made = new(f"hot_made_l{i}")
        self.map_used = new(f"map_used_l{i}")
        self.tok_made = new(f"tok_made_l{i}")
        self.owner_made = new(f"owner_made_l{i}")
        self.owner_psum = new(f"owner_psum_l{i}")
        self.owner_ready = new(f"owner_ready_l{i}")
        self.sh_psum = new(f"sh_psum_l{i}")
        self.sh_made = new(f"sh_made_l{i}")
        self.base_psum = new(f"base_psum_l{i}")
        self.based = new(f"based_l{i}")
        self.added = new(f"added_l{i}")
        self.got_in0 = new(f"got_in0_l{i}")
        self.got_in1 = new(f"got_in1_l{i}")
        self.got_in = [self.got_in0, self.got_in1]


class LoopSemaphores:

    def __init__(self, new):
        self.xgT_psum = new("xgT_psum")
        self.xgT_made = new("xgT_made")
        self.h_psum = new("h_psum")
        self.gate_made = new("gate_made")
        self.half_made = new("half_made")
        self.hid_made = new("hid_made")
        self.hidT_psum = new("hidT_psum")
        self.hidT_made = new("hidT_made")
        self.y_psum = new("y_psum")
        self.y_made = new("y_made")
        self.gathered0 = new("gathered0")
        self.gathered1 = new("gathered1")
        self.gathered2 = new("gathered2")
        self.gathered3 = new("gathered3")
        self.y_out0 = new("y_out0")
        self.y_out1 = new("y_out1")
        self.y_out2 = new("y_out2")
        self.y_out3 = new("y_out3")
        self.gathered = [self.gathered0, self.gathered1, self.gathered2, self.gathered3]
        self.y_out = [self.y_out0, self.y_out1, self.y_out2, self.y_out3]


class AttentionSemaphores:

    def __init__(self, new):
        self.wqkT_psum = new("wqkT_psum")
        self.wqkT_made = new("wqkT_made")
        self.qk_psum = new("qk_psum")
        self.qk_made = new("qk_made")
        self.e_psum = new("e_psum")
        self.neg_made = new("neg_made")
        self.aexp_made = new("aexp_made")
        self.rec_made = new("rec_made")
        self.att_made = new("att_made")
        self.attT_psum = new("attT_psum")
        self.attT_made = new("attT_made")
        self.xn_made = new("xn_made")
        self.xnT_psum = new("xnT_psum")
        self.xnT_a = new("xnT_a")
        self.xnT_v = new("xnT_v")
        self.att_psum = new("att_psum")
        self.x3_made = new("x3_made")
        self.out_done = new("out_done")
        self.hg_made = new("hg_made")
        self.shT_ones = new("shT_ones")
        self.hidT_ones = new("hidT_ones")
        self.wgu_in = new("wgu_in")
        self.sh_gate = new("sh_gate")
        self.sh_half = new("sh_half")


class Layer:

    def __init__(self, i, done, slot_done, E, K, tiles, last, s, rows, y_rows, logits, chosen, posf, full,
                 hot, wexp, wgt, wgt_g, rowf, row_i, tile_i, slot_i, tile_f, slot_f):
        self.i = i
        self.done = done
        self.slot_done = slot_done
        self.E = E
        self.K = K
        self.tiles = tiles
        self.last = last
        self.s = s
        self.rows = rows
        self.y_rows = y_rows
        self.logits = logits
        self.chosen = chosen
        self.posf = posf
        self.full = full
        self.hot = hot
        self.wexp = wexp
        self.wgt = wgt
        self.wgt_g = wgt_g
        self.rowf = rowf
        self.row_i = row_i
        self.tile_i = tile_i
        self.slot_i = slot_i
        self.tile_f = tile_f
        self.slot_f = slot_f


def flamingo_two_layer_kernel(nc, io, out):
    B, L, DM = io["x"].shape
    DC = io["ctx_1024"].shape[2]
    DI = io["L0_xattn_in_proj_w"].shape[0]
    TAPS = io["L0_xattn_conv_w"].shape[1]
    DR = io["L0_xattn_dt_proj_w"].shape[1]
    DS = io["L0_xattn_A_log"].shape[1]
    E0, _, H0 = io["L0_ffn_rw1"].shape
    NSH = io["L0_ffn_sw1"].shape[0]
    E1, _, H1 = io["L1_ffn_Wg"].shape
    K0, K1 = 6, 2
    T = B * L
    NT = T // P
    HH = H0 // 2
    TILES0 = (T * K0 + E0 * (P - 1)) // P
    TILES1 = (T * K1 + E1 * (P - 1)) // P
    CH = 2 * L
    NB = DS * 2
    U = 4
    assert DC == P and DI == 2 * P and DM == 2 * P and L == 2 * P and B == 4 and H1 == P
    assert TILES0 % U == U - 1 and TILES1 % U == U - 1

    with ExitStack() as stack:
        def sb(name, shape, dt=F32, on=stack):
            return on.enter_context(nc.sbuf_tensor(name, shape, dt))

        def semaphore(name):
            return stack.enter_context(nc.semaphore(name))

        bank = stack.enter_context(nc.psum_tensor("bank", [P, 8, 512], F32))

        xn_rows0 = nc.dram_tensor("xn_rows0", [T, DM], F32, kind="Internal").ap()
        xn_rows1 = nc.dram_tensor("xn_rows1", [T, DM], F32, kind="Internal").ap()
        y_rows0 = nc.dram_tensor("y_rows0", [TILES0 * P, DM], F32, kind="Internal").ap()
        y_rows1 = nc.dram_tensor("y_rows1", [TILES1 * P, DM], F32, kind="Internal").ap()

        ident = sb("ident", [P, P])
        eye3 = sb("eye3", [3 * NB, NB], BF16)
        before = sb("before", [P, P], BF16)
        ones16 = sb("ones16", [P, P], BF16)
        ones_row = sb("ones_row", [1, P])
        iota_i = sb("iota_i", [P, P], I32)
        iota_f = sb("iota_f", [P, P])
        iota_h = sb("iota_h", [P, P], F16)
        fill_i = sb("fill_i", [P, NT], I32)
        fill_f = sb("fill_f", [P, NT])
        tokid_i = sb("tokid_i", [P, NT], I32)
        tokid = sb("tokid", [P, NT])
        minus_half = sb("minus_half", [P, NT])
        gates_raw = sb("gates_raw", [P, 4])
        gates = sb("gates", [P, 4])
        xs = sb("xs", [P, NT, DM])
        ctxT = sb("ctxT", [P, B, TAPS - 1 + L])
        hg_moe = sb("hg_moe", [P, 2])
        stats = sb("stats", [P, NT, 6])
        meanvar = sb("meanvar", [P, NT, 2])
        vareps = sb("vareps", [P, NT])
        rstd = sb("rstd", [P, NT])
        wq = sb("wq", [P, P])
        wk = sb("wk", [P, P])
        wqkT = sb("wqkT", [P, 2, P])
        bqk = sb("bqk", [P, 2])
        router0 = sb("router0", [P, 2, E0])
        rbias0 = sb("rbias0", [1, E0])
        router1 = sb("router1", [P, 2, E1])
        wr_rows = sb("wr_rows", [E1, DM])
        rbias1 = sb("rbias1", [1, E1])
        sw1 = sb("sw1", [P, NSH * 2, H0])
        sb1 = sb("sb1", [HH, NSH, 2])
        sw2 = sb("sw2", [HH + 1, NSH, 2, DM])
        swg = sb("swg", [P, 2, H1])
        swu = sb("swu", [P, 2, H1])
        swd = sb("swd", [P, DM])

        r1 = ExitStack()
        w1 = sb("w1", [P, E0, 2, H0], on=r1)
        r1.close()
        r1 = ExitStack()
        shT = sb("shT", [HH + 1, NSH * 2, T], on=r1)
        got = sb("got", [P, 2, K0, DM], on=r1)
        gg = sb("gg", [P, CH], on=r1)
        gu = sb("gu", [P, CH], on=r1)
        shT1 = sb("shT1", [P, T], on=r1)
        r1.close()
        hold1 = sb("hold1", [P, E0 * 2 * H0])
        r2 = ExitStack()
        w2 = sb("w2", [HH + 1, E0, 2, DM], on=r2)
        r2.close()
        r2 = ExitStack()
        wgu = sb("wgu", [P, E1 * 2, 2, H1], on=r2)
        wd = sb("wd", [P, E1, DM], on=r2)
        r2.close()
        hold2 = sb("hold2", [P, E0 * 2 * DM])
        r3 = ExitStack()
        cu = sb("cu", [P, 2, T], on=r3)
        delta = sb("delta", [P, 2, T], on=r3)
        du = sb("du", [P, 2, T], on=r3)
        sz = sb("sz", [P, NT, DM], on=r3)
        bcp = sb("bcp", [3 * NB, T], BF16, on=r3)
        cw = sb("cw", [P, 2, TAPS], on=r3)
        cb = sb("cb", [P, 2], on=r3)
        hcb = sb("hcb", [P, 2], on=r3)
        dtb = sb("dtb", [P, 2], on=r3)
        dsk = sb("dsk", [P, 2], on=r3)
        a_log = sb("a_log", [P, 2, DS], on=r3)
        a_exp = sb("a_exp", [P, 2, DS], on=r3)
        a_neg = sb("a_neg", [P, 2, DS], on=r3)
        dg = sb("dg", [P, 2, P], on=r3)
        hg = sb("hg", [P, 1], on=r3)
        r3a = ExitStack()
        ctx_nat = sb("ctx_nat", [P, NT, DC], on=r3a)
        wip = sb("wip", [P, 2, DC], on=r3a)
        wcv = sb("wcv", [P, 2, TAPS, DC], on=r3a)
        wcT = sb("wcT", [P, TAPS, 2, P], on=r3a)
        xpw = sb("xpw", [DR + NB, DI], on=r3a)
        dtw = sb("dtw", [P, 2, DR], on=r3a)
        wbcT = sb("wbcT", [P, 2, 3 * NB], on=r3a)
        wdtT = sb("wdtT", [P, 2, DR], on=r3a)
        dtpT = sb("dtpT", [DR, 2, P], on=r3a)
        dtl = sb("dtl", [DR, T], on=r3a)
        th = sb("th", [P, 2, CH], on=r3a)
        part = sb("part", [3 * NB, CH], on=r3a)
        part16 = sb("part16", [3 * NB, CH], BF16, on=r3a)
        sp2 = sb("sp2", [P, 2, CH], on=r3a)
        sp3 = sb("sp3", [P, 2, CH], on=r3a)
        r3a.close()
        r3b = ExitStack()
        b_sb = sb("b_sb", [P, 2, CH], on=r3b)
        decay = sb("decay", [P, 2, 2, 2, L], on=r3b)
        inflow = sb("inflow", [P, 2, 2, CH], on=r3b)
        state = sb("state", [P, 2, CH], on=r3b)
        prod = sb("prod", [P, 2, 2, CH], on=r3b)
        r3b.close()
        r3.close()
        r3 = ExitStack()
        attT = sb("attT", [P, B, 2, L], on=r3)
        xn = sb("xn", [P, NT, DM], on=r3)
        b1_bc = sb("b1_bc", [P, E0, H0], on=r3)
        logits = sb("logits", [P, NT, E0], on=r3)
        top = sb("top", [P, NT, 8], on=r3)
        topi = sb("topi", [P, NT, 8], U32, on=r3)
        topf = sb("topf", [P, NT, 8], on=r3)
        wexp = sb("wexp", [P, NT, K0], on=r3)
        wsum = sb("wsum", [P, NT], on=r3)
        wall = sb("wall", [P, NT], on=r3)
        wrec = sb("wrec", [P, NT], on=r3)
        wgt = sb("wgt", [P, NT, K0], on=r3)
        wgt_g = sb("wgt_g", [P, NT, K0], on=r3)
        chosen = sb("chosen", [P, NT, E0], BF16, on=r3)
        full = sb("full", [P, E0, NT], on=r3)
        ntiles = sb("ntiles", [P, E0], on=r3)
        tile_end = sb("tile_end", [P, E0], on=r3)
        row0 = sb("row0", [P, E0], on=r3)
        posf = sb("posf", [P, NT, E0], on=r3)
        rowf = sb("rowf", [P, NT, K0], on=r3)
        row_i = sb("row_i", [P, NT, K0], I32, on=r3)
        tile_i = sb("tile_i", [P, NT, K0], I32, on=r3)
        slot_i = sb("slot_i", [P, NT, K0], I32, on=r3)
        tile_f = sb("tile_f", [P, NT, K0], on=r3)
        slot_f = sb("slot_f", [P, NT, K0], on=r3)
        tok_of = sb("tok_of", [P, TILES0 + 1], I32, on=r3)
        ended = sb("ended", [P, E0], on=r3)
        owner = sb("owner", [P, 1], on=r3)
        owner_i = sb("owner_i", [1, P], I32, on=r3)
        r3d = ExitStack()
        att = sb("att", [P, 2, L], on=r3d)
        r3d.close()
        r3d = ExitStack()
        slot_hot = sb("slot_hot", [P, K0, P], F16, on=r3d)
        r3d.close()
        hold3 = sb("hold3", [P, 2 * L], on=r3)
        att_max = sb("att_max", [P, 2 * B], on=r3)
        att_neg = sb("att_neg", [P, 2 * B], on=r3)
        att_sum = sb("att_sum", [P, 2 * B], on=r3)
        att_rec = sb("att_rec", [P, 2 * B], on=r3)
        xnT = sb("xnT", [P, 2, T], on=r3)
        r3c = ExitStack()
        hot = sb("hot", [P, NT, K0, E0], on=r3c)
        qT = sb("qT", [P, T], on=r3c)
        kT = sb("kT", [P, T], on=r3c)
        tile_tok = sb("tile_tok", [P, K0, TILES0], F16, on=r3c)
        r3c.close()
        xg = sb("xg", [P, U, DM], on=r3)
        xgT = sb("xgT", [P, 2, 2, P], on=r3)
        hid = sb("hid", [P, 2, DM], on=r3)
        gate_th = sb("gate_th", [P, 2, H1], on=r3)
        hidT = sb("hidT", [P, 2, 2, P], on=r3)
        yt = sb("yt", [P, U, DM], on=r3)
        r3.close()

        def flat(t, n, start=0):
            ap = t[:]
            if len(ap.shape) > 2:
                names = " ".join("abcde"[:len(ap.shape) - 1])
                ap = ap.rearrange(f"p {names} -> p ({names})")
            return ap[:, start:start + n]

        def cols(p):
            return slice(p * CH, (p + 1) * CH)

        s = MambaSemaphores(semaphore)
        lp = LoopSemaphores(semaphore)
        layers = []
        for i, (E, K, tiles, H) in enumerate(((E0, K0, TILES0, H0), (E1, K1, TILES1, H1))):
            layers.append(Layer(
                i=i, done=(0, TILES0)[i], slot_done=[(0, (TILES0 - 1 - u) // U + 1)[i] for u in range(U)], E=E, K=K, tiles=tiles, last=tiles + 1 - U, s=LayerSemaphores(semaphore, i),
                rows=(xn_rows0, xn_rows1)[i], y_rows=(y_rows0, y_rows1)[i],
                logits=flat(logits, NT * E).rearrange("p (j e) -> p j e", e=E),
                chosen=flat(chosen, NT * E), posf=flat(posf, NT * E).rearrange("p (j e) -> p j e", e=E),
                full=flat(full, E * NT).rearrange("p (e m) -> p e m", m=NT),
                hot=flat(hot, NT * K * E).rearrange("p (j k e) -> p j k e", k=K, e=E),
                wexp=flat(wexp, NT * K).rearrange("p (j k) -> p j k", k=K),
                wgt=flat(wgt, NT * K).rearrange("p (j k) -> p j k", k=K),
                wgt_g=flat(wgt_g, NT * K).rearrange("p (j k) -> p j k", k=K),
                rowf=flat(rowf, NT * K), row_i=flat(row_i, NT * K).rearrange("p (j k) -> p j k", k=K),
                tile_i=flat(tile_i, NT * K), slot_i=flat(slot_i, NT * K),
                tile_f=flat(tile_f, NT * K).rearrange("p (j k) -> p j k", k=K),
                slot_f=flat(slot_f, NT * K).rearrange("p (j k) -> p j k", k=K),
            ))
        a = AttentionSemaphores(semaphore)

        def first_tiles(t0, u, n):
            return isinstance(t0, int) and t0 + u < n

        def after(t0, u):
            return (t0 + U, 0) if u == U - 1 else (t0, u + 1)

        def turns(eng, ly, body):
            for u in range(U):
                body(0, u)
            with eng.Fori(U, ly.last, U) as t0:
                for u in range(U):
                    body(t0, u)
            for u in range(U - 1):
                body(ly.last, u)

        def expert(engine, ly, t0, u):
            return nc.values_load(owner_i[0:1, bass.ds(t0 + u, 1)], engines=(engine,), min_val=0, max_val=ly.E - 1,
                                  skip_runtime_bounds_check_because="VectorE clamped it to the experts")

        def slot_count(t0, n):
            return t0 * (16 // U) + 16 * n

        CONV_BANK = (5, 6, 7, 0)
        Y_BANK = ((5, 6), (7, 0))
        N_CONSTS = 18

        block = stack.enter_context(nc.Block())

        @block.sync
        def _(sp):
            sp.dma_start(ctx_nat[:], io["ctx_1024"].rearrange("b (s p) d -> p (b s) d", p=P)).then_inc(s.ctx_in, 16)
            for dst, src in (
                (wip[:], io["L0_xattn_in_proj_w"].rearrange("(h p) d -> p h d", p=P)),
                (cw[:], io["L0_xattn_conv_w"].rearrange("(h p) k -> p h k", p=P)),
                (cb[:], io["L0_xattn_conv_b"].rearrange("(h p) -> p h", p=P)),
                (xpw[:], io["L0_xattn_x_proj_w"]),
                (dtw[:], io["L0_xattn_dt_proj_w"].rearrange("(h p) r -> p h r", p=P)),
                (dtb[:], io["L0_xattn_dt_proj_b"].rearrange("(h p) -> p h", p=P)),
                (dsk[:], io["L0_xattn_D"].rearrange("(h p) -> p h", p=P)),
                (a_log[:], io["L0_xattn_A_log"].rearrange("(h p) n -> p h n", p=P)),
            ):
                sp.dma_start(dst, src, allow_slow_non_contiguous=True).then_inc(s.mamba_in, 16)
            sp.dma_start(xs[:], io["x"].rearrange("b (s p) d -> p (b s) d", p=P)).then_inc(s.x_in, 16)
            for i, name in enumerate(("g_xattn", "g_ffn")):
                sp.dma_start(gates_raw[:, 2 * i:2 * i + 2], io[name].partition_broadcast(P)).then_inc(s.gates_in, 16)
            quarter = E0 // 4
            for q in range(4):
                e = slice(q * quarter, (q + 1) * quarter)
                sp.dma_start(w1[:, e].rearrange("p e k h -> p (e k) h"),
                             io["L0_ffn_rw1"][e].rearrange("e (k p) h -> p (e k) h", p=P)).then_inc(s.w1_in, 16)
                sp.dma_start(w2[0:HH, e].rearrange("p e k d -> p (e k) d"),
                             io["L0_ffn_rw2"][e].rearrange("e (k p) d -> p (e k) d", p=HH)).then_inc(s.w2_in, 16)
            sp.dma_start(w2[HH:HH + 1, :, 1, :], io["L0_ffn_rb2"].unsqueeze(0)).then_inc(s.w2_in, 16)
            for dst, src in (
                (router0[:], io["L0_ffn_router_w"].rearrange("(k p) e -> p k e", p=P)),
                (rbias0[:], io["L0_ffn_router_b"].unsqueeze(0)),
                (sw1[:], io["L0_ffn_sw1"].rearrange("e (k p) h -> p (e k) h", p=P)),
                (sb1[:], io["L0_ffn_sb1"].rearrange("e (m p) -> p e m", p=HH)),
                (sw2[0:HH].rearrange("p e k d -> p (e k) d"), io["L0_ffn_sw2"].rearrange("e (k p) d -> p (e k) d", p=HH)),
                (sw2[HH:HH + 1, :, 1, :], io["L0_ffn_sb2"].unsqueeze(0)),
            ):
                sp.dma_start(dst, src, allow_slow_non_contiguous=True).then_inc(s.l0_in, 16)
            for dst, src in (
                (wq[:], io["L1_xattn_Wq"]), (wk[:], io["L1_xattn_Wk"]),
                (bqk[:, 0:1], io["L1_xattn_bq"].unsqueeze(1)), (bqk[:, 1:2], io["L1_xattn_bk"].unsqueeze(1)),
            ):
                sp.dma_start(dst, src, allow_slow_non_contiguous=True).then_inc(s.att_in, 16)
            for dst, src in (
                (wr_rows[:], io["L1_ffn_Wr"]), (rbias1[:], io["L1_ffn_bias"].unsqueeze(0)),
                (swg[:], io["L1_ffn_sWg"].rearrange("(k p) i -> p k i", p=P)),
                (swu[:], io["L1_ffn_sWu"].rearrange("(k p) i -> p k i", p=P)), (swd[:], io["L1_ffn_sWd"]),
            ):
                sp.dma_start(dst, src).then_inc(s.l1_in, 16)
            sp.wait_ge(s.x1_made, 4)
            sp.dma_start(b1_bc[:].rearrange("p e h -> p (e h)"),
                         io["L0_ffn_rb1"].rearrange("e h -> (e h)").partition_broadcast(P)).then_inc(s.b1_in, 16)
            for ly in layers:
                sp.wait_ge(ly.s.xn_made, NT)
                sp.dma_start(ly.rows.rearrange("(j p) d -> p j d", p=P), xn[:]).then_inc(ly.s.xn_out, 16)

                def store(t0, u):
                    sp.wait_ge(lp.y_made, t0 + (ly.done + u + 1))
                    sp.dma_start(ly.y_rows[bass.ds(t0 * P + u * P, P), :], yt[:, u, :]).then_inc(lp.y_out[u], 16)

                turns(sp, ly, store)
                if ly.i == 0:
                    sp.wait_ge(lp.y_psum, ly.done + ly.tiles)
                    for k in range(2):
                        for g, name in enumerate(("L1_ffn_Wg", "L1_ffn_Wu")):
                            sp.dma_start(wgu[:, k:2 * E1:2, g, :], io[name].rearrange("e (k p) i -> k p e i", p=P)[k]
                                         ).then_inc(a.wgu_in, 16)
                    sp.dma_start(wd[:], io["L1_ffn_Wd"].rearrange("e i d -> i e d")).then_inc(a.wgu_in, 16)
            sp.wait_ge(layers[1].s.added, NT)
            sp.dma_start(out.rearrange("b (s p) d -> p (b s) d", p=P), xs[:]).then_inc(a.out_done, 16)
            sp.wait_ge(a.out_done, 16)

        @block.gpsimd
        def _(pool):
            def const(ins):
                ins.then_inc(s.consts, 1)
                made[0] += 1
                pool.wait_ge(s.consts, made[0])

            made = [0]
            const(pool.memset(ident[:], 0.0))
            const(pool.affine_select(out=ident[:], in_=ident[:], compare_op=ALU.not_equal, fill=1.0, base=0,
                                     pattern=[[-1, P]], channel_multiplier=1))
            const(pool.memset(ctxT[:, :, 0:TAPS - 1], 0.0))
            const(pool.memset(minus_half[:], -0.5))
            const(pool.memset(eye3[:], 0.0))
            for q in range(3):
                const(pool.affine_select(out=eye3[:], in_=eye3[:], compare_op=ALU.not_equal, fill=1.0, base=-NB * q,
                                         pattern=[[-1, NB]], channel_multiplier=1))
            const(pool.memset(ones16[:], 1.0))
            const(pool.affine_select(out=before[:], in_=ones16[:], compare_op=ALU.is_gt, fill=0.0, base=0,
                                     pattern=[[1, P]], channel_multiplier=-1))
            const(pool.memset(ones_row[:], 1.0))
            const(pool.iota(iota_i[:], pattern=[[1, P]], base=0, channel_multiplier=0))
            const(pool.tensor_copy(iota_f[:], iota_i[:]))
            const(pool.tensor_copy(iota_h[:], iota_i[:]))
            const(pool.iota(fill_i[:], pattern=[[P, NT]], base=0, channel_multiplier=0))
            const(pool.tensor_copy(fill_f[:], fill_i[:]))
            const(pool.iota(tokid_i[:], pattern=[[P, NT]], base=0, channel_multiplier=1))
            const(pool.tensor_copy(tokid[:], tokid_i[:]))
            assert made[0] == N_CONSTS

            pool.wait_ge(s.var_made, 1)
            pool.tensor_tensor(rstd[:], vareps[:], minus_half[:], ALU.pow).then_inc(s.rstd_made, 1)

            for q in range(4):
                p, h = q // 2, q % 2
                pool.wait_ge(s.w_made_1, q + 1)
                pool.tensor_tensor(sp2[:, q % 2], sp2[:, q % 2], th[:, q % 2], ALU.subtract).then_inc(s.low_made, 1)
                pool.wait_ge(s.delta_made, q + 1)
                pool.tensor_tensor(du[:, h, cols(p)], delta[:, h, cols(p)], cu[:, h, cols(p)],
                                   ALU.mult).then_inc(s.du_made, 1)

            def step(p, t, slot):
                for h in range(2):
                    if h == 0:
                        pool.wait_ge(s.b_copied, t + 1)
                    if not (isinstance(t, int) and t < 2):
                        pool.wait_ge(s.scanned, 2 * (t - 2) + h + 1)
                    pool.tensor_tensor(inflow[:, slot, h], du[:, h, cols(p)], b_sb[:, slot],
                                       ALU.mult).then_inc(s.inflow_made, 1)

            pool.wait_ge(s.region_free, 1)
            for p in range(2):
                for i in range(2):
                    step(p, p * DS + i, i)
                with pool.Fori(1, DS // 2) as m:
                    for i in range(2):
                        step(p, 2 * m + (p * DS + i), i)

            def inverse_deviation(k):
                pool.wait_ge(s.var_made, k)
                pool.tensor_tensor(rstd[:], vareps[:], minus_half[:], ALU.pow).then_inc(s.rstd_made, 1)

            for ly in layers:
                ls = ly.s
                if ly.i == 0:
                    inverse_deviation(2)
                else:
                    inverse_deviation(3)
                    inverse_deviation(4)
                pool.wait_ge(ls.xn_out, 16)
                pool.wait_ge(ls.tok_made, 1)

                for t in range(ly.tiles):
                    if t >= U:
                        pool.wait_ge(lp.xgT_psum, ly.done + t - (U - 1))
                    pool.indirect_dma_start(xg[:, t % U, :], None, ly.rows,
                                            bass.IndirectOffsetOnAxis(ap=tok_of[:, t:t + 1], axis=0)
                                            ).then_inc(lp.gathered[t % U], 16)
                for u in range(U):
                    pool.wait_ge(lp.y_out[u], 16 * (ly.slot_done[u] + (ly.tiles - 1 - u) // U + 1))
                for j in range(NT):
                    b = j % 2
                    if j >= 2:
                        pool.wait_ge(ls.added, j - 1)
                    for k in range(ly.K):
                        pool.indirect_dma_start(got[:, b, k, :], None, ly.y_rows,
                                                bass.IndirectOffsetOnAxis(ap=ly.row_i[:, j, k:k + 1], axis=0)
                                                ).then_inc(ls.got_in[b], 16)

        @block.scalar
        def _(act):
            act.wait_ge(s.gates_in, 32)
            act.activation(gates[:], gates_raw[:], ACT.Tanh).then_inc(s.gates_made, 1)
            act.wait_ge(s.mamba_in, 128)
            act.activation(a_exp[:], a_log[:], ACT.Exp).then_inc(s.a_made, 1)
            act.wait_ge(s.a_made, 1)
            act.mul(a_neg[:], a_exp[:], -1.0).then_inc(s.a_made, 1)
            act.wait_ge(s.consts, 3)
            for i in range(2):
                act.wait_ge(s.ctxT_psum, i + 1)
                act.copy(ctxT[:, 2 * i:2 * i + 2, TAPS - 1:],
                         bank[:, i].rearrange("p (b l) -> p b l", b=2)).then_inc(s.ctxT_made, 1)

            act.wait_ge(s.hcb_made, 1)
            for p in range(2):
                for h in range(2):
                    q = 2 * p + h
                    act.wait_ge(s.conv_psum, q + 1)
                    if q >= 2:
                        act.wait_ge(s.u_made, q - 1)
                    act.activation(th[:, h], bank[:, CONV_BANK[q]], ACT.Tanh, bias=hcb[:, h:h + 1],
                                   scale=0.5).then_inc(s.th_made, 1)
                act.wait_ge(s.bc_psum, p + 1)
                if p >= 1:
                    act.wait_ge(s.parts_made, 4 * p)
                act.copy(part16[:], bank[0:3 * NB, 1 + p]).then_inc(s.hi_made, 1)
                act.copy(bcp[0:NB, cols(p)], bank[0:NB, 1 + p]).then_inc(s.hi_made, 1)
                act.wait_ge(s.dt_psum, p + 1)
                act.copy(dtl[:, cols(p)], bank[0:DR, 3 + p]).then_inc(s.dtl_made, 1)
            for i in range(4):
                act.wait_ge(s.z_normed, 2 * i + 2)
                if i >= 2:
                    act.wait_ge(s.z_made, i - 1)
                act.activation(sp3[:, i % 2], flat(sz, CH, i * CH), ACT.Tanh, scale=0.5).then_inc(s.z_th, 1)
            for q in range(4):
                h = q % 2
                act.wait_ge(s.dpre_psum, q + 1)
                if q >= 2:
                    act.wait_ge(s.delta_made, q - 1)
                else:
                    act.wait_ge(s.u_made, 4)
                    act.wait_ge(s.z_made, 4)
                act.activation(th[:, h], bank[:, CONV_BANK[q]], ACT.Abs, bias=dtb[:, h:h + 1]).then_inc(s.abs_made, 1)
                act.wait_ge(s.abs_made, q + 1)
                act.activation(sp2[:, h], th[:, h], ACT.Exp, scale=-1.0).then_inc(s.exp_made, 1)
                act.wait_ge(s.exp_made, q + 1)
                act.activation(sp3[:, h], sp2[:, h], ACT.Ln, bias=1.0).then_inc(s.ln_made, 1)

            a_of = a_neg[:].rearrange("p h (m i) -> p h m i", i=2)

            def step(p, t, m, slot):
                act.wait_ge(s.b_bcast, t + 1)
                first = isinstance(t, int) and t < 2
                if not first:
                    act.wait_ge(s.inflow_made, 2 * (t - 1))
                act.copy(b_sb[:, slot], bank[:, 1 + slot]).then_inc(s.b_copied, 1)
                for h in range(2):
                    if not first:
                        act.wait_ge(s.scanned, 2 * (t - 2) + h + 1)
                    act.activation(decay[:, slot, h, :, 1:],
                                   delta[:, h, cols(p)].rearrange("p (b l) -> p b l", b=2)[:, :, 1:],
                                   ACT.Exp, scale=a_of[:, h, bass.ds(m, 1), slot]).then_inc(s.decay_made, 1)

            act.wait_ge(s.region_free, 1)
            act.wait_ge(s.a_made, 2)
            for p in range(2):
                for i in range(2):
                    step(p, p * DS + i, 0, i)
                with act.Fori(1, DS // 2) as m:
                    for i in range(2):
                        step(p, 2 * m + (p * DS + i), m, i)

            def transposed_half(psum, made):
                for c in range(2):
                    act.wait_ge(psum, 1)
                    act.copy(xnT[:, 0, cols(c)], bank[:, 1 + c]).then_inc(made, 1)

            for ly in layers:
                ls = ly.s
                if ly.i == 1:
                    for c in range(4):
                        act.wait_ge(a.qk_psum, c + 1)
                        act.activation((qT, kT)[c // 2][:, cols(c % 2)], bank[:, (5, 6, 7, 0)[c]], ACT.Identity,
                                       bias=bqk[:, c // 2:c // 2 + 1]).then_inc(a.qk_made, 1)
                    for n in range(2 * B + 1):
                        if n < 2 * B:
                            act.wait_ge(a.neg_made, n + 1)
                            if n >= 2:
                                act.wait_ge(a.attT_psum, n - 1)
                            act.activation(att[:, n % 2], bank[:, 5 + n % 2, 0:L], ACT.Exp, bias=att_neg[:, n:n + 1],
                                           accum_out=att_sum[:, n:n + 1]).then_inc(a.aexp_made, 1)
                        if n >= 1:
                            i = n - 1
                            act.wait_ge(a.attT_psum, i + 1)
                            act.copy(attT[:, i // 2, :, (i % 2) * P:(i % 2 + 1) * P],
                                     bank[:, (7, 0)[i % 2], 0:2 * P].rearrange("p (k r) -> p k r", k=2)
                                     ).then_inc(a.attT_made, 1)
                    transposed_half(a.xnT_psum, a.xnT_a)
                transposed_half(ls.xnT_psum, ls.xnT_a)
                act.wait_ge(ls.shifted, 1)
                act.activation(ly.wexp, ly.wexp, ACT.Exp).then_inc(ls.exped, 1)
                if ly.i == 1:
                    act.activation(ly.posf, ly.posf, ACT.Exp).then_inc(ls.exped, 1)
                    for c in range(2):
                        act.wait_ge(ls.sh_psum, 2 * c + 1)
                        if c:
                            act.wait_ge(ls.sh_made, c)
                        act.activation(gg[:], bank[:, 1], ACT.Tanh, scale=0.5).then_inc(a.sh_gate, 1)

                def transpose_out(t0, u):
                    act.wait_ge(lp.xgT_psum, t0 + (ly.done + u + 1))
                    if not first_tiles(t0, u, 2):
                        act.wait_ge(lp.h_psum, t0 + (ly.done + u - 1))
                    act.copy(flat(xgT, 2 * P, (u % 2) * 2 * P), bank[:, u % 2, 0:2 * P]).then_inc(lp.xgT_made, 1)

                def tile(t0, u):
                    if ly.i == 1:
                        act.wait_ge(lp.h_psum, t0 + (ly.done + u + 1))
                        if not first_tiles(t0, u, 2):
                            act.wait_ge(lp.hid_made, t0 + (ly.done + u - 1))
                        act.activation(gate_th[:, u % 2], bank[:, 2 + u % 2, 0:H1], ACT.Tanh,
                                       scale=0.5).then_inc(lp.gate_made, 1)
                    if not (isinstance(t0, int) and t0 + u == ly.tiles - 1):
                        transpose_out(*after(t0, u))
                    act.wait_ge(lp.hidT_psum, t0 + (ly.done + u + 1))
                    if not first_tiles(t0, u, 2):
                        act.wait_ge(lp.y_psum, t0 + (ly.done + u - 1))
                    if ly.i == 0:
                        act.activation(hidT[0:HH, u % 2].rearrange("p k r -> p (k r)"), bank[0:HH, 4 + u % 2, 0:2 * P],
                                       ACT.Relu).then_inc(lp.hidT_made, 1)
                    else:
                        act.copy(hidT[:, u % 2, 0], bank[:, 4 + u % 2, 0:P]).then_inc(lp.hidT_made, 1)

                if ly.i == 0:
                    act.wait_ge(a.hidT_ones, 1)
                transpose_out(0, 0)
                turns(act, ly, tile)
                if ly.i == 0:
                    act.wait_ge(a.shT_ones, 1)
                    for n in range(NSH * 4):
                        act.wait_ge(ls.sh_psum, n + 1)
                        em, c = n // 2, n % 2
                        act.activation(shT[0:HH, em, cols(c)], bank[0:HH, 1 + n % 2], ACT.Relu,
                                       bias=sb1[:, em // 2, em % 2:em % 2 + 1]).then_inc(ls.sh_made, 1)

        @block.tensor
        def _(pe):
            pe.wait_ge(s.consts, 2)
            pe.wait_ge(s.ctx_in, 16)
            for j in range(NT):
                mm = pe.transpose(bank[:, j // 4, (j % 4) * P:(j % 4 + 1) * P], ctx_nat[:, j, :], ident[:])
                if j % 4 == 3:
                    mm.then_inc(s.ctxT_psum, 1)
            pe.wait_ge(s.wcv_made, 2 * TAPS)
            for k in range(TAPS):
                for h in range(2):
                    c = (k % 2) * 2 + h
                    mm = pe.transpose(bank[:, 2 + k // 2, c * P:(c + 1) * P], wcv[:, h, k, :], ident[:])
                if k % 2 == 1:
                    mm.then_inc(s.wcT_psum, 1)
            pe.wait_ge(s.mamba_in, 128)
            for h in range(2):
                pe.transpose(bank[:, 4, h * (DR + NB):(h + 1) * (DR + NB)], xpw[:, h * P:(h + 1) * P],
                             ident[0:DR + NB, 0:DR + NB])
                mm = pe.transpose(bank[0:DR, 4, (1 + h) * P:(2 + h) * P], dtw[:, h, :], ident[:])
            mm.then_inc(s.xw_psum, 1)
            pe.wait_ge(s.wcT_made, 2)
            pe.wait_ge(s.ctxT_made, 2)
            for q in range(4):
                p, h = q // 2, q % 2
                for k in range(TAPS):
                    mm = pe.matmul(bank[:, CONV_BANK[q]], wcT[:, k, h, :], ctxT[:, 2 * p:2 * p + 2, k:k + L],
                                   start=k == 0, stop=k == TAPS - 1)
                mm.then_inc(s.conv_psum, 1)
            pe.wait_ge(s.xw_made, 5)
            for p in range(2):
                pe.wait_ge(s.u_made, 2 * p + 2)
                for h in range(2):
                    mm = pe.matmul(bank[0:3 * NB, 1 + p], wbcT[:, h, :], cu[:, h, cols(p)], start=h == 0, stop=h == 1)
                mm.then_inc(s.bc_psum, 1)
                for h in range(2):
                    mm = pe.matmul(bank[0:DR, 3 + p], wdtT[:, h, :], cu[:, h, cols(p)], start=h == 0, stop=h == 1)
                mm.then_inc(s.dt_psum, 1)
                pe.wait_ge(s.dtl_made, p + 1)
                for h in range(2):
                    pe.matmul(bank[:, CONV_BANK[2 * p + h]], dtpT[:, h, :], dtl[:, cols(p)],
                              start=True, stop=True).then_inc(s.dpre_psum, 1)

            pick = eye3[:].rearrange("k (m i) -> k m i", i=2)

            def broadcast_b(p, t, m, slot):
                if not (isinstance(t, int) and t < 2):
                    pe.wait_ge(s.b_copied, t - 1)
                pe.matmul(bank[:, 1 + slot], pick[:, bass.ds(m, 1), slot].to_broadcast([3 * NB, P]), bcp[:, cols(p)],
                          start=True, stop=True).then_inc(s.b_bcast, 1)

            def broadcast_c(p, t, m, slot):
                if not (isinstance(t, int) and t < 2):
                    pe.wait_ge(s.prod_made, 2 * (t - 1))
                pe.matmul(bank[:, 3 + slot], pick[:, bass.ds(m + DS // 2, 1), slot].to_broadcast([3 * NB, P]), bcp[:, cols(p)],
                          start=True, stop=True).then_inc(s.c_bcast, 1)

            def ysum(p, t, slot, stop=False):
                for h in range(2):
                    pe.wait_ge(s.prod_made, 2 * t + h + 1)
                    pe.matmul(bank[:, Y_BANK[p][h]], ident[:], prod[:, slot, h], start=False,
                              stop=stop).then_inc(s.y_summed, 1)

            pe.wait_ge(s.region_free, 1)
            pe.wait_ge(s.dg_made, 2)
            for p in range(2):
                t0 = p * DS
                for h in range(2):
                    pe.matmul(bank[:, Y_BANK[p][h]], dg[:, h, :], cu[:, h, cols(p)], start=True, stop=False)
                broadcast_b(p, t0, 0, 0)
                broadcast_b(p, t0 + 1, 0, 1)
                broadcast_c(p, t0, 0, 0)

                def two_steps(m):
                    for i in range(2):
                        broadcast_b(p, 2 * m + (t0 + 2 + i), m + 1, i)
                        broadcast_c(p, 2 * m + (t0 + 1 + i), m + i, 1 - i)
                        ysum(p, 2 * m + (t0 + i), i)

                two_steps(0)
                with pe.Fori(1, DS // 2 - 1) as m:
                    two_steps(m)
                broadcast_c(p, t0 + DS - 1, DS // 2 - 1, 1)
                ysum(p, t0 + DS - 2, 0)
                ysum(p, t0 + DS - 1, 1, stop=True)
                pe.wait_ge(s.gated, 2 * p + 2)
                for b in range(2):
                    for lt in range(2):
                        for h in range(2):
                            mm = pe.transpose(bank[:, Y_BANK[p][b], lt * DM + h * P:lt * DM + (h + 1) * P],
                                              sz[:, 4 * p + 2 * b + h, lt * P:(lt + 1) * P], ident[:])
                    mm.then_inc(s.mix_psum, 1)

            def transpose_rows(made, psum):
                pe.wait_ge(made, NT)
                for k in range(2):
                    for j in range(NT):
                        mm = pe.transpose(bank[:, 1 + 2 * k + j // 4, (j % 4) * P:(j % 4 + 1) * P],
                                          xn[:, j, k * P:(k + 1) * P], ident[:])
                mm.then_inc(psum, 1)

            for ly in layers:
                ls = ly.s
                if ly.i == 0:
                    pe.wait_ge(s.x1_made, 4)
                else:
                    pe.wait_ge(s.att_in, 64)
                    pe.wait_ge(s.l1_in, 80)
                    pe.wait_ge(lp.y_made, layers[0].tiles)
                    for c, w in enumerate((wq, wk)):
                        pe.transpose(bank[:, 5, c * P:(c + 1) * P], w[:], ident[:])
                    for k in range(2):
                        mm = pe.transpose(bank[:, 5, 2 * P + k * E1:2 * P + (k + 1) * E1], wr_rows[:, k * P:(k + 1) * P],
                                          ident[0:E1, 0:E1])
                    mm.then_inc(a.wqkT_psum, 1)
                    pe.wait_ge(a.wqkT_made, 2)
                    for c in range(4):
                        p = c % 2
                        pe.matmul(bank[:, (5, 6, 7, 0)[c]], wqkT[:, c // 2, :], ctxT[:, 2 * p:2 * p + 2, TAPS - 1:],
                                  start=True, stop=True).then_inc(a.qk_psum, 1)
                    pe.wait_ge(a.qk_made, 4)
                    for n in range(2 * B + 1):
                        if n < 2 * B:
                            b = n // 2
                            if n >= 2:
                                pe.wait_ge(a.aexp_made, n - 1)
                            pe.matmul(bank[:, 5 + n % 2, 0:L], qT[:, n * P:(n + 1) * P], kT[:, b * L:(b + 1) * L],
                                      start=True, stop=True).then_inc(a.e_psum, 1)
                        if n >= 1:
                            i = n - 1
                            pe.wait_ge(a.att_made, i + 1)
                            if i >= 2:
                                pe.wait_ge(a.attT_made, i - 1)
                            for k in range(2):
                                mm = pe.transpose(bank[:, (7, 0)[i % 2], k * P:(k + 1) * P],
                                                  att[:, i % 2, k * P:(k + 1) * P], ident[:])
                            mm.then_inc(a.attT_psum, 1)
                    transpose_rows(a.xn_made, a.xnT_psum)
                    pe.wait_ge(a.xnT_a, 2)
                    pe.wait_ge(a.xnT_v, 2)
                    pe.wait_ge(a.attT_made, 2 * B)
                    for j in range(NT):
                        if j >= 2:
                            pe.wait_ge(a.x3_made, j - 1)
                        for k in range(2):
                            mm = pe.matmul(bank[:, 5 + j % 2, 0:L], xnT[:, k, j * P:(j + 1) * P], attT[:, j // 2, k, :],
                                           start=k == 0, stop=k == 1)
                        mm.then_inc(a.att_psum, 1)
                transpose_rows(ls.xn_made, ls.xnT_psum)
                router, rbias = ((router0, rbias0), (router1, rbias1))[ly.i]
                pe.wait_ge(s.l0_in, 96)
                pe.wait_ge(ls.xnT_a, 2)
                pe.wait_ge(ls.xnT_v, 2)
                for j in range(NT):
                    dst = bank[:, 5, j * ly.E:(j + 1) * ly.E]
                    pe.matmul(dst, ones_row[:], rbias[:], start=True, stop=False)
                    for k in range(2):
                        mm = pe.matmul(dst, xnT[:, k, j * P:(j + 1) * P], router[:, k, :], start=False, stop=k == 1)
                mm.then_inc(ls.logits_psum, 1)
                pe.wait_ge(ls.chosen_made, 1)
                W = NT * ly.E
                pe.matmul(bank[:, 6, 0:W], before[:], ly.chosen, start=True, stop=False)
                for d in range(1, NT):
                    mm = pe.matmul(bank[:, 6, d * ly.E:W], ones16[:], ly.chosen[:, 0:W - d * ly.E],
                                   start=False, stop=d == NT - 1)
                mm.then_inc(ls.rank_psum, 1)
                for j in range(NT):
                    mm = pe.matmul(bank[:, 7, 0:ly.E], ones16[:], ly.chosen[:, j * ly.E:(j + 1) * ly.E],
                                   start=j == 0, stop=j == NT - 1)
                mm.then_inc(ls.rank_psum, 1)
                if ly.i == 1:
                    for c in range(2):
                        if c:
                            pe.wait_ge(ls.sh_made, c)
                        for g, w in enumerate((swg, swu)):
                            for k in range(2):
                                mm = pe.matmul(bank[:, 1 + g], w[:, k, :], xnT[:, k, cols(c)], start=k == 0, stop=k == 1)
                            mm.then_inc(ls.sh_psum, 1)
                for j in range(NT):
                    for k in range(ly.K):
                        n = j * ly.K + k
                        pe.wait_ge(ls.hot_made, 2 * n + 2)
                        pe.matmul(bank[:, 0, 0:ly.tiles], slot_hot[:, k, :], tile_tok[:, k, 0:ly.tiles],
                                  start=n == 0, stop=n == NT * ly.K - 1).then_inc(ls.map_used, 1)
                pe.wait_ge(ls.owner_made, 1)
                pe.transpose(bank[0:1, 7, 0:P], owner[:], ident[:]).then_inc(ls.owner_psum, 1)

                def rows_in(t0, u):
                    pe.wait_ge(lp.gathered[u], slot_count(t0, ly.slot_done[u] + 1))
                    if not first_tiles(t0, u, 2):
                        pe.wait_ge(lp.xgT_made, t0 + (ly.done + u - 1))
                    for k in range(2):
                        mm = pe.transpose(bank[:, u % 2, k * P:(k + 1) * P], xg[:, u, k * P:(k + 1) * P], ident[:])
                    mm.then_inc(lp.xgT_psum, 1)

                PE = mybir.EngineType.PE
                owners = [None] * U

                def down(t0, u):
                    e = owners[u]
                    pe.wait_ge(lp.hidT_made, t0 + (ly.done + u + 1))
                    if not first_tiles(t0, u, 2):
                        pe.wait_ge(lp.y_made, t0 + (ly.done + u - 1))
                    dst = bank[:, 6 + u % 2, 0:DM]
                    if ly.i == 0:
                        pe.matmul(dst, hidT[0:HH, u % 2, 0], w2[0:HH, bass.ds(e, 1), 0, :], start=True, stop=False)
                        mm = pe.matmul(dst, hidT[0:HH + 1, u % 2, 1], w2[0:HH + 1, bass.ds(e, 1), 1, :],
                                       start=False, stop=True)
                    else:
                        mm = pe.matmul(dst, hidT[:, u % 2, 0], wd[:, bass.ds(e, 1), :], start=True, stop=True)
                    mm.then_inc(lp.y_psum, 1)

                def tile(t0, u):
                    if u == 0:
                        owners[0] = expert(PE, ly, t0, 0)
                        if not first_tiles(t0, 0, 1):
                            owners[U - 1] = expert(PE, ly, t0 - U, U - 1)
                    e = owners[u]
                    pe.wait_ge(lp.xgT_made, t0 + (ly.done + u + 1))
                    if not first_tiles(t0, u, 2):
                        pe.wait_ge(lp.hid_made, t0 + (ly.done + u - 1))
                    for k in range(2):
                        if ly.i == 0:
                            mm = pe.matmul(bank[:, 2 + u % 2, 0:H0], xgT[:, u % 2, k], w1[:, bass.ds(e, 1), k, :],
                                           start=k == 0, stop=k == 1)
                        else:
                            w = wgu[:].rearrange("p (e k) g i -> p e k (g i)", k=2)
                            mm = pe.matmul(bank[:, 2 + u % 2, 0:2 * H1], xgT[:, u % 2, k], w[:, bass.ds(e, 1), k, :],
                                           start=k == 0, stop=k == 1)
                    mm.then_inc(lp.h_psum, 1)
                    is_last = isinstance(t0, int) and t0 + u == ly.tiles - 1
                    if not is_last:
                        rows_in(*after(t0, u))
                    if not first_tiles(t0, u, 1):
                        down(t0 if u else t0 - U, (u - 1) % U)
                    if u < U - 1 and not is_last:
                        owners[u + 1] = expert(PE, ly, t0, u + 1)
                    pe.wait_ge(lp.hid_made, t0 + (ly.done + u + 1))
                    if not first_tiles(t0, u, 2):
                        pe.wait_ge(lp.hidT_made, t0 + (ly.done + u - 1))
                    if ly.i == 0:
                        for k in range(2):
                            mm = pe.transpose(bank[0:HH, 4 + u % 2, k * P:(k + 1) * P],
                                              hid[:, u % 2, k * HH:(k + 1) * HH], ident[:])
                    else:
                        mm = pe.transpose(bank[:, 4 + u % 2, 0:P], hid[:, u % 2, 0:H1], ident[:])
                    mm.then_inc(lp.hidT_psum, 1)

                pe.wait_ge(ls.tok_made, 1)
                pe.wait_ge(ls.owner_ready, 1)
                if ly.i == 0:
                    pe.wait_ge(s.w1_in, 64)
                    pe.wait_ge(s.w2_in, 80)
                else:
                    pe.wait_ge(a.wgu_in, 80)
                rows_in(0, 0)
                turns(pe, ly, tile)
                down(ly.last, U - 2)
                pe.wait_ge(lp.y_made, ly.done + ly.tiles)
                if ly.i == 0:
                    for n in range(NSH * 4):
                        em, c = n // 2, n % 2
                        if n >= 2:
                            pe.wait_ge(ls.sh_made, n - 1)
                        for k in range(2):
                            mm = pe.matmul(bank[0:HH, 1 + n % 2], sw1[:, em // 2 * 2 + k, em % 2 * HH:(em % 2 + 1) * HH],
                                           xnT[:, k, cols(c)], start=k == 0, stop=k == 1)
                        mm.then_inc(ls.sh_psum, 1)
                    pe.wait_ge(ls.sh_made, NSH * 4)
                for j in range(NT):
                    if j >= 2:
                        pe.wait_ge(ls.based, j - 1)
                    tok = slice(j * P, (j + 1) * P)
                    if ly.i == 0:
                        for em in range(NSH * 2):
                            K = HH + em % 2
                            mm = pe.matmul(bank[:, 3 + j % 2, 0:DM], shT[0:K, em, tok], sw2[0:K, em // 2, em % 2, :],
                                           start=em == 0, stop=em == NSH * 2 - 1)
                    else:
                        mm = pe.matmul(bank[:, 3 + j % 2, 0:DM], shT1[:, tok], swd[:], start=True, stop=True)
                    mm.then_inc(ls.base_psum, 1)

        @block.vector
        def _(dve):
            def link(ins):
                ins.then_inc(s.dve_step, 1)
                steps[0] += 1
                dve.wait_ge(s.dve_step, steps[0])

            steps = [0]
            dve.wait_ge(s.mamba_in, 128)
            for h in range(2):
                for k in range(TAPS):
                    dve.tensor_scalar(wcv[:, h, k, :], wip[:, h, :], cw[:, h, k:k + 1], None,
                                      ALU.mult).then_inc(s.wcv_made, 1)
            dve.tensor_scalar(hcb[:], cb[:], 0.5, None, ALU.mult).then_inc(s.hcb_made, 1)
            dve.wait_ge(s.consts, 2)
            for h in range(2):
                dve.tensor_scalar(dg[:, h, :], ident[:], dsk[:, h:h + 1], None, ALU.mult).then_inc(s.dg_made, 1)

            dve.wait_ge(s.x_in, 16)
            for j in range(NT):
                ins = dve.bn_stats(stats[:, j, :], xs[:, j, :])
            link(ins)
            for j in range(NT):
                ins = dve.bn_aggr(meanvar[:, j, :], stats[:, j, :])
            link(ins)
            dve.tensor_scalar(vareps[:], meanvar[:, :, 1], EPS_LN, None, ALU.add).then_inc(s.var_made, 1)

            for i in range(2):
                dve.wait_ge(s.wcT_psum, i + 1)
                dve.tensor_copy(flat(wcT, CH, i * CH), bank[:, 2 + i]).then_inc(s.wcT_made, 1)
            dve.wait_ge(s.xw_psum, 1)
            xw = bank[:, 4, 0:2 * (DR + NB)].rearrange("p (h c) -> p h c", h=2)
            for r in range(3):
                dve.tensor_copy(wbcT[:, :, r * NB:(r + 1) * NB], xw[:, :, DR:]).then_inc(s.xw_made, 1)
            dve.tensor_copy(wdtT[:], xw[:, :, 0:DR]).then_inc(s.xw_made, 1)
            dve.tensor_copy(dtpT[:], bank[0:DR, 4, P:3 * P].rearrange("p (h c) -> p h c", h=2)).then_inc(s.xw_made, 1)

            dve.wait_ge(s.rstd_made, 1)
            for j in range(NT):
                dve.tensor_scalar(sz[:, j, :], xs[:, j, :], meanvar[:, j, 0:1], rstd[:, j:j + 1],
                                  ALU.subtract, ALU.mult).then_inc(s.z_normed, 1)

            dve.wait_ge(s.hcb_made, 1)
            for p in range(2):
                for h in range(2):
                    q = 2 * p + h
                    dve.wait_ge(s.th_made, q + 1)
                    link(dve.tensor_scalar(cu[:, h, cols(p)], bank[:, CONV_BANK[q]], 0.5, hcb[:, h:h + 1],
                                           ALU.mult, ALU.add))
                    dve.scalar_tensor_tensor(cu[:, h, cols(p)], th[:, h], 1.0, cu[:, h, cols(p)],
                                             ALU.add, ALU.mult).then_inc(s.u_made, 1)
            for p in range(2):
                dve.wait_ge(s.hi_made, 2 * p + 2)
                ps = bank[:, 1 + p]
                dve.tensor_tensor(bcp[NB:2 * NB, cols(p)], ps[NB:2 * NB], part16[NB:2 * NB],
                                  ALU.subtract).then_inc(s.parts_made, 1)
                dve.tensor_tensor(part[2 * NB:3 * NB], ps[2 * NB:3 * NB], part16[2 * NB:3 * NB],
                                  ALU.subtract).then_inc(s.parts_made, 1)
                dve.wait_ge(s.parts_made, 4 * p + 2)
                dve.tensor_copy(part16[2 * NB:3 * NB], part[2 * NB:3 * NB]).then_inc(s.parts_made, 1)
                dve.wait_ge(s.parts_made, 4 * p + 3)
                dve.tensor_tensor(bcp[2 * NB:3 * NB, cols(p)], part[2 * NB:3 * NB], part16[2 * NB:3 * NB],
                                  ALU.subtract).then_inc(s.parts_made, 1)
            for i in range(4):
                dve.wait_ge(s.z_th, i + 1)
                dve.scalar_tensor_tensor(flat(sz, CH, i * CH), sp3[:, i % 2], 1.0, flat(sz, CH, i * CH),
                                         ALU.add, ALU.mult).then_inc(s.z_made, 1)
            for q in range(4):
                p, h = q // 2, q % 2
                dve.wait_ge(s.abs_made, q + 1)
                link(dve.tensor_scalar(delta[:, h, cols(p)], bank[:, CONV_BANK[q]], dtb[:, h:h + 1], 0.0,
                                       ALU.add, ALU.max))
                dve.wait_ge(s.exp_made, q + 1)
                dve.wait_ge(s.ln_made, q + 1)
                dve.tensor_scalar(th[:, h], sp2[:, h], 1.0, -1.0, ALU.add, ALU.add).then_inc(s.w_made_1, 1)
                link(dve.tensor_tensor(delta[:, h, cols(p)], delta[:, h, cols(p)], sp3[:, h], ALU.add))
                dve.wait_ge(s.low_made, q + 1)
                dve.tensor_tensor(delta[:, h, cols(p)], delta[:, h, cols(p)], sp2[:, h],
                                  ALU.add).then_inc(s.delta_made, 1)
            dve.wait_ge(s.du_made, 4)
            dve.memset(decay[:, :, :, :, 0:1].rearrange("p a b c o -> p (a b c) o"), 0.0).then_inc(s.region_free, 1)

            def step(p, t, slot):
                for h in range(2):
                    dve.wait_ge(s.decay_made, 2 * t + h + 1)
                    dve.wait_ge(s.inflow_made, 2 * t + h + 1)
                    if not (isinstance(t, int) and t < 1):
                        dve.wait_ge(s.prod_made, 2 * (t - 1) + h + 1)
                    dve.tensor_tensor_scan(state[:, h], decay[:, slot, h].rearrange("p b l -> p (b l)"),
                                           inflow[:, slot, h], 0.0, ALU.mult, ALU.add).then_inc(s.scanned, 1)
                for h in range(2):
                    if h == 0:
                        dve.wait_ge(s.c_bcast, t + 1)
                    dve.wait_ge(s.scanned, 2 * t + h + 1)
                    if not (isinstance(t, int) and t < 2):
                        dve.wait_ge(s.y_summed, 2 * (t - 2) + h + 1)
                    dve.tensor_tensor(prod[:, slot, h], state[:, h], bank[:, 3 + slot],
                                      ALU.mult).then_inc(s.prod_made, 1)

            dve.wait_ge(s.region_free, 1)
            dve.wait_ge(s.gates_made, 1)
            link(dve.tensor_scalar(hg[:], gates[:, 0:1], 0.5, None, ALU.mult))
            for p in range(2):
                t0 = p * DS
                for i in range(2):
                    step(p, t0 + i, i)
                with dve.Fori(1, DS // 2) as m:
                    for i in range(2):
                        step(p, 2 * m + (t0 + i), i)
                dve.wait_ge(s.y_summed, 2 * (t0 + DS))
                dve.wait_ge(s.z_made, 4)
                for h in range(2):
                    z = sz[:, 4 * p + h:4 * p + 4:2, :]
                    dve.tensor_tensor(z, z, bank[:, Y_BANK[p][h]].rearrange("p (b l) -> p b l", b=2),
                                      ALU.mult).then_inc(s.gated, 1)
                for b in range(2):
                    j = 4 * p + 2 * b
                    dve.wait_ge(s.mix_psum, 2 * p + b + 1)
                    dve.scalar_tensor_tensor(flat(xs, CH, j * DM), bank[:, Y_BANK[p][b]], hg[:, 0:1],
                                             flat(xs, CH, j * DM), ALU.mult, ALU.add).then_inc(s.x1_made, 1)

            def layer_norm(k, made):
                for j in range(NT):
                    ins = dve.bn_stats(stats[:, j, :], xs[:, j, :])
                link(ins)
                for j in range(NT):
                    ins = dve.bn_aggr(meanvar[:, j, :], stats[:, j, :])
                link(ins)
                dve.tensor_scalar(vareps[:], meanvar[:, :, 1], EPS_LN, None, ALU.add).then_inc(s.var_made, 1)
                dve.wait_ge(s.rstd_made, k)
                for j in range(NT):
                    dve.tensor_scalar(xn[:, j, :], xs[:, j, :], meanvar[:, j, 0:1], rstd[:, j:j + 1],
                                      ALU.subtract, ALU.mult).then_inc(made, 1)

            def transposed_half(psum, made):
                for c in range(2):
                    dve.wait_ge(psum, 1)
                    dve.tensor_copy(xnT[:, 1, cols(c)], bank[:, 3 + c]).then_inc(made, 1)

            dve.wait_ge(s.x1_made, 4)
            for g in range(2):
                dve.tensor_scalar(hg_moe[:, g:g + 1], gates[:, 2 + g:3 + g], 0.5, None, ALU.mult).then_inc(a.hg_made, 1)
            for ly in layers:
                ls = ly.s
                if ly.i == 1:
                    dve.wait_ge(a.wqkT_psum, 1)
                    dve.tensor_copy(flat(wqkT, 2 * P), bank[:, 5, 0:2 * P]).then_inc(a.wqkT_made, 1)
                    dve.tensor_copy(flat(router1, 2 * E1), bank[:, 5, 2 * P:2 * P + 2 * E1]).then_inc(a.wqkT_made, 1)
                    for n in range(2 * B):
                        dve.wait_ge(a.e_psum, n + 1)
                        dve.tensor_reduce(att_neg[:, n:n + 1], bank[:, 5 + n % 2, 0:L], AX.X, ALU.max,
                                          negate=True).then_inc(a.neg_made, 1)
                        dve.wait_ge(a.aexp_made, n + 1)
                        dve.reciprocal(att_rec[:, n:n + 1], att_sum[:, n:n + 1]).then_inc(a.rec_made, 1)
                        dve.wait_ge(a.rec_made, n + 1)
                        dve.tensor_scalar(att[:, n % 2], att[:, n % 2], att_rec[:, n:n + 1], None,
                                          ALU.mult).then_inc(a.att_made, 1)
                    layer_norm(3, a.xn_made)
                    transposed_half(a.xnT_psum, a.xnT_v)
                    for j in range(NT):
                        dve.wait_ge(a.att_psum, j + 1)
                        dve.scalar_tensor_tensor(xs[:, j, :], bank[:, 5 + j % 2, 0:L], gates[:, 1:2], xs[:, j, :],
                                                 ALU.mult, ALU.add).then_inc(a.x3_made, 1)
                    dve.wait_ge(a.x3_made, NT)
                layer_norm(2 + 2 * ly.i, ls.xn_made)
                transposed_half(ls.xnT_psum, ls.xnT_v)

                E, K = ly.E, ly.K
                dve.wait_ge(ls.logits_psum, 1)
                link(dve.tensor_copy(flat(logits, NT * E), bank[:, 5, 0:NT * E]))
                for j in range(NT):
                    ins = dve.max(top[:, j, :], ly.logits[:, j, :])
                link(ins)
                for j in range(NT):
                    ins = dve.max_index(topi[:, j, :], top[:, j, :], ly.logits[:, j, :])
                link(ins)
                largest = top[:, :, 0:1]
                ins = dve.tensor_tensor(ly.wexp, top[:, :, 0:K], largest.to_broadcast([P, NT, K]), ALU.subtract)
                if ly.i == 1:
                    ins = dve.tensor_tensor(ly.posf, ly.logits, largest.to_broadcast([P, NT, E]), ALU.subtract)
                ins.then_inc(ls.shifted, 1)
                link(dve.tensor_copy(topf[:], topi[:]))
                link(dve.tensor_tensor(ly.hot, iota_f[:, 0:E].unsqueeze(1).unsqueeze(1).to_broadcast([P, NT, K, E]),
                                       topf[:, :, 0:K].unsqueeze(3).to_broadcast([P, NT, K, E]), ALU.is_equal))
                with nc.allow_low_precision(reason="sums of zeros and one one"):
                    dve.tensor_reduce(ly.chosen.rearrange("p (j e) -> p j e", e=E),
                                      ly.hot.rearrange("p j k e -> p j e k"), AX.X, ALU.add).then_inc(ls.chosen_made, 1)
                dve.wait_ge(ls.exped, 1 + ly.i)
                link(dve.tensor_reduce(wsum[:], ly.wexp, AX.X, ALU.add))
                if ly.i == 1:
                    link(dve.tensor_reduce(wall[:], ly.posf, AX.X, ALU.add))
                    link(dve.scalar_tensor_tensor(wsum[:], wall[:], 1e-9, wsum[:], ALU.mult, ALU.add))
                link(dve.reciprocal(wrec[:], wsum[:]))
                link(dve.tensor_tensor(ly.wgt, ly.wexp, wrec[:].unsqueeze(2).to_broadcast([P, NT, K]), ALU.mult))
                dve.wait_ge(a.hg_made, 2)
                gate = (gates[:, 2:3], hg_moe[:, 1:2])[ly.i]
                link(dve.tensor_scalar(ly.wgt_g, ly.wgt, gate, None, ALU.mult))
                dve.wait_ge(ls.rank_psum, 2)
                link(dve.tensor_tensor(ly.full, bank[:, 7, 0:E].unsqueeze(2).to_broadcast([P, E, NT]),
                                       fill_f[:].unsqueeze(1).to_broadcast([P, E, NT]), ALU.is_gt))
                link(dve.tensor_reduce(ntiles[:, 0:E], ly.full, AX.X, ALU.add))
                link(dve.tensor_tensor_scan(tile_end[:, 0:E], ntiles[:, 0:E], ntiles[:, 0:E], 0.0, ALU.add, ALU.max))
                link(dve.tensor_scalar(ended[:, 0:E], tile_end[:, 0:E], tokid[:, 0:1], None, ALU.is_le))
                link(dve.tensor_reduce(owner[:], ended[:, 0:E], AX.X, ALU.add))
                dve.tensor_scalar(owner[:], owner[:], float(E - 1), None, ALU.min).then_inc(ls.owner_made, 1)
                link(dve.tensor_tensor(row0[:, 0:E], tile_end[:, 0:E], ntiles[:, 0:E], ALU.subtract))
                link(dve.tensor_scalar(row0[:, 0:E], row0[:, 0:E], float(P), None, ALU.mult))
                link(dve.tensor_tensor(ly.posf, bank[:, 6, 0:NT * E].rearrange("p (j e) -> p j e", e=E),
                                       row0[:, 0:E].unsqueeze(1).to_broadcast([P, NT, E]), ALU.add))
                link(dve.tensor_tensor(ly.hot, ly.hot, ly.posf.unsqueeze(2).to_broadcast([P, NT, K, E]), ALU.mult))
                link(dve.tensor_reduce(ly.rowf.rearrange("p (j k) -> p j k", k=K), ly.hot, AX.X, ALU.add))
                rows = flat(row_i, NT * K)
                link(dve.tensor_copy(rows, ly.rowf))
                dve.tensor_scalar(ly.tile_i, rows, P.bit_length() - 1, None, ALU.logical_shift_right)
                link(dve.tensor_scalar(ly.slot_i, rows, P - 1, None, ALU.bitwise_and))
                dve.tensor_copy(flat(tile_f, NT * K), ly.tile_i)
                link(dve.tensor_copy(flat(slot_f, NT * K), ly.slot_i))
                if ly.i == 1:
                    for c in range(2):
                        dve.wait_ge(a.sh_gate, c + 1)
                        dve.scalar_tensor_tensor(gu[:], gg[:], 1.0, bank[:, 1], ALU.add, ALU.mult).then_inc(a.sh_half, 1)
                        dve.wait_ge(a.sh_half, c + 1)
                        dve.wait_ge(ls.sh_psum, 2 * c + 2)
                        dve.tensor_tensor(shT1[:, cols(c)], gu[:], bank[:, 2], ALU.mult).then_inc(ls.sh_made, 1)

                def choices(j):
                    for k in range(K):
                        if not isinstance(j, int):
                            dve.wait_ge(ls.map_used, j * K + (k + 1 - K))
                        token = bass.ds(j, 1)
                        dve.tensor_scalar(slot_hot[:, k, :], iota_h[:], ly.slot_f[:, token, k], None,
                                          ALU.is_equal).then_inc(ls.hot_made, 1)
                        dve.tensor_scalar(tile_tok[:, k, 0:ly.tiles], iota_h[:, 0:ly.tiles], ly.tile_f[:, token, k],
                                          tokid[:, token], ALU.is_equal, ALU.mult).then_inc(ls.hot_made, 1)

                choices(0)
                with dve.Fori(1, NT) as j:
                    choices(j)
                dve.wait_ge(ls.map_used, NT * K)
                dve.tensor_copy(tok_of[:, 0:ly.tiles], bank[:, 0, 0:ly.tiles]).then_inc(ls.tok_made, 1)
                dve.wait_ge(ls.owner_psum, 1)
                dve.tensor_copy(owner_i[:], bank[0:1, 7, 0:P]).then_inc(ls.owner_ready, 1)

                if ly.i == 0:
                    dve.wait_ge(s.b1_in, 16)
                    dve.memset(hidT[64:HH + 1], 1.0).then_inc(a.hidT_ones, 1)
                dve.wait_ge(ls.owner_ready, 1)

                def y_out(t0, u):
                    dve.wait_ge(lp.y_psum, t0 + (ly.done + u + 1))
                    if not first_tiles(t0, u, U):
                        dve.wait_ge(lp.y_out[u], slot_count(t0, ly.slot_done[u]))
                    dve.tensor_copy(yt[:, u, :], bank[:, 6 + u % 2, 0:DM]).then_inc(lp.y_made, 1)

                def tile(t0, u):
                    v = u % 2
                    if not first_tiles(t0, u, 2):
                        dve.wait_ge(lp.hidT_psum, t0 + (ly.done + u - 1))
                    if ly.i == 0:
                        e = expert(mybir.EngineType.DVE, ly, t0, u)
                        dve.wait_ge(lp.h_psum, t0 + (ly.done + u + 1))
                        dve.tensor_tensor(hid[:, v, 0:H0], bank[:, 2 + v, 0:H0], b1_bc[:, bass.ds(e, 1), :].squeeze(1),
                                          ALU.add).then_inc(lp.hid_made, 1)
                    else:
                        dve.wait_ge(lp.gate_made, t0 + (u + 1))
                        dve.scalar_tensor_tensor(hid[:, v, 0:H1], gate_th[:, v], 1.0, bank[:, 2 + v, 0:H1],
                                                 ALU.add, ALU.mult).then_inc(lp.half_made, 1)
                        dve.wait_ge(lp.half_made, t0 + (u + 1))
                        dve.tensor_tensor(hid[:, v, 0:H1], hid[:, v, 0:H1], bank[:, 2 + v, H1:2 * H1],
                                          ALU.mult).then_inc(lp.hid_made, 1)
                    if not first_tiles(t0, u, 1):
                        y_out(t0 if u else t0 - U, (u - 1) % U)

                turns(dve, ly, tile)
                y_out(ly.last, U - 2)
                if ly.i == 0:
                    dve.wait_ge(lp.y_psum, ly.done + ly.tiles)
                    dve.memset(shT[64:HH + 1], 1.0).then_inc(a.shT_ones, 1)
                for j in range(NT):
                    dve.wait_ge(ls.base_psum, j + 1)
                    dve.scalar_tensor_tensor(xs[:, j, :], bank[:, 3 + j % 2, 0:DM], hg_moe[:, ly.i:ly.i + 1], xs[:, j, :],
                                             ALU.mult, ALU.add).then_inc(ls.based, 1)
                dve.wait_ge(ls.based, NT)
                for j in range(NT):
                    dve.wait_ge(ls.got_in[j % 2], 16 * K * (j // 2 + 1))
                    for k in range(K):
                        ins = dve.scalar_tensor_tensor(xs[:, j, :], got[:, j % 2, k, :], ly.wgt_g[:, j, k:k + 1],
                                                       xs[:, j, :], ALU.mult, ALU.add)
                        if k < K - 1:
                            link(ins)
                    ins.then_inc(ls.added, 1)
                dve.wait_ge(ls.added, NT)


_OUT = ((4, 256, 256), "float32")


def kernel(**inputs):
    import numpy as _np
    import concourse.bacc as _bacc
    from concourse.bass_utils import run_bass_kernel_spmd as _run

    nc = _bacc.Bacc("TRN2", target_bir_lowering=False, num_devices=1)
    arrays, io = {}, {}
    for name, value in inputs.items():
        value = _np.ascontiguousarray(value)
        arrays[f"in_{name}"] = value
        io[name] = nc.dram_tensor(f"in_{name}", value.shape, mybir.dt.from_np(value.dtype), kind="ExternalInput").ap()
    out = nc.dram_tensor("out_x", _OUT[0], F32, kind="ExternalOutput").ap()
    flamingo_two_layer_kernel(nc, io, out)
    result = _run(nc, [arrays], core_ids=[0])
    return result.results[0]["out_x"]
```

```python
from contextlib import ExitStack

import concourse.bass as bass
from concourse import mybir
from concourse.alu_op_type import AluOpType as ALU

F32 = mybir.dt.float32
BF16 = mybir.dt.bfloat16
F16 = mybir.dt.float16
I32 = mybir.dt.int32
U32 = mybir.dt.uint32
ACT = mybir.ActivationFunctionType
AX = mybir.AxisListType

P = 128
EPS_LN = 1e-5


class MambaSemaphores:

    def __init__(self, new):
        self.consts = new("consts")
        self.ctx_in = new("ctx_in")
        self.mamba_in = new("mamba_in")
        self.gates_in = new("gates_in")
        self.x_in = new("x_in")
        self.att_in = new("att_in")
        self.l0_in = new("l0_in")
        self.l1_in = new("l1_in")
        self.w1_in = new("w1_in")
        self.w2_in = new("w2_in")
        self.b1_in = new("b1_in")
        self.gates_made = new("gates_made")
        self.hcb_made = new("hcb_made")
        self.wcv_made = new("wcv_made")
        self.dg_made = new("dg_made")
        self.var_made = new("var_made")
        self.rstd_made = new("rstd_made")
        self.dve_step = new("dve_step")
        self.pool_step = new("pool_step")
        self.ctxT_psum = new("ctxT_psum")
        self.ctxT_made = new("ctxT_made")
        self.wcT_psum = new("wcT_psum")
        self.wcT_made = new("wcT_made")
        self.xw_psum = new("xw_psum")
        self.xw_made = new("xw_made")
        self.a_made = new("a_made")
        self.conv_psum = new("conv_psum")
        self.th_made = new("th_made")
        self.u_made = new("u_made")
        self.bc_psum = new("bc_psum")
        self.dt_psum = new("dt_psum")
        self.hi_made = new("hi_made")
        self.dtl_made = new("dtl_made")
        self.parts_made = new("parts_made")
        self.dpre_psum = new("dpre_psum")
        self.abs_made = new("abs_made")
        self.exp_made = new("exp_made")
        self.ln_made = new("ln_made")
        self.w_made_1 = new("w_made_1")
        self.low_made = new("low_made")
        self.delta_made = new("delta_made")
        self.du_made = new("du_made")
        self.z_normed = new("z_normed")
        self.z_th = new("z_th")
        self.z_made = new("z_made")
        self.region_free = new("region_free")
        self.b_bcast = new("b_bcast")
        self.c_bcast = new("c_bcast")
        self.b_copied = new("b_copied")
        self.decay_made = new("decay_made")
        self.inflow_made = new("inflow_made")
        self.scanned = new("scanned")
        self.prod_made = new("prod_made")
        self.y_init = new("y_init")
        self.y_summed = new("y_summed")
        self.gated = new("gated")
        self.mix_psum = new("mix_psum")
        self.x1_made = new("x1_made")


class LayerSemaphores:

    def __init__(self, new, i):
        self.xn_out = new(f"xn_out_l{i}")
        self.logits_psum = new(f"logits_psum_l{i}")
        self.shifted = new(f"shifted_l{i}")
        self.exped = new(f"exped_l{i}")
        self.chosen_made = new(f"chosen_made_l{i}")
        self.rank_psum = new(f"rank_psum_l{i}")
        self.hot_made = new(f"hot_made_l{i}")
        self.map_used = new(f"map_used_l{i}")
        self.tok_made = new(f"tok_made_l{i}")
        self.owner_made = new(f"owner_made_l{i}")
        self.owner_psum = new(f"owner_psum_l{i}")
        self.owner_ready = new(f"owner_ready_l{i}")
        self.sh_psum = new(f"sh_psum_l{i}")
        self.sh_made = new(f"sh_made_l{i}")
        self.base_psum = new(f"base_psum_l{i}")
        self.based = new(f"based_l{i}")
        self.added = new(f"added_l{i}")
        self.got_in0 = new(f"got_in0_l{i}")
        self.got_in1 = new(f"got_in1_l{i}")
        self.got_in2 = new(f"got_in2_l{i}")
        self.got_in3 = new(f"got_in3_l{i}")
        self.got_in = [self.got_in0, self.got_in1, self.got_in2, self.got_in3]


class LoopSemaphores:

    def __init__(self, new):
        self.xgT_psum = new("xgT_psum")
        self.xgT_made = new("xgT_made")
        self.h_psum = new("h_psum")
        self.gate_made = new("gate_made")
        self.half_made = new("half_made")
        self.hid_made = new("hid_made")
        self.hidT_psum = new("hidT_psum")
        self.hidT_made = new("hidT_made")
        self.y_psum = new("y_psum")
        self.y_made = new("y_made")
        self.gathered0 = new("gathered0")
        self.gathered1 = new("gathered1")
        self.gathered2 = new("gathered2")
        self.gathered3 = new("gathered3")
        self.y_out0 = new("y_out0")
        self.y_out1 = new("y_out1")
        self.y_out2 = new("y_out2")
        self.y_out3 = new("y_out3")
        self.gathered = [self.gathered0, self.gathered1, self.gathered2, self.gathered3]
        self.y_out = [self.y_out0, self.y_out1, self.y_out2, self.y_out3]


class AttentionSemaphores:

    def __init__(self, new):
        self.wqkT_psum = new("wqkT_psum")
        self.wqkT_made = new("wqkT_made")
        self.qk_psum = new("qk_psum")
        self.qk_made = new("qk_made")
        self.e_psum = new("e_psum")
        self.neg_made = new("neg_made")
        self.aexp_made = new("aexp_made")
        self.rec_made = new("rec_made")
        self.att_made = new("att_made")
        self.attT_psum = new("attT_psum")
        self.attT_made = new("attT_made")
        self.att_psum = new("att_psum")
        self.x3_made = new("x3_made")
        self.out_done = new("out_done")
        self.hg_made = new("hg_made")
        self.shT_ones = new("shT_ones")
        self.hidT_ones = new("hidT_ones")
        self.wgu_in = new("wgu_in")
        self.sh_gate = new("sh_gate")
        self.sh_half = new("sh_half")


class NormSemaphores:

    def __init__(self, new):
        self.var_found = new("var_found")
        self.std_found = new("std_found")
        self.normed = new("normed")
        self.turned_psum = new("turned_psum")
        self.turned = new("turned")


class Layer:

    def __init__(self, i, done, slot_done, E, K, tiles, last, s, rows, y_rows, logits, chosen, posf, full,
                 hot, wexp, wgt, wgt_g, rowf, row_i, tile_i, slot_i, tile_f, slot_f):
        self.i = i
        self.done = done
        self.slot_done = slot_done
        self.E = E
        self.K = K
        self.tiles = tiles
        self.last = last
        self.s = s
        self.rows = rows
        self.y_rows = y_rows
        self.logits = logits
        self.chosen = chosen
        self.posf = posf
        self.full = full
        self.hot = hot
        self.wexp = wexp
        self.wgt = wgt
        self.wgt_g = wgt_g
        self.rowf = rowf
        self.row_i = row_i
        self.tile_i = tile_i
        self.slot_i = slot_i
        self.tile_f = tile_f
        self.slot_f = slot_f


def flamingo_two_layer_kernel(nc, io, out):
    B, L, DM = io["x"].shape
    DC = io["ctx_1024"].shape[2]
    DI = io["L0_xattn_in_proj_w"].shape[0]
    TAPS = io["L0_xattn_conv_w"].shape[1]
    DR = io["L0_xattn_dt_proj_w"].shape[1]
    DS = io["L0_xattn_A_log"].shape[1]
    E0, _, H0 = io["L0_ffn_rw1"].shape
    NSH = io["L0_ffn_sw1"].shape[0]
    E1, _, H1 = io["L1_ffn_Wg"].shape
    K0, K1 = 6, 2
    T = B * L
    NT = T // P
    HH = H0 // 2
    TILES0 = (T * K0 + E0 * (P - 1)) // P
    TILES1 = (T * K1 + E1 * (P - 1)) // P
    CH = 2 * L
    NB = DS * 2
    U = 4
    assert DC == P and DI == 2 * P and DM == 2 * P and L == 2 * P and B == 4 and H1 == P
    assert TILES0 % U == U - 1 and TILES1 % U == U - 1

    with ExitStack() as stack:
        def sb(name, shape, dt=F32, on=stack):
            return on.enter_context(nc.sbuf_tensor(name, shape, dt))

        def semaphore(name):
            return stack.enter_context(nc.semaphore(name))

        bank = stack.enter_context(nc.psum_tensor("bank", [P, 8, 512], F32))

        xn_rows0 = nc.dram_tensor("xn_rows0", [T, DM], F32, kind="Internal").ap()
        xn_rows1 = nc.dram_tensor("xn_rows1", [T, DM], F32, kind="Internal").ap()
        y_rows0 = nc.dram_tensor("y_rows0", [TILES0 * P, DM], F32, kind="Internal").ap()
        y_rows1 = nc.dram_tensor("y_rows1", [TILES1 * P, DM], F32, kind="Internal").ap()

        ident = sb("ident", [P, P])
        eye3 = sb("eye3", [3 * NB, NB], BF16)
        before = sb("before", [P, P], BF16)
        ones16 = sb("ones16", [P, P], BF16)
        ones_row = sb("ones_row", [1, P])
        iota_i = sb("iota_i", [P, P], I32)
        iota_f = sb("iota_f", [P, P])
        iota_h = sb("iota_h", [P, P], F16)
        count_i = sb("count_i", [P, NT], I32)
        fill_f = sb("fill_f", [P, NT])
        tokid = sb("tokid", [P, NT])
        minus_half = sb("minus_half", [P, NT])
        gates_raw = sb("gates_raw", [P, 4])
        gates = sb("gates", [P, 4])
        xs = sb("xs", [P, NT, DM])
        ctxT = sb("ctxT", [P, B, TAPS - 1 + L])
        hg_moe = sb("hg_moe", [P, 2])
        stats = sb("stats", [P, NT, 6])
        meanvar = sb("meanvar", [P, NT, 2])
        vareps = sb("vareps", [P, NT])
        rstd = sb("rstd", [P, NT])
        std = sb("std", [P, NT])
        eps = sb("eps", [P, 1])
        wq = sb("wq", [P, P])
        wk = sb("wk", [P, P])
        wqkT = sb("wqkT", [P, 2, P])
        bqk = sb("bqk", [P, 2])
        router0 = sb("router0", [P, 2, E0])
        rbias0 = sb("rbias0", [1, E0])
        router1 = sb("router1", [P, 2, E1])
        wr_rows = sb("wr_rows", [E1, DM])
        rbias1 = sb("rbias1", [1, E1])
        sw1 = sb("sw1", [P, NSH * 2, H0])
        sb1 = sb("sb1", [HH, NSH, 2])
        sw2 = sb("sw2", [HH + 1, NSH, 2, DM])
        swg = sb("swg", [P, 2, H1])
        swu = sb("swu", [P, 2, H1])
        swd = sb("swd", [P, DM])

        r1 = ExitStack()
        w1 = sb("w1", [P, E0, 2, H0], on=r1)
        r1.close()
        r1 = ExitStack()
        got = sb("got", [P, 4, K0, DM], on=r1)
        gg = sb("gg", [P, CH], on=r1)
        gu = sb("gu", [P, CH], on=r1)
        shT1 = sb("shT1", [P, T], on=r1)
        r1.close()
        hold1 = sb("hold1", [P, E0 * 2 * H0])
        r2 = ExitStack()
        w2 = sb("w2", [HH + 1, E0, 2, DM], on=r2)
        r2.close()
        r2 = ExitStack()
        wgu = sb("wgu", [P, E1 * 2, 2, H1], on=r2)
        wd = sb("wd", [P, E1, DM], on=r2)
        r2.close()
        hold2 = sb("hold2", [P, E0 * 2 * DM])
        r3 = ExitStack()
        cu = sb("cu", [P, 2, T], on=r3)
        delta = sb("delta", [P, 2, T], on=r3)
        du = sb("du", [P, 2, T], on=r3)
        sz = sb("sz", [P, NT, DM], on=r3)
        bcp = sb("bcp", [3 * NB, T], BF16, on=r3)
        cw = sb("cw", [P, 2, TAPS], on=r3)
        cb = sb("cb", [P, 2], on=r3)
        hcb = sb("hcb", [P, 2], on=r3)
        dtb = sb("dtb", [P, 2], on=r3)
        dsk = sb("dsk", [P, 2], on=r3)
        a_log = sb("a_log", [P, 2, DS], on=r3)
        a_exp = sb("a_exp", [P, 2, DS], on=r3)
        a_neg = sb("a_neg", [P, 2, DS], on=r3)
        dg = sb("dg", [P, 2, P], on=r3)
        hg = sb("hg", [P, 1], on=r3)
        r3a = ExitStack()
        ctx_nat = sb("ctx_nat", [P, NT, DC], on=r3a)
        wip = sb("wip", [P, 2, DC], on=r3a)
        wcv = sb("wcv", [P, 2, TAPS, DC], on=r3a)
        wcT = sb("wcT", [P, TAPS, 2, P], on=r3a)
        xpw = sb("xpw", [DR + NB, DI], on=r3a)
        dtw = sb("dtw", [P, 2, DR], on=r3a)
        wbcT = sb("wbcT", [P, 2, 3 * NB], on=r3a)
        wdtT = sb("wdtT", [P, 2, DR], on=r3a)
        dtpT = sb("dtpT", [DR, 2, P], on=r3a)
        dtl = sb("dtl", [DR, T], on=r3a)
        th = sb("th", [P, 2, CH], on=r3a)
        part = sb("part", [3 * NB, CH], on=r3a)
        part16 = sb("part16", [3 * NB, CH], BF16, on=r3a)
        sp2 = sb("sp2", [P, 2, CH], on=r3a)
        sp3 = sb("sp3", [P, 2, CH], on=r3a)
        r3a.close()
        r3b = ExitStack()
        b_sb = sb("b_sb", [P, 2, CH], on=r3b)
        decay = sb("decay", [P, 2, 2, 2, L], on=r3b)
        inflow = sb("inflow", [P, 2, 2, CH], on=r3b)
        state = sb("state", [P, 2, CH], on=r3b)
        prod = sb("prod", [P, 2, 2, CH], on=r3b)
        r3b.close()
        r3.close()
        r3 = ExitStack()
        attT = sb("attT", [P, B, 2, L], on=r3)
        xn = sb("xn", [P, NT, DM], on=r3)
        b1_bc = sb("b1_bc", [P, E0, H0], on=r3)
        logits = sb("logits", [P, NT, E0], on=r3)
        top = sb("top", [P, NT, 8], on=r3)
        topi = sb("topi", [P, NT, 8], U32, on=r3)
        topf = sb("topf", [P, NT, 8], on=r3)
        wexp = sb("wexp", [P, NT, K0], on=r3)
        wsum = sb("wsum", [P, NT], on=r3)
        wall = sb("wall", [P, NT], on=r3)
        wrec = sb("wrec", [P, NT], on=r3)
        wgt = sb("wgt", [P, NT, K0], on=r3)
        wgt_g = sb("wgt_g", [P, NT, K0], on=r3)
        chosen = sb("chosen", [P, NT, E0], BF16, on=r3)
        full = sb("full", [P, E0, NT], on=r3)
        ntiles = sb("ntiles", [P, E0], on=r3)
        tile_end = sb("tile_end", [P, E0], on=r3)
        row0 = sb("row0", [P, E0], on=r3)
        posf = sb("posf", [P, NT, E0], on=r3)
        rowf = sb("rowf", [P, NT, K0], on=r3)
        row_i = sb("row_i", [P, NT, K0], I32, on=r3)
        tile_i = sb("tile_i", [P, NT, K0], I32, on=r3)
        slot_i = sb("slot_i", [P, NT, K0], I32, on=r3)
        tile_f = sb("tile_f", [P, NT, K0], on=r3)
        slot_f = sb("slot_f", [P, NT, K0], on=r3)
        tok_of = sb("tok_of", [P, TILES0 + 1], I32, on=r3)
        ended = sb("ended", [P, E0], on=r3)
        owner = sb("owner", [P, 1], on=r3)
        owner_i = sb("owner_i", [1, P], I32, on=r3)
        r3d = ExitStack()
        att = sb("att", [P, 2, L], on=r3d)
        r3d.close()
        r3d = ExitStack()
        slot_hot = sb("slot_hot", [P, K0, P], F16, on=r3d)
        r3d.close()
        hold3 = sb("hold3", [P, 2 * L], on=r3)
        att_max = sb("att_max", [P, 2 * B], on=r3)
        att_neg = sb("att_neg", [P, 2 * B], on=r3)
        att_sum = sb("att_sum", [P, 2 * B], on=r3)
        att_rec = sb("att_rec", [P, 2 * B], on=r3)
        xnT = sb("xnT", [P, 2, T], on=r3)
        r3c = ExitStack()
        hot = sb("hot", [P, NT, K0, E0], on=r3c)
        r3e = ExitStack()
        qT = sb("qT", [P, T], on=r3e)
        kT = sb("kT", [P, T], on=r3e)
        r3e.close()
        r3e = ExitStack()
        shT = sb("shT", [HH + 1, NSH * 2, CH], on=r3e)
        r3e.close()
        hold4 = sb("hold4", [P, 2 * T], on=r3c)
        tile_tok = sb("tile_tok", [P, K0, TILES0], F16, on=r3c)
        r3c.close()
        xg = sb("xg", [P, U, DM], on=r3)
        xgT = sb("xgT", [P, 2, 2, P], on=r3)
        hid = sb("hid", [P, 2, DM], on=r3)
        gate_th = sb("gate_th", [P, 2, H1], on=r3)
        hidT = sb("hidT", [P, 2, 2, P], on=r3)
        yt = sb("yt", [P, U, DM], on=r3)
        r3.close()

        def flat(t, n, start=0):
            ap = t[:]
            if len(ap.shape) > 2:
                names = " ".join("abcde"[:len(ap.shape) - 1])
                ap = ap.rearrange(f"p {names} -> p ({names})")
            return ap[:, start:start + n]

        def cols(p):
            return slice(p * CH, (p + 1) * CH)

        s = MambaSemaphores(semaphore)
        lp = LoopSemaphores(semaphore)
        norm = NormSemaphores(semaphore)
        layers = []
        for i, (E, K, tiles, H) in enumerate(((E0, K0, TILES0, H0), (E1, K1, TILES1, H1))):
            layers.append(Layer(
                i=i, done=(0, TILES0)[i], slot_done=[(0, (TILES0 - 1 - u) // U + 1)[i] for u in range(U)], E=E, K=K, tiles=tiles, last=tiles + 1 - U, s=LayerSemaphores(semaphore, i),
                rows=(xn_rows0, xn_rows1)[i], y_rows=(y_rows0, y_rows1)[i],
                logits=flat(logits, NT * E).rearrange("p (j e) -> p j e", e=E),
                chosen=flat(chosen, NT * E), posf=flat(posf, NT * E).rearrange("p (j e) -> p j e", e=E),
                full=flat(full, E * NT).rearrange("p (e m) -> p e m", m=NT),
                hot=flat(hot, NT * K * E).rearrange("p (j k e) -> p j k e", k=K, e=E),
                wexp=flat(wexp, NT * K).rearrange("p (j k) -> p j k", k=K),
                wgt=flat(wgt, NT * K).rearrange("p (j k) -> p j k", k=K),
                wgt_g=flat(wgt_g, NT * K).rearrange("p (j k) -> p j k", k=K),
                rowf=flat(rowf, NT * K), row_i=flat(row_i, NT * K).rearrange("p (j k) -> p j k", k=K),
                tile_i=flat(tile_i, NT * K), slot_i=flat(slot_i, NT * K),
                tile_f=flat(tile_f, NT * K).rearrange("p (j k) -> p j k", k=K),
                slot_f=flat(slot_f, NT * K).rearrange("p (j k) -> p j k", k=K),
            ))
        a = AttentionSemaphores(semaphore)

        def first_tiles(t0, u, n):
            return isinstance(t0, int) and t0 + u < n

        def after(t0, u):
            return (t0 + U, 0) if u == U - 1 else (t0, u + 1)

        def turns(eng, ly, body):
            for u in range(U):
                body(0, u)
            with eng.Fori(U, ly.last, U) as t0:
                for u in range(U):
                    body(t0, u)
            for u in range(U - 1):
                body(ly.last, u)

        def expert(engine, ly, t0, u):
            return nc.values_load(owner_i[0:1, bass.ds(t0 + u, 1)], engines=(engine,), min_val=0, max_val=ly.E - 1,
                                  skip_runtime_bounds_check_because="VectorE clamped it to the experts")

        def slot_count(t0, n):
            return t0 * (16 // U) + 16 * n

        norm_order = [("moe0", j) for j in range(NT)]
        for j in range(NT + 1):
            if j < NT:
                norm_order.append(("attention", j))
            if j >= 1:
                norm_order.append(("moe1", j - 1))

        def norm_count(kind, j):
            return norm_order.index((kind, j)) + 1

        def moe_norm(ly, j):
            return norm_count(f"moe{ly.i}", j)

        CONV_BANK = (5, 6, 7, 0)
        Y_BANK = ((5, 6), (7, 0))
        LOGIT_BANK = (5, 0)
        BASE_BANK = ((1, 2, 5, 6), (3, 4, 5, 6))
        N_CONSTS = 19

        block = stack.enter_context(nc.Block())

        @block.sync
        def _(sp):
            sp.dma_start(ctx_nat[:], io["ctx_1024"].rearrange("b (s p) d -> p (b s) d", p=P)).then_inc(s.ctx_in, 16)
            for dst, src in (
                (wip[:], io["L0_xattn_in_proj_w"].rearrange("(h p) d -> p h d", p=P)),
                (cw[:], io["L0_xattn_conv_w"].rearrange("(h p) k -> p h k", p=P)),
                (cb[:], io["L0_xattn_conv_b"].rearrange("(h p) -> p h", p=P)),
                (xpw[:], io["L0_xattn_x_proj_w"]),
                (dtw[:], io["L0_xattn_dt_proj_w"].rearrange("(h p) r -> p h r", p=P)),
                (dtb[:], io["L0_xattn_dt_proj_b"].rearrange("(h p) -> p h", p=P)),
                (dsk[:], io["L0_xattn_D"].rearrange("(h p) -> p h", p=P)),
                (a_log[:], io["L0_xattn_A_log"].rearrange("(h p) n -> p h n", p=P)),
            ):
                sp.dma_start(dst, src, allow_slow_non_contiguous=True).then_inc(s.mamba_in, 16)
            sp.dma_start(xs[:], io["x"].rearrange("b (s p) d -> p (b s) d", p=P)).then_inc(s.x_in, 16)
            for i, name in enumerate(("g_xattn", "g_ffn")):
                sp.dma_start(gates_raw[:, 2 * i:2 * i + 2], io[name].partition_broadcast(P)).then_inc(s.gates_in, 16)
            quarter = E0 // 4
            for q in range(4):
                e = slice(q * quarter, (q + 1) * quarter)
                sp.dma_start(w1[:, e].rearrange("p e k h -> p (e k) h"),
                             io["L0_ffn_rw1"][e].rearrange("e (k p) h -> p (e k) h", p=P)).then_inc(s.w1_in, 16)
                sp.dma_start(w2[0:HH, e].rearrange("p e k d -> p (e k) d"),
                             io["L0_ffn_rw2"][e].rearrange("e (k p) d -> p (e k) d", p=HH)).then_inc(s.w2_in, 16)
            sp.dma_start(w2[HH:HH + 1, :, 1, :], io["L0_ffn_rb2"].unsqueeze(0)).then_inc(s.w2_in, 16)
            for dst, src in (
                (router0[:], io["L0_ffn_router_w"].rearrange("(k p) e -> p k e", p=P)),
                (rbias0[:], io["L0_ffn_router_b"].unsqueeze(0)),
                (sw1[:], io["L0_ffn_sw1"].rearrange("e (k p) h -> p (e k) h", p=P)),
                (sb1[:], io["L0_ffn_sb1"].rearrange("e (m p) -> p e m", p=HH)),
                (sw2[0:HH].rearrange("p e k d -> p (e k) d"), io["L0_ffn_sw2"].rearrange("e (k p) d -> p (e k) d", p=HH)),
                (sw2[HH:HH + 1, :, 1, :], io["L0_ffn_sb2"].unsqueeze(0)),
            ):
                sp.dma_start(dst, src, allow_slow_non_contiguous=True).then_inc(s.l0_in, 16)
            for dst, src in (
                (wq[:], io["L1_xattn_Wq"]), (wk[:], io["L1_xattn_Wk"]),
                (bqk[:, 0:1], io["L1_xattn_bq"].unsqueeze(1)), (bqk[:, 1:2], io["L1_xattn_bk"].unsqueeze(1)),
            ):
                sp.dma_start(dst, src, allow_slow_non_contiguous=True).then_inc(s.att_in, 16)
            for dst, src in (
                (wr_rows[:], io["L1_ffn_Wr"]), (rbias1[:], io["L1_ffn_bias"].unsqueeze(0)),
                (swg[:], io["L1_ffn_sWg"].rearrange("(k p) i -> p k i", p=P)),
                (swu[:], io["L1_ffn_sWu"].rearrange("(k p) i -> p k i", p=P)), (swd[:], io["L1_ffn_sWd"]),
            ):
                sp.dma_start(dst, src).then_inc(s.l1_in, 16)
            sp.wait_ge(s.x1_made, 4)
            sp.dma_start(b1_bc[:].rearrange("p e h -> p (e h)"),
                         io["L0_ffn_rb1"].rearrange("e h -> (e h)").partition_broadcast(P)).then_inc(s.b1_in, 16)
            for ly in layers:
                for j in range(NT):
                    sp.wait_ge(norm.normed, moe_norm(ly, j))
                    sp.dma_start(ly.rows[j * P:(j + 1) * P, :], xn[:, j, :]).then_inc(ly.s.xn_out, 16)

                def store(t0, u):
                    sp.wait_ge(lp.y_made, t0 + (ly.done + u + 1))
                    sp.dma_start(ly.y_rows[bass.ds(t0 * P + u * P, P), :], yt[:, u, :]).then_inc(lp.y_out[u], 16)

                turns(sp, ly, store)
                if ly.i == 0:
                    sp.wait_ge(lp.y_psum, ly.done + ly.tiles)
                    for k in range(2):
                        for g, name in enumerate(("L1_ffn_Wg", "L1_ffn_Wu")):
                            sp.dma_start(wgu[:, k:2 * E1:2, g, :], io[name].rearrange("e (k p) i -> k p e i", p=P)[k]
                                         ).then_inc(a.wgu_in, 16)
                    sp.dma_start(wd[:], io["L1_ffn_Wd"].rearrange("e i d -> i e d")).then_inc(a.wgu_in, 16)
            for j in range(NT):
                sp.wait_ge(layers[1].s.added, j + 1)
                sp.dma_start(out[j // 2, j % 2 * P:(j % 2 + 1) * P, :], xs[:, j, :]).then_inc(a.out_done, 16)
            sp.wait_ge(a.out_done, 16 * NT)

        @block.gpsimd
        def _(pool):
            def const(ins):
                ins.then_inc(s.consts, 1)
                made[0] += 1
                pool.wait_ge(s.consts, made[0])

            made = [0]
            const(pool.memset(ident[:], 0.0))
            const(pool.affine_select(out=ident[:], in_=ident[:], compare_op=ALU.not_equal, fill=1.0, base=0,
                                     pattern=[[-1, P]], channel_multiplier=1))
            const(pool.memset(ctxT[:, :, 0:TAPS - 1], 0.0))
            const(pool.memset(minus_half[:], -0.5))
            const(pool.memset(eps[:], EPS_LN))
            const(pool.memset(eye3[:], 0.0))
            for q in range(3):
                const(pool.affine_select(out=eye3[:], in_=eye3[:], compare_op=ALU.not_equal, fill=1.0, base=-NB * q,
                                         pattern=[[-1, NB]], channel_multiplier=1))
            const(pool.memset(ones16[:], 1.0))
            const(pool.affine_select(out=before[:], in_=ones16[:], compare_op=ALU.is_gt, fill=0.0, base=0,
                                     pattern=[[1, P]], channel_multiplier=-1))
            const(pool.memset(ones_row[:], 1.0))
            const(pool.iota(iota_i[:], pattern=[[1, P]], base=0, channel_multiplier=0))
            const(pool.tensor_copy(iota_f[:], iota_i[:]))
            const(pool.tensor_copy(iota_h[:], iota_i[:]))
            const(pool.iota(count_i[:], pattern=[[P, NT]], base=0, channel_multiplier=0))
            const(pool.tensor_copy(fill_f[:], count_i[:]))
            const(pool.iota(count_i[:], pattern=[[P, NT]], base=0, channel_multiplier=1))
            const(pool.tensor_copy(tokid[:], count_i[:]))
            assert made[0] == N_CONSTS

            pool.wait_ge(s.var_made, 1)
            pool.tensor_tensor(rstd[:], vareps[:], minus_half[:], ALU.pow).then_inc(s.rstd_made, 1)

            for q in range(4):
                p, h = q // 2, q % 2
                pool.wait_ge(s.w_made_1, q + 1)
                pool.tensor_tensor(sp2[:, q % 2], sp2[:, q % 2], th[:, q % 2], ALU.subtract).then_inc(s.low_made, 1)
                pool.wait_ge(s.delta_made, q + 1)
                pool.tensor_tensor(du[:, h, cols(p)], delta[:, h, cols(p)], cu[:, h, cols(p)],
                                   ALU.mult).then_inc(s.du_made, 1)

            def step(p, t, slot):
                for h in range(2):
                    if h == 0:
                        pool.wait_ge(s.b_copied, t + 1)
                    if not (isinstance(t, int) and t < 2):
                        pool.wait_ge(s.scanned, 2 * (t - 2) + h + 1)
                    pool.tensor_tensor(inflow[:, slot, h], du[:, h, cols(p)], b_sb[:, slot],
                                       ALU.mult).then_inc(s.inflow_made, 1)

            pool.wait_ge(s.region_free, 1)
            for p in range(2):
                for i in range(2):
                    step(p, p * DS + i, i)
                with pool.Fori(1, DS // 2) as m:
                    for i in range(2):
                        step(p, 2 * m + (p * DS + i), i)

            pool.wait_ge(s.x1_made, 4)
            pool.memset(shT[64:HH + 1], 1.0).then_inc(a.shT_ones, 1)

            for ly in layers:
                ls = ly.s
                pool.wait_ge(ls.xn_out, 16 * NT)
                pool.wait_ge(ls.tok_made, 1)

                for t in range(ly.tiles):
                    if t >= U:
                        pool.wait_ge(lp.xgT_psum, ly.done + t - (U - 1))
                    pool.indirect_dma_start(xg[:, t % U, :], None, ly.rows,
                                            bass.IndirectOffsetOnAxis(ap=tok_of[:, t:t + 1], axis=0)
                                            ).then_inc(lp.gathered[t % U], 16)
                for u in range(U):
                    pool.wait_ge(lp.y_out[u], 16 * (ly.slot_done[u] + (ly.tiles - 1 - u) // U + 1))
                for j in range(NT):
                    b = j % 4
                    if j >= 4:
                        pool.wait_ge(ls.added, j - 3)
                    for k in range(ly.K):
                        pool.indirect_dma_start(got[:, b, k, :], None, ly.y_rows,
                                                bass.IndirectOffsetOnAxis(ap=ly.row_i[:, j, k:k + 1], axis=0)
                                                ).then_inc(ls.got_in[b], 16)

        @block.scalar
        def _(act):
            act.wait_ge(s.gates_in, 32)
            act.activation(gates[:], gates_raw[:], ACT.Tanh).then_inc(s.gates_made, 1)
            act.wait_ge(s.mamba_in, 128)
            act.activation(a_exp[:], a_log[:], ACT.Exp).then_inc(s.a_made, 1)
            act.wait_ge(s.a_made, 1)
            act.mul(a_neg[:], a_exp[:], -1.0).then_inc(s.a_made, 1)
            act.wait_ge(s.consts, 3)
            for i in range(2):
                act.wait_ge(s.ctxT_psum, i + 1)
                act.copy(ctxT[:, 2 * i:2 * i + 2, TAPS - 1:],
                         bank[:, i].rearrange("p (b l) -> p b l", b=2)).then_inc(s.ctxT_made, 1)

            act.wait_ge(s.hcb_made, 1)
            for p in range(2):
                for h in range(2):
                    q = 2 * p + h
                    act.wait_ge(s.conv_psum, q + 1)
                    if q >= 2:
                        act.wait_ge(s.u_made, q - 1)
                    act.activation(th[:, h], bank[:, CONV_BANK[q]], ACT.Tanh, bias=hcb[:, h:h + 1],
                                   scale=0.5).then_inc(s.th_made, 1)
                act.wait_ge(s.bc_psum, p + 1)
                if p >= 1:
                    act.wait_ge(s.parts_made, 4 * p)
                act.copy(part16[:], bank[0:3 * NB, 1 + p]).then_inc(s.hi_made, 1)
                act.copy(bcp[0:NB, cols(p)], bank[0:NB, 1 + p]).then_inc(s.hi_made, 1)
                act.wait_ge(s.dt_psum, p + 1)
                act.copy(dtl[:, cols(p)], bank[0:DR, 3 + p]).then_inc(s.dtl_made, 1)
            for i in range(4):
                act.wait_ge(s.z_normed, 2 * i + 2)
                if i >= 2:
                    act.wait_ge(s.z_made, i - 1)
                act.activation(sp3[:, i % 2], flat(sz, CH, i * CH), ACT.Tanh, scale=0.5).then_inc(s.z_th, 1)
            for q in range(4):
                h = q % 2
                act.wait_ge(s.dpre_psum, q + 1)
                if q >= 2:
                    act.wait_ge(s.delta_made, q - 1)
                else:
                    act.wait_ge(s.u_made, 4)
                    act.wait_ge(s.z_made, 4)
                act.activation(th[:, h], bank[:, CONV_BANK[q]], ACT.Abs, bias=dtb[:, h:h + 1]).then_inc(s.abs_made, 1)
                act.wait_ge(s.abs_made, q + 1)
                act.activation(sp2[:, h], th[:, h], ACT.Exp, scale=-1.0).then_inc(s.exp_made, 1)
                act.wait_ge(s.exp_made, q + 1)
                act.activation(sp3[:, h], sp2[:, h], ACT.Ln, bias=1.0).then_inc(s.ln_made, 1)

            a_of = a_neg[:].rearrange("p h (m i) -> p h m i", i=2)

            def step(p, t, m, slot):
                act.wait_ge(s.b_bcast, t + 1)
                first = isinstance(t, int) and t < 2
                if not first:
                    act.wait_ge(s.inflow_made, 2 * (t - 1))
                act.copy(b_sb[:, slot], bank[:, 1 + slot]).then_inc(s.b_copied, 1)
                for h in range(2):
                    if not first:
                        act.wait_ge(s.scanned, 2 * (t - 2) + h + 1)
                    act.activation(decay[:, slot, h, :, 1:],
                                   delta[:, h, cols(p)].rearrange("p (b l) -> p b l", b=2)[:, :, 1:],
                                   ACT.Exp, scale=a_of[:, h, bass.ds(m, 1), slot]).then_inc(s.decay_made, 1)

            act.wait_ge(s.region_free, 1)
            act.wait_ge(s.a_made, 2)
            for p in range(2):
                for i in range(2):
                    step(p, p * DS + i, 0, i)
                with act.Fori(1, DS // 2) as m:
                    for i in range(2):
                        step(p, 2 * m + (p * DS + i), m, i)

            def deviation(n):
                j = norm_order[n - 1][1]
                act.wait_ge(norm.var_found, n)
                act.activation(std[:, j:j + 1], meanvar[:, j, 1:2], ACT.Sqrt, bias=eps[:]).then_inc(norm.std_found, 1)

            def turned(n):
                j = norm_order[n - 1][1]
                act.wait_ge(norm.turned_psum, n)
                act.copy(xnT[:, :, j * P:(j + 1) * P],
                         bank[:, 1 + n % 2, 0:DM].rearrange("p (k t) -> p k t", k=2)).then_inc(norm.turned, 1)

            def shared_hidden(c):
                ls = layers[0].s
                if c:
                    act.wait_ge(ls.base_psum, 4)
                for em in range(NSH * 2):
                    n = c * NSH * 2 + em
                    act.wait_ge(ls.sh_psum, n + 1)
                    act.activation(shT[0:HH, em], bank[0:HH, 3 + n % 2], ACT.Relu,
                                   bias=sb1[:, em // 2, em % 2:em % 2 + 1]).then_inc(ls.sh_made, 1)

            for ly in layers:
                ls = ly.s
                if ly.i == 1:
                    for c in range(4):
                        act.wait_ge(a.qk_psum, c + 1)
                        if c == 2:
                            for u in range(U):
                                act.wait_ge(lp.y_out[u], 16 * layers[1].slot_done[u])
                        act.activation((qT, kT)[c // 2][:, cols(c % 2)], bank[:, (5, 6, 7, 0)[c]], ACT.Identity,
                                       bias=bqk[:, c // 2:c // 2 + 1]).then_inc(a.qk_made, 1)
                    for n in range(2 * B + 1):
                        if n < 2 * B:
                            act.wait_ge(a.neg_made, n + 1)
                            if n >= 2:
                                act.wait_ge(a.attT_psum, n - 1)
                            act.activation(att[:, n % 2], bank[:, 5 + n % 2, 0:L], ACT.Exp, bias=att_neg[:, n:n + 1],
                                           accum_out=att_sum[:, n:n + 1]).then_inc(a.aexp_made, 1)
                        if n >= 1:
                            i = n - 1
                            act.wait_ge(a.attT_psum, i + 1)
                            act.copy(attT[:, i // 2, :, (i % 2) * P:(i % 2 + 1) * P],
                                     bank[:, (7, 0)[i % 2], 0:2 * P].rearrange("p (k r) -> p k r", k=2)
                                     ).then_inc(a.attT_made, 1)
                    for n in range(NT + 1, 3 * NT + 1):
                        deviation(n)
                        turned(n)
                else:
                    deviation(1)
                    for n in range(1, NT + 1):
                        if n < NT:
                            deviation(n + 1)
                        turned(n)
                    act.wait_ge(a.shT_ones, 1)
                    shared_hidden(0)
                act.wait_ge(ls.shifted, 1)
                act.activation(ly.wexp, ly.wexp, ACT.Exp).then_inc(ls.exped, 1)
                if ly.i == 0:
                    shared_hidden(1)
                if ly.i == 1:
                    act.activation(ly.posf, ly.posf, ACT.Exp).then_inc(ls.exped, 1)
                    for c in range(2):
                        act.wait_ge(ls.sh_psum, 2 * c + 1)
                        if c:
                            act.wait_ge(ls.sh_made, c)
                        act.activation(gg[:], bank[:, 1], ACT.Tanh, scale=0.5).then_inc(a.sh_gate, 1)

                def transpose_out(t0, u):
                    act.wait_ge(lp.xgT_psum, t0 + (ly.done + u + 1))
                    if not first_tiles(t0, u, 2):
                        act.wait_ge(lp.h_psum, t0 + (ly.done + u - 1))
                    act.copy(flat(xgT, 2 * P, (u % 2) * 2 * P), bank[:, u % 2, 0:2 * P]).then_inc(lp.xgT_made, 1)

                def tile(t0, u):
                    if ly.i == 1:
                        act.wait_ge(lp.h_psum, t0 + (ly.done + u + 1))
                        if not first_tiles(t0, u, 2):
                            act.wait_ge(lp.hid_made, t0 + (ly.done + u - 1))
                        act.activation(gate_th[:, u % 2], bank[:, 2 + u % 2, 0:H1], ACT.Tanh,
                                       scale=0.5).then_inc(lp.gate_made, 1)
                    if not (isinstance(t0, int) and t0 + u == ly.tiles - 1):
                        transpose_out(*after(t0, u))
                    act.wait_ge(lp.hidT_psum, t0 + (ly.done + u + 1))
                    if not first_tiles(t0, u, 2):
                        act.wait_ge(lp.y_psum, t0 + (ly.done + u - 1))
                    if ly.i == 0:
                        act.activation(hidT[0:HH, u % 2].rearrange("p k r -> p (k r)"), bank[0:HH, 4 + u % 2, 0:2 * P],
                                       ACT.Relu).then_inc(lp.hidT_made, 1)
                    else:
                        act.copy(hidT[:, u % 2, 0], bank[:, 4 + u % 2, 0:P]).then_inc(lp.hidT_made, 1)

                if ly.i == 0:
                    act.wait_ge(a.hidT_ones, 1)
                transpose_out(0, 0)
                turns(act, ly, tile)

        @block.tensor
        def _(pe):
            pe.wait_ge(s.consts, 2)
            pe.wait_ge(s.ctx_in, 16)
            for j in range(NT):
                mm = pe.transpose(bank[:, j // 4, (j % 4) * P:(j % 4 + 1) * P], ctx_nat[:, j, :], ident[:])
                if j % 4 == 3:
                    mm.then_inc(s.ctxT_psum, 1)
            pe.wait_ge(s.wcv_made, 2 * TAPS)
            for k in range(TAPS):
                for h in range(2):
                    c = (k % 2) * 2 + h
                    mm = pe.transpose(bank[:, 2 + k // 2, c * P:(c + 1) * P], wcv[:, h, k, :], ident[:])
                if k % 2 == 1:
                    mm.then_inc(s.wcT_psum, 1)
            pe.wait_ge(s.mamba_in, 128)
            for h in range(2):
                pe.transpose(bank[:, 4, h * (DR + NB):(h + 1) * (DR + NB)], xpw[:, h * P:(h + 1) * P],
                             ident[0:DR + NB, 0:DR + NB])
                mm = pe.transpose(bank[0:DR, 4, (1 + h) * P:(2 + h) * P], dtw[:, h, :], ident[:])
            mm.then_inc(s.xw_psum, 1)
            pe.wait_ge(s.wcT_made, 2)
            pe.wait_ge(s.ctxT_made, 2)
            for q in range(4):
                p, h = q // 2, q % 2
                for k in range(TAPS):
                    mm = pe.matmul(bank[:, CONV_BANK[q]], wcT[:, k, h, :], ctxT[:, 2 * p:2 * p + 2, k:k + L],
                                   start=k == 0, stop=k == TAPS - 1)
                mm.then_inc(s.conv_psum, 1)
            pe.wait_ge(s.xw_made, 5)
            for p in range(2):
                pe.wait_ge(s.u_made, 2 * p + 2)
                for h in range(2):
                    mm = pe.matmul(bank[0:3 * NB, 1 + p], wbcT[:, h, :], cu[:, h, cols(p)], start=h == 0, stop=h == 1)
                mm.then_inc(s.bc_psum, 1)
                for h in range(2):
                    mm = pe.matmul(bank[0:DR, 3 + p], wdtT[:, h, :], cu[:, h, cols(p)], start=h == 0, stop=h == 1)
                mm.then_inc(s.dt_psum, 1)
                pe.wait_ge(s.dtl_made, p + 1)
                for h in range(2):
                    pe.matmul(bank[:, CONV_BANK[2 * p + h]], dtpT[:, h, :], dtl[:, cols(p)],
                              start=True, stop=True).then_inc(s.dpre_psum, 1)

            pick = eye3[:].rearrange("k (m i) -> k m i", i=2)

            def broadcast_b(p, t, m, slot):
                if not (isinstance(t, int) and t < 2):
                    pe.wait_ge(s.b_copied, t - 1)
                pe.matmul(bank[:, 1 + slot], pick[:, bass.ds(m, 1), slot].to_broadcast([3 * NB, P]), bcp[:, cols(p)],
                          start=True, stop=True).then_inc(s.b_bcast, 1)

            def broadcast_c(p, t, m, slot):
                if not (isinstance(t, int) and t < 2):
                    pe.wait_ge(s.prod_made, 2 * (t - 1))
                pe.matmul(bank[:, 3 + slot], pick[:, bass.ds(m + DS // 2, 1), slot].to_broadcast([3 * NB, P]), bcp[:, cols(p)],
                          start=True, stop=True).then_inc(s.c_bcast, 1)

            def ysum(p, t, slot, stop=False):
                for h in range(2):
                    pe.wait_ge(s.prod_made, 2 * t + h + 1)
                    pe.matmul(bank[:, Y_BANK[p][h]], ident[:], prod[:, slot, h], start=False,
                              stop=stop).then_inc(s.y_summed, 1)

            pe.wait_ge(s.region_free, 1)
            pe.wait_ge(s.dg_made, 2)
            for p in range(2):
                t0 = p * DS
                for h in range(2):
                    pe.matmul(bank[:, Y_BANK[p][h]], dg[:, h, :], cu[:, h, cols(p)], start=True, stop=False)
                broadcast_b(p, t0, 0, 0)
                broadcast_b(p, t0 + 1, 0, 1)
                broadcast_c(p, t0, 0, 0)

                def two_steps(m):
                    for i in range(2):
                        broadcast_b(p, 2 * m + (t0 + 2 + i), m + 1, i)
                        broadcast_c(p, 2 * m + (t0 + 1 + i), m + i, 1 - i)
                        ysum(p, 2 * m + (t0 + i), i)

                two_steps(0)
                with pe.Fori(1, DS // 2 - 1) as m:
                    two_steps(m)
                broadcast_c(p, t0 + DS - 1, DS // 2 - 1, 1)
                ysum(p, t0 + DS - 2, 0)
                ysum(p, t0 + DS - 1, 1, stop=True)
                pe.wait_ge(s.gated, 2 * p + 2)
                for b in range(2):
                    for lt in range(2):
                        for h in range(2):
                            mm = pe.transpose(bank[:, Y_BANK[p][b], lt * DM + h * P:lt * DM + (h + 1) * P],
                                              sz[:, 4 * p + 2 * b + h, lt * P:(lt + 1) * P], ident[:])
                    mm.then_inc(s.mix_psum, 1)

            def turn(n):
                j = norm_order[n - 1][1]
                pe.wait_ge(norm.normed, n)
                if n > 2:
                    pe.wait_ge(norm.turned, n - 2)
                for k in range(2):
                    mm = pe.transpose(bank[:, 1 + n % 2, k * P:(k + 1) * P], xn[:, j, k * P:(k + 1) * P], ident[:])
                mm.then_inc(norm.turned_psum, 1)

            def router_logits(ly, j):
                router, rbias = ((router0, rbias0), (router1, rbias1))[ly.i]
                pe.wait_ge(norm.turned, moe_norm(ly, j))
                dst = bank[:, LOGIT_BANK[ly.i], j * ly.E:(j + 1) * ly.E]
                pe.matmul(dst, ones_row[:], rbias[:], start=True, stop=False)
                for k in range(2):
                    mm = pe.matmul(dst, xnT[:, k, j * P:(j + 1) * P], router[:, k, :], start=False, stop=k == 1)
                if j == NT - 1:
                    mm.then_inc(ly.s.logits_psum, 1)

            def attend(j):
                pe.wait_ge(norm.turned, norm_count("attention", j))
                if j >= 2:
                    pe.wait_ge(a.x3_made, j - 1)
                for k in range(2):
                    mm = pe.matmul(bank[:, 5 + j % 2, 0:L], xnT[:, k, j * P:(j + 1) * P], attT[:, j // 2, k, :],
                                   start=k == 0, stop=k == 1)
                mm.then_inc(a.att_psum, 1)

            def shared_hidden(n):
                ls = layers[0].s
                em, c = n % 4, n // 4
                if n >= 2:
                    pe.wait_ge(ls.sh_made, n - 1)
                for k in range(2):
                    mm = pe.matmul(bank[0:HH, 3 + n % 2], sw1[:, em // 2 * 2 + k, em % 2 * HH:(em % 2 + 1) * HH],
                                   xnT[:, k, cols(c)], start=k == 0, stop=k == 1)
                mm.then_inc(ls.sh_psum, 1)

            def shared_out(ly, j):
                dst = bank[:, BASE_BANK[ly.i][j // 2], j % 2 * DM:(j % 2 + 1) * DM]
                if ly.i == 0:
                    pe.wait_ge(ly.s.sh_made, NSH * 2 * (j // 4 + 1))
                    tok = slice(j % 4 * P, (j % 4 + 1) * P)
                    for em in range(NSH * 2):
                        K = HH + em % 2
                        mm = pe.matmul(dst, shT[0:K, em, tok], sw2[0:K, em // 2, em % 2, :],
                                       start=em == 0, stop=em == NSH * 2 - 1)
                else:
                    mm = pe.matmul(dst, shT1[:, j * P:(j + 1) * P], swd[:], start=True, stop=True)
                mm.then_inc(ly.s.base_psum, 1)

            for ly in layers:
                ls = ly.s
                if ly.i == 0:
                    pe.wait_ge(s.l0_in, 96)
                    turn(1)
                    for j in range(NT):
                        if j < NT - 1:
                            turn(j + 2)
                        router_logits(ly, j)
                    for n in range(4):
                        shared_hidden(n)
                else:
                    pe.wait_ge(s.att_in, 64)
                    pe.wait_ge(s.l1_in, 80)
                    pe.wait_ge(lp.y_made, layers[0].tiles)
                    for c, w in enumerate((wq, wk)):
                        pe.transpose(bank[:, 5, c * P:(c + 1) * P], w[:], ident[:])
                    for k in range(2):
                        mm = pe.transpose(bank[:, 5, 2 * P + k * E1:2 * P + (k + 1) * E1], wr_rows[:, k * P:(k + 1) * P],
                                          ident[0:E1, 0:E1])
                    mm.then_inc(a.wqkT_psum, 1)
                    pe.wait_ge(a.wqkT_made, 2)
                    for c in range(4):
                        p = c % 2
                        pe.matmul(bank[:, (5, 6, 7, 0)[c]], wqkT[:, c // 2, :], ctxT[:, 2 * p:2 * p + 2, TAPS - 1:],
                                  start=True, stop=True).then_inc(a.qk_psum, 1)
                    pe.wait_ge(a.qk_made, 4)
                    for n in range(2 * B + 1):
                        if n < 2 * B:
                            b = n // 2
                            if n >= 2:
                                pe.wait_ge(a.aexp_made, n - 1)
                            pe.matmul(bank[:, 5 + n % 2, 0:L], qT[:, n * P:(n + 1) * P], kT[:, b * L:(b + 1) * L],
                                      start=True, stop=True).then_inc(a.e_psum, 1)
                        if n >= 1:
                            i = n - 1
                            pe.wait_ge(a.att_made, i + 1)
                            if i >= 2:
                                pe.wait_ge(a.attT_made, i - 1)
                            for k in range(2):
                                mm = pe.transpose(bank[:, (7, 0)[i % 2], k * P:(k + 1) * P],
                                                  att[:, i % 2, k * P:(k + 1) * P], ident[:])
                            mm.then_inc(a.attT_psum, 1)
                    pe.wait_ge(a.attT_made, 2 * B)
                    for n in range(NT + 1, 3 * NT + 1):
                        kind, j = norm_order[n - 1]
                        turn(n)
                        if kind == "attention":
                            attend(j)
                        else:
                            router_logits(ly, j)
                pe.wait_ge(ls.chosen_made, 1)
                W = NT * ly.E
                pe.matmul(bank[:, 6, 0:W], before[:], ly.chosen, start=True, stop=False)
                for d in range(1, NT):
                    mm = pe.matmul(bank[:, 6, d * ly.E:W], ones16[:], ly.chosen[:, 0:W - d * ly.E],
                                   start=False, stop=d == NT - 1)
                mm.then_inc(ls.rank_psum, 1)
                for j in range(NT):
                    mm = pe.matmul(bank[:, 7, 0:ly.E], ones16[:], ly.chosen[:, j * ly.E:(j + 1) * ly.E],
                                   start=j == 0, stop=j == NT - 1)
                mm.then_inc(ls.rank_psum, 1)
                if ly.i == 1:
                    for c in range(2):
                        if c:
                            pe.wait_ge(ls.sh_made, c)
                        for g, w in enumerate((swg, swu)):
                            for k in range(2):
                                mm = pe.matmul(bank[:, 1 + g], w[:, k, :], xnT[:, k, cols(c)], start=k == 0, stop=k == 1)
                            mm.then_inc(ls.sh_psum, 1)
                    pe.wait_ge(ls.sh_made, 2)
                if ly.i == 0:
                    for j in range(4):
                        shared_out(ly, j)
                for j in range(NT):
                    if ly.i == 0 and j in (1, 2):
                        for n in range(2 * j + 2, 2 * j + 4):
                            shared_hidden(n)
                    if ly.i == 0 and j >= 4:
                        shared_out(ly, j)
                    if ly.i == 1:
                        shared_out(ly, j)
                    for k in range(ly.K):
                        n = j * ly.K + k
                        pe.wait_ge(ls.hot_made, 2 * n + 2)
                        pe.matmul(bank[:, 0, 0:ly.tiles], slot_hot[:, k, :], tile_tok[:, k, 0:ly.tiles],
                                  start=n == 0, stop=n == NT * ly.K - 1).then_inc(ls.map_used, 1)
                pe.wait_ge(ls.owner_made, 1)
                pe.transpose(bank[0:1, 7, 0:P], owner[:], ident[:]).then_inc(ls.owner_psum, 1)

                def rows_in(t0, u):
                    pe.wait_ge(lp.gathered[u], slot_count(t0, ly.slot_done[u] + 1))
                    if not first_tiles(t0, u, 2):
                        pe.wait_ge(lp.xgT_made, t0 + (ly.done + u - 1))
                    for k in range(2):
                        mm = pe.transpose(bank[:, u % 2, k * P:(k + 1) * P], xg[:, u, k * P:(k + 1) * P], ident[:])
                    mm.then_inc(lp.xgT_psum, 1)

                PE = mybir.EngineType.PE
                owners = [None] * U

                def down(t0, u):
                    e = owners[u]
                    pe.wait_ge(lp.hidT_made, t0 + (ly.done + u + 1))
                    if not first_tiles(t0, u, 2):
                        pe.wait_ge(lp.y_made, t0 + (ly.done + u - 1))
                    dst = bank[:, 6 + u % 2, 0:DM]
                    if ly.i == 0:
                        pe.matmul(dst, hidT[0:HH, u % 2, 0], w2[0:HH, bass.ds(e, 1), 0, :], start=True, stop=False)
                        mm = pe.matmul(dst, hidT[0:HH + 1, u % 2, 1], w2[0:HH + 1, bass.ds(e, 1), 1, :],
                                       start=False, stop=True)
                    else:
                        mm = pe.matmul(dst, hidT[:, u % 2, 0], wd[:, bass.ds(e, 1), :], start=True, stop=True)
                    mm.then_inc(lp.y_psum, 1)

                def tile(t0, u):
                    if u == 0:
                        owners[0] = expert(PE, ly, t0, 0)
                        if not first_tiles(t0, 0, 1):
                            owners[U - 1] = expert(PE, ly, t0 - U, U - 1)
                    e = owners[u]
                    pe.wait_ge(lp.xgT_made, t0 + (ly.done + u + 1))
                    if not first_tiles(t0, u, 2):
                        pe.wait_ge(lp.hid_made, t0 + (ly.done + u - 1))
                    for k in range(2):
                        if ly.i == 0:
                            mm = pe.matmul(bank[:, 2 + u % 2, 0:H0], xgT[:, u % 2, k], w1[:, bass.ds(e, 1), k, :],
                                           start=k == 0, stop=k == 1)
                        else:
                            w = wgu[:].rearrange("p (e k) g i -> p e k (g i)", k=2)
                            mm = pe.matmul(bank[:, 2 + u % 2, 0:2 * H1], xgT[:, u % 2, k], w[:, bass.ds(e, 1), k, :],
                                           start=k == 0, stop=k == 1)
                    mm.then_inc(lp.h_psum, 1)
                    is_last = isinstance(t0, int) and t0 + u == ly.tiles - 1
                    if not is_last:
                        rows_in(*after(t0, u))
                    if not first_tiles(t0, u, 1):
                        down(t0 if u else t0 - U, (u - 1) % U)
                    if u < U - 1 and not is_last:
                        owners[u + 1] = expert(PE, ly, t0, u + 1)
                    pe.wait_ge(lp.hid_made, t0 + (ly.done + u + 1))
                    if not first_tiles(t0, u, 2):
                        pe.wait_ge(lp.hidT_made, t0 + (ly.done + u - 1))
                    if ly.i == 0:
                        for k in range(2):
                            mm = pe.transpose(bank[0:HH, 4 + u % 2, k * P:(k + 1) * P],
                                              hid[:, u % 2, k * HH:(k + 1) * HH], ident[:])
                    else:
                        mm = pe.transpose(bank[:, 4 + u % 2, 0:P], hid[:, u % 2, 0:H1], ident[:])
                    mm.then_inc(lp.hidT_psum, 1)

                pe.wait_ge(ls.tok_made, 1)
                pe.wait_ge(ls.owner_ready, 1)
                if ly.i == 0:
                    pe.wait_ge(s.w1_in, 64)
                    pe.wait_ge(s.w2_in, 80)
                else:
                    pe.wait_ge(a.wgu_in, 80)
                rows_in(0, 0)
                pe.wait_ge(ls.based, NT)
                turns(pe, ly, tile)
                down(ly.last, U - 2)

        @block.vector
        def _(dve):
            def link(ins):
                ins.then_inc(s.dve_step, 1)
                steps[0] += 1
                dve.wait_ge(s.dve_step, steps[0])

            steps = [0]
            dve.wait_ge(s.mamba_in, 128)
            for h in range(2):
                for k in range(TAPS):
                    dve.tensor_scalar(wcv[:, h, k, :], wip[:, h, :], cw[:, h, k:k + 1], None,
                                      ALU.mult).then_inc(s.wcv_made, 1)
            dve.tensor_scalar(hcb[:], cb[:], 0.5, None, ALU.mult).then_inc(s.hcb_made, 1)
            dve.wait_ge(s.consts, 2)
            for h in range(2):
                dve.tensor_scalar(dg[:, h, :], ident[:], dsk[:, h:h + 1], None, ALU.mult).then_inc(s.dg_made, 1)

            dve.wait_ge(s.x_in, 16)
            for j in range(NT):
                ins = dve.bn_stats(stats[:, j, :], xs[:, j, :])
            link(ins)
            for j in range(NT):
                ins = dve.bn_aggr(meanvar[:, j, :], stats[:, j, :])
            link(ins)
            dve.tensor_scalar(vareps[:], meanvar[:, :, 1], EPS_LN, None, ALU.add).then_inc(s.var_made, 1)

            for i in range(2):
                dve.wait_ge(s.wcT_psum, i + 1)
                dve.tensor_copy(flat(wcT, CH, i * CH), bank[:, 2 + i]).then_inc(s.wcT_made, 1)
            dve.wait_ge(s.xw_psum, 1)
            xw = bank[:, 4, 0:2 * (DR + NB)].rearrange("p (h c) -> p h c", h=2)
            for r in range(3):
                dve.tensor_copy(wbcT[:, :, r * NB:(r + 1) * NB], xw[:, :, DR:]).then_inc(s.xw_made, 1)
            dve.tensor_copy(wdtT[:], xw[:, :, 0:DR]).then_inc(s.xw_made, 1)
            dve.tensor_copy(dtpT[:], bank[0:DR, 4, P:3 * P].rearrange("p (h c) -> p h c", h=2)).then_inc(s.xw_made, 1)

            dve.wait_ge(s.rstd_made, 1)
            for j in range(NT):
                dve.tensor_scalar(sz[:, j, :], xs[:, j, :], meanvar[:, j, 0:1], rstd[:, j:j + 1],
                                  ALU.subtract, ALU.mult).then_inc(s.z_normed, 1)

            dve.wait_ge(s.hcb_made, 1)
            for p in range(2):
                for h in range(2):
                    q = 2 * p + h
                    dve.wait_ge(s.th_made, q + 1)
                    link(dve.tensor_scalar(cu[:, h, cols(p)], bank[:, CONV_BANK[q]], 0.5, hcb[:, h:h + 1],
                                           ALU.mult, ALU.add))
                    dve.scalar_tensor_tensor(cu[:, h, cols(p)], th[:, h], 1.0, cu[:, h, cols(p)],
                                             ALU.add, ALU.mult).then_inc(s.u_made, 1)
            for p in range(2):
                dve.wait_ge(s.hi_made, 2 * p + 2)
                ps = bank[:, 1 + p]
                dve.tensor_tensor(bcp[NB:2 * NB, cols(p)], ps[NB:2 * NB], part16[NB:2 * NB],
                                  ALU.subtract).then_inc(s.parts_made, 1)
                dve.tensor_tensor(part[2 * NB:3 * NB], ps[2 * NB:3 * NB], part16[2 * NB:3 * NB],
                                  ALU.subtract).then_inc(s.parts_made, 1)
                dve.wait_ge(s.parts_made, 4 * p + 2)
                dve.tensor_copy(part16[2 * NB:3 * NB], part[2 * NB:3 * NB]).then_inc(s.parts_made, 1)
                dve.wait_ge(s.parts_made, 4 * p + 3)
                dve.tensor_tensor(bcp[2 * NB:3 * NB, cols(p)], part[2 * NB:3 * NB], part16[2 * NB:3 * NB],
                                  ALU.subtract).then_inc(s.parts_made, 1)
            for i in range(4):
                dve.wait_ge(s.z_th, i + 1)
                dve.scalar_tensor_tensor(flat(sz, CH, i * CH), sp3[:, i % 2], 1.0, flat(sz, CH, i * CH),
                                         ALU.add, ALU.mult).then_inc(s.z_made, 1)
            for q in range(4):
                p, h = q // 2, q % 2
                dve.wait_ge(s.abs_made, q + 1)
                link(dve.tensor_scalar(delta[:, h, cols(p)], bank[:, CONV_BANK[q]], dtb[:, h:h + 1], 0.0,
                                       ALU.add, ALU.max))
                dve.wait_ge(s.exp_made, q + 1)
                dve.wait_ge(s.ln_made, q + 1)
                dve.tensor_scalar(th[:, h], sp2[:, h], 1.0, -1.0, ALU.add, ALU.add).then_inc(s.w_made_1, 1)
                link(dve.tensor_tensor(delta[:, h, cols(p)], delta[:, h, cols(p)], sp3[:, h], ALU.add))
                dve.wait_ge(s.low_made, q + 1)
                dve.tensor_tensor(delta[:, h, cols(p)], delta[:, h, cols(p)], sp2[:, h],
                                  ALU.add).then_inc(s.delta_made, 1)
            dve.wait_ge(s.du_made, 4)
            dve.memset(decay[:, :, :, :, 0:1].rearrange("p a b c o -> p (a b c) o"), 0.0).then_inc(s.region_free, 1)

            def step(p, t, slot):
                for h in range(2):
                    dve.wait_ge(s.decay_made, 2 * t + h + 1)
                    dve.wait_ge(s.inflow_made, 2 * t + h + 1)
                    if not (isinstance(t, int) and t < 1):
                        dve.wait_ge(s.prod_made, 2 * (t - 1) + h + 1)
                    dve.tensor_tensor_scan(state[:, h], decay[:, slot, h].rearrange("p b l -> p (b l)"),
                                           inflow[:, slot, h], 0.0, ALU.mult, ALU.add).then_inc(s.scanned, 1)
                for h in range(2):
                    if h == 0:
                        dve.wait_ge(s.c_bcast, t + 1)
                    dve.wait_ge(s.scanned, 2 * t + h + 1)
                    if not (isinstance(t, int) and t < 2):
                        dve.wait_ge(s.y_summed, 2 * (t - 2) + h + 1)
                    dve.tensor_tensor(prod[:, slot, h], state[:, h], bank[:, 3 + slot],
                                      ALU.mult).then_inc(s.prod_made, 1)

            dve.wait_ge(s.region_free, 1)
            dve.wait_ge(s.gates_made, 1)
            link(dve.tensor_scalar(hg[:], gates[:, 0:1], 0.5, None, ALU.mult))

            def normalise(kind, j):
                link(dve.bn_stats(stats[:, j, :], xs[:, j, :]))
                dve.bn_aggr(meanvar[:, j, :], stats[:, j, :]).then_inc(norm.var_found, 1)
                dve.wait_ge(norm.std_found, norm_count(kind, j))
                link(dve.reciprocal(rstd[:, j:j + 1], std[:, j:j + 1]))
                dve.tensor_scalar(xn[:, j, :], xs[:, j, :], meanvar[:, j, 0:1], rstd[:, j:j + 1],
                                  ALU.subtract, ALU.mult).then_inc(norm.normed, 1)

            for p in range(2):
                t0 = p * DS
                for i in range(2):
                    step(p, t0 + i, i)
                with dve.Fori(1, DS // 2) as m:
                    for i in range(2):
                        step(p, 2 * m + (t0 + i), i)
                if p == 1:
                    normalise("moe0", 0)
                dve.wait_ge(s.y_summed, 2 * (t0 + DS))
                dve.wait_ge(s.z_made, 4)
                for h in range(2):
                    z = sz[:, 4 * p + h:4 * p + 4:2, :]
                    dve.tensor_tensor(z, z, bank[:, Y_BANK[p][h]].rearrange("p (b l) -> p b l", b=2),
                                      ALU.mult).then_inc(s.gated, 1)
                if p == 1:
                    for j in range(1, 4):
                        normalise("moe0", j)
                for b in range(2):
                    j = 4 * p + 2 * b
                    dve.wait_ge(s.mix_psum, 2 * p + b + 1)
                    dve.scalar_tensor_tensor(flat(xs, CH, j * DM), bank[:, Y_BANK[p][b]], hg[:, 0:1],
                                             flat(xs, CH, j * DM), ALU.mult, ALU.add).then_inc(s.x1_made, 1)
                    if p == 1:
                        dve.wait_ge(s.x1_made, 3 + b)
                        for i in range(j, j + 2):
                            normalise("moe0", i)

            dve.wait_ge(s.x1_made, 4)
            for g in range(2):
                dve.tensor_scalar(hg_moe[:, g:g + 1], gates[:, 2 + g:3 + g], 0.5, None, ALU.mult).then_inc(a.hg_made, 1)

            def add_rows(ly, j):
                dve.wait_ge(ly.s.got_in[j % 4], 16 * ly.K * (j // 4 + 1))
                for k in range(ly.K):
                    ins = dve.scalar_tensor_tensor(xs[:, j, :], got[:, j % 4, k, :], ly.wgt_g[:, j, k:k + 1],
                                                   xs[:, j, :], ALU.mult, ALU.add)
                    if k < ly.K - 1:
                        link(ins)
                ins.then_inc(ly.s.added, 1)
                dve.wait_ge(ly.s.added, j + 1)

            for ly in layers:
                ls = ly.s
                if ly.i == 1:
                    dve.wait_ge(a.wqkT_psum, 1)
                    dve.tensor_copy(flat(wqkT, 2 * P), bank[:, 5, 0:2 * P]).then_inc(a.wqkT_made, 1)
                    dve.tensor_copy(flat(router1, 2 * E1), bank[:, 5, 2 * P:2 * P + 2 * E1]).then_inc(a.wqkT_made, 1)
                    for n in range(2 * B):
                        dve.wait_ge(a.e_psum, n + 1)
                        dve.tensor_reduce(att_neg[:, n:n + 1], bank[:, 5 + n % 2, 0:L], AX.X, ALU.max,
                                          negate=True).then_inc(a.neg_made, 1)
                        dve.wait_ge(a.aexp_made, n + 1)
                        dve.reciprocal(att_rec[:, n:n + 1], att_sum[:, n:n + 1]).then_inc(a.rec_made, 1)
                        dve.wait_ge(a.rec_made, n + 1)
                        dve.tensor_scalar(att[:, n % 2], att[:, n % 2], att_rec[:, n:n + 1], None,
                                          ALU.mult).then_inc(a.att_made, 1)

                    for j in range(NT + 1):
                        if j < NT:
                            add_rows(layers[0], j)
                            normalise("attention", j)
                        if j >= 1:
                            i = j - 1
                            dve.wait_ge(a.att_psum, i + 1)
                            dve.scalar_tensor_tensor(xs[:, i, :], bank[:, 5 + i % 2, 0:L], gates[:, 1:2], xs[:, i, :],
                                                     ALU.mult, ALU.add).then_inc(a.x3_made, 1)
                            dve.wait_ge(a.x3_made, i + 1)
                            normalise("moe1", i)

                E, K = ly.E, ly.K
                dve.wait_ge(ls.logits_psum, 1)
                link(dve.tensor_copy(flat(logits, NT * E), bank[:, LOGIT_BANK[ly.i], 0:NT * E]))
                for j in range(NT):
                    ins = dve.max(top[:, j, :], ly.logits[:, j, :])
                link(ins)
                for j in range(NT):
                    ins = dve.max_index(topi[:, j, :], top[:, j, :], ly.logits[:, j, :])
                link(ins)
                largest = top[:, :, 0:1]
                ins = dve.tensor_tensor(ly.wexp, top[:, :, 0:K], largest.to_broadcast([P, NT, K]), ALU.subtract)
                if ly.i == 1:
                    ins = dve.tensor_tensor(ly.posf, ly.logits, largest.to_broadcast([P, NT, E]), ALU.subtract)
                ins.then_inc(ls.shifted, 1)
                link(dve.tensor_copy(topf[:], topi[:]))
                link(dve.tensor_tensor(ly.hot, iota_f[:, 0:E].unsqueeze(1).unsqueeze(1).to_broadcast([P, NT, K, E]),
                                       topf[:, :, 0:K].unsqueeze(3).to_broadcast([P, NT, K, E]), ALU.is_equal))
                with nc.allow_low_precision(reason="sums of zeros and one one"):
                    dve.tensor_reduce(ly.chosen.rearrange("p (j e) -> p j e", e=E),
                                      ly.hot.rearrange("p j k e -> p j e k"), AX.X, ALU.add).then_inc(ls.chosen_made, 1)
                dve.wait_ge(ls.exped, 1 + ly.i)
                link(dve.tensor_reduce(wsum[:], ly.wexp, AX.X, ALU.add))
                if ly.i == 1:
                    link(dve.tensor_reduce(wall[:], ly.posf, AX.X, ALU.add))
                    link(dve.scalar_tensor_tensor(wsum[:], wall[:], 1e-9, wsum[:], ALU.mult, ALU.add))
                link(dve.reciprocal(wrec[:], wsum[:]))
                link(dve.tensor_tensor(ly.wgt, ly.wexp, wrec[:].unsqueeze(2).to_broadcast([P, NT, K]), ALU.mult))
                dve.wait_ge(a.hg_made, 2)
                gate = (gates[:, 2:3], hg_moe[:, 1:2])[ly.i]
                link(dve.tensor_scalar(ly.wgt_g, ly.wgt, gate, None, ALU.mult))
                dve.wait_ge(ls.rank_psum, 2)
                link(dve.tensor_tensor(ly.full, bank[:, 7, 0:E].unsqueeze(2).to_broadcast([P, E, NT]),
                                       fill_f[:].unsqueeze(1).to_broadcast([P, E, NT]), ALU.is_gt))
                link(dve.tensor_reduce(ntiles[:, 0:E], ly.full, AX.X, ALU.add))
                link(dve.tensor_tensor_scan(tile_end[:, 0:E], ntiles[:, 0:E], ntiles[:, 0:E], 0.0, ALU.add, ALU.max))
                link(dve.tensor_scalar(ended[:, 0:E], tile_end[:, 0:E], tokid[:, 0:1], None, ALU.is_le))
                link(dve.tensor_reduce(owner[:], ended[:, 0:E], AX.X, ALU.add))
                dve.tensor_scalar(owner[:], owner[:], float(E - 1), None, ALU.min).then_inc(ls.owner_made, 1)
                link(dve.tensor_tensor(row0[:, 0:E], tile_end[:, 0:E], ntiles[:, 0:E], ALU.subtract))
                link(dve.tensor_scalar(row0[:, 0:E], row0[:, 0:E], float(P), None, ALU.mult))
                link(dve.tensor_tensor(ly.posf, bank[:, 6, 0:NT * E].rearrange("p (j e) -> p j e", e=E),
                                       row0[:, 0:E].unsqueeze(1).to_broadcast([P, NT, E]), ALU.add))
                link(dve.tensor_tensor(ly.hot, ly.hot, ly.posf.unsqueeze(2).to_broadcast([P, NT, K, E]), ALU.mult))
                link(dve.tensor_reduce(ly.rowf.rearrange("p (j k) -> p j k", k=K), ly.hot, AX.X, ALU.add))
                rows = flat(row_i, NT * K)
                link(dve.tensor_copy(rows, ly.rowf))
                dve.tensor_scalar(ly.tile_i, rows, P.bit_length() - 1, None, ALU.logical_shift_right)
                link(dve.tensor_scalar(ly.slot_i, rows, P - 1, None, ALU.bitwise_and))
                dve.tensor_copy(flat(tile_f, NT * K), ly.tile_i)
                link(dve.tensor_copy(flat(slot_f, NT * K), ly.slot_i))
                if ly.i == 1:
                    for c in range(2):
                        dve.wait_ge(a.sh_gate, c + 1)
                        dve.scalar_tensor_tensor(gu[:], gg[:], 1.0, bank[:, 1], ALU.add, ALU.mult).then_inc(a.sh_half, 1)
                        dve.wait_ge(a.sh_half, c + 1)
                        dve.wait_ge(ls.sh_psum, 2 * c + 2)
                        dve.tensor_tensor(shT1[:, cols(c)], gu[:], bank[:, 2], ALU.mult).then_inc(ls.sh_made, 1)

                def choices(j):
                    for k in range(K):
                        if not isinstance(j, int):
                            dve.wait_ge(ls.map_used, j * K + (k + 1 - K))
                        token = bass.ds(j, 1)
                        dve.tensor_scalar(slot_hot[:, k, :], iota_h[:], ly.slot_f[:, token, k], None,
                                          ALU.is_equal).then_inc(ls.hot_made, 1)
                        dve.tensor_scalar(tile_tok[:, k, 0:ly.tiles], iota_h[:, 0:ly.tiles], ly.tile_f[:, token, k],
                                          tokid[:, token], ALU.is_equal, ALU.mult).then_inc(ls.hot_made, 1)

                choices(0)
                with dve.Fori(1, NT) as j:
                    choices(j)
                dve.wait_ge(ls.map_used, NT * K)
                dve.tensor_copy(tok_of[:, 0:ly.tiles], bank[:, 0, 0:ly.tiles]).then_inc(ls.tok_made, 1)
                dve.wait_ge(ls.owner_psum, 1)
                dve.tensor_copy(owner_i[:], bank[0:1, 7, 0:P]).then_inc(ls.owner_ready, 1)

                if ly.i == 0:
                    dve.wait_ge(s.b1_in, 16)
                    dve.memset(hidT[64:HH + 1], 1.0).then_inc(a.hidT_ones, 1)
                for j in range(NT):
                    dve.wait_ge(ls.base_psum, j + 1)
                    dve.scalar_tensor_tensor(xs[:, j, :], bank[:, BASE_BANK[ly.i][j // 2], j % 2 * DM:(j % 2 + 1) * DM],
                                             hg_moe[:, ly.i:ly.i + 1], xs[:, j, :], ALU.mult, ALU.add
                                             ).then_inc(ls.based, 1)
                dve.wait_ge(ls.owner_ready, 1)

                def y_out(t0, u):
                    dve.wait_ge(lp.y_psum, t0 + (ly.done + u + 1))
                    if not first_tiles(t0, u, U):
                        dve.wait_ge(lp.y_out[u], slot_count(t0, ly.slot_done[u]))
                    dve.tensor_copy(yt[:, u, :], bank[:, 6 + u % 2, 0:DM]).then_inc(lp.y_made, 1)

                def tile(t0, u):
                    v = u % 2
                    if not first_tiles(t0, u, 2):
                        dve.wait_ge(lp.hidT_psum, t0 + (ly.done + u - 1))
                    if ly.i == 0:
                        e = expert(mybir.EngineType.DVE, ly, t0, u)
                        dve.wait_ge(lp.h_psum, t0 + (ly.done + u + 1))
                        dve.tensor_tensor(hid[:, v, 0:H0], bank[:, 2 + v, 0:H0], b1_bc[:, bass.ds(e, 1), :].squeeze(1),
                                          ALU.add).then_inc(lp.hid_made, 1)
                    else:
                        dve.wait_ge(lp.gate_made, t0 + (u + 1))
                        dve.scalar_tensor_tensor(hid[:, v, 0:H1], gate_th[:, v], 1.0, bank[:, 2 + v, 0:H1],
                                                 ALU.add, ALU.mult).then_inc(lp.half_made, 1)
                        dve.wait_ge(lp.half_made, t0 + (u + 1))
                        dve.tensor_tensor(hid[:, v, 0:H1], hid[:, v, 0:H1], bank[:, 2 + v, H1:2 * H1],
                                          ALU.mult).then_inc(lp.hid_made, 1)
                    if not first_tiles(t0, u, 1):
                        y_out(t0 if u else t0 - U, (u - 1) % U)

                turns(dve, ly, tile)
                y_out(ly.last, U - 2)
            for j in range(NT):
                add_rows(layers[1], j)


_OUT = ((4, 256, 256), "float32")


def kernel(**inputs):
    import numpy as _np
    import concourse.bacc as _bacc
    from concourse.bass_utils import run_bass_kernel_spmd as _run

    nc = _bacc.Bacc("TRN2", target_bir_lowering=False, num_devices=1)
    arrays, io = {}, {}
    for name, value in inputs.items():
        value = _np.ascontiguousarray(value)
        arrays[f"in_{name}"] = value
        io[name] = nc.dram_tensor(f"in_{name}", value.shape, mybir.dt.from_np(value.dtype), kind="ExternalInput").ap()
    out = nc.dram_tensor("out_x", _OUT[0], F32, kind="ExternalOutput").ap()
    flamingo_two_layer_kernel(nc, io, out)
    result = _run(nc, [arrays], core_ids=[0])
    return result.results[0]["out_x"]
```

```python
from contextlib import ExitStack

import concourse.bass as bass
from concourse import mybir
from concourse.alu_op_type import AluOpType as ALU

F32 = mybir.dt.float32
BF16 = mybir.dt.bfloat16
F16 = mybir.dt.float16
I32 = mybir.dt.int32
U32 = mybir.dt.uint32
ACT = mybir.ActivationFunctionType
AX = mybir.AxisListType

P = 128
EPS_LN = 1e-5


class MambaSemaphores:

    def __init__(self, new):
        self.consts = new("consts")
        self.ctx_in = new("ctx_in")
        self.mamba_in = new("mamba_in")
        self.gates_in = new("gates_in")
        self.x_in = new("x_in")
        self.att_in = new("att_in")
        self.l0_in = new("l0_in")
        self.l1_in = new("l1_in")
        self.w1_in = new("w1_in")
        self.w2_in = new("w2_in")
        self.b1_in = new("b1_in")
        self.gates_made = new("gates_made")
        self.hcb_made = new("hcb_made")
        self.wcv_made = new("wcv_made")
        self.dg_made = new("dg_made")
        self.var_made = new("var_made")
        self.rstd_made = new("rstd_made")
        self.dve_step = new("dve_step")
        self.pool_step = new("pool_step")
        self.ctxT_psum = new("ctxT_psum")
        self.ctxT_made = new("ctxT_made")
        self.wcT_psum = new("wcT_psum")
        self.wcT_made = new("wcT_made")
        self.xw_psum = new("xw_psum")
        self.xw_made = new("xw_made")
        self.a_made = new("a_made")
        self.conv_psum = new("conv_psum")
        self.th_made = new("th_made")
        self.u_made = new("u_made")
        self.xp_psum = new("xp_psum")
        self.hi_made = new("hi_made")
        self.dtl_made = new("dtl_made")
        self.parts_made = new("parts_made")
        self.dpre_psum = new("dpre_psum")
        self.abs_made = new("abs_made")
        self.exp_made = new("exp_made")
        self.ln_made = new("ln_made")
        self.w_made_1 = new("w_made_1")
        self.low_made = new("low_made")
        self.low_added = new("low_added")
        self.delta_made = new("delta_made")
        self.du_made = new("du_made")
        self.du2_made = new("du2_made")
        self.z_normed = new("z_normed")
        self.z_th = new("z_th")
        self.z_made = new("z_made")
        self.region_free = new("region_free")
        self.b_bcast = new("b_bcast")
        self.c_bcast = new("c_bcast")
        self.b_copied = new("b_copied")
        self.decay_made = new("decay_made")
        self.inflow_made = new("inflow_made")
        self.scanned = new("scanned")
        self.prod_made = new("prod_made")
        self.y_init = new("y_init")
        self.y_summed = new("y_summed")
        self.gated = new("gated")
        self.mix_psum = new("mix_psum")
        self.x1_made = new("x1_made")


class LayerSemaphores:

    def __init__(self, new, i):
        self.xn_out = new(f"xn_out_l{i}")
        self.logits_psum = new(f"logits_psum_l{i}")
        self.shifted = new(f"shifted_l{i}")
        self.exped = new(f"exped_l{i}")
        self.chosen_made = new(f"chosen_made_l{i}")
        self.rank_psum = new(f"rank_psum_l{i}")
        self.hot_made = new(f"hot_made_l{i}")
        self.map_used = new(f"map_used_l{i}")
        self.pool_hot_made = new(f"pool_hot_made_l{i}")
        self.tok_made = new(f"tok_made_l{i}")
        self.owner_made = new(f"owner_made_l{i}")
        self.owner_psum = new(f"owner_psum_l{i}")
        self.owner_ready = new(f"owner_ready_l{i}")
        self.sh_psum = new(f"sh_psum_l{i}")
        self.sh_made = new(f"sh_made_l{i}")
        self.base_psum = new(f"base_psum_l{i}")
        self.based = new(f"based_l{i}")
        self.added = new(f"added_l{i}")
        self.got_in0 = new(f"got_in0_l{i}")
        self.last_in = [new(f"last_in_l{i}_{k}") for k in range((6, 2)[i])]
        self.got_in1 = new(f"got_in1_l{i}")
        self.got_in2 = new(f"got_in2_l{i}")
        self.got_in3 = new(f"got_in3_l{i}")
        self.got_in = [self.got_in0, self.got_in1, self.got_in2, self.got_in3]


class LoopSemaphores:

    def __init__(self, new):
        self.xgT_psum = new("xgT_psum")
        self.xgT_made = new("xgT_made")
        self.h_psum = new("h_psum")
        self.gate_made = new("gate_made")
        self.half_made = new("half_made")
        self.hid_made = new("hid_made")
        self.hidT_psum = new("hidT_psum")
        self.hidT_made = new("hidT_made")
        self.y_psum = new("y_psum")
        self.y_made = new("y_made")
        self.gathered0 = new("gathered0")
        self.gathered1 = new("gathered1")
        self.gathered2 = new("gathered2")
        self.gathered3 = new("gathered3")
        self.y_out0 = new("y_out0")
        self.y_out1 = new("y_out1")
        self.y_out2 = new("y_out2")
        self.y_out3 = new("y_out3")
        self.gathered = [self.gathered0, self.gathered1, self.gathered2, self.gathered3]
        self.y_out = [self.y_out0, self.y_out1, self.y_out2, self.y_out3]


class AttentionSemaphores:

    def __init__(self, new):
        self.wqkT_psum = new("wqkT_psum")
        self.wqkT_made = new("wqkT_made")
        self.qk_psum = new("qk_psum")
        self.qk_made = new("qk_made")
        self.e_psum = new("e_psum")
        self.neg_made = new("neg_made")
        self.aexp_made = new("aexp_made")
        self.rec_made = new("rec_made")
        self.att_made = new("att_made")
        self.attT_psum = new("attT_psum")
        self.attT_made = new("attT_made")
        self.att_psum = new("att_psum")
        self.x3_made = new("x3_made")
        self.out_done = new("out_done")
        self.hg_made = new("hg_made")
        self.shT_ones = new("shT_ones")
        self.hidT_ones = new("hidT_ones")
        self.wgu_in = new("wgu_in")
        self.sh_gated = new("sh_gated")
        self.sh_copied = new("sh_copied")
        self.sh_half = new("sh_half")


class NormSemaphores:

    def __init__(self, new):
        self.var_found = new("var_found")
        self.std_found = new("std_found")
        self.normed = new("normed")
        self.turned_psum = new("turned_psum")
        self.turned = new("turned")


class Layer:

    def __init__(self, i, done, slot_done, E, K, tiles, last, s, rows, y_rows, logits, chosen, posf, full,
                 hot, wexp, wgt, wgt_g, rowf, row_i, tile_i, slot_i, tile_f, slot_f):
        self.i = i
        self.done = done
        self.slot_done = slot_done
        self.E = E
        self.K = K
        self.tiles = tiles
        self.last = last
        self.s = s
        self.rows = rows
        self.y_rows = y_rows
        self.logits = logits
        self.chosen = chosen
        self.posf = posf
        self.full = full
        self.hot = hot
        self.wexp = wexp
        self.wgt = wgt
        self.wgt_g = wgt_g
        self.rowf = rowf
        self.row_i = row_i
        self.tile_i = tile_i
        self.slot_i = slot_i
        self.tile_f = tile_f
        self.slot_f = slot_f


def flamingo_two_layer_kernel(nc, io, out):
    B, L, DM = io["x"].shape
    DC = io["ctx_1024"].shape[2]
    DI = io["L0_xattn_in_proj_w"].shape[0]
    TAPS = io["L0_xattn_conv_w"].shape[1]
    DR = io["L0_xattn_dt_proj_w"].shape[1]
    DS = io["L0_xattn_A_log"].shape[1]
    E0, _, H0 = io["L0_ffn_rw1"].shape
    NSH = io["L0_ffn_sw1"].shape[0]
    E1, _, H1 = io["L1_ffn_Wg"].shape
    K0, K1 = 6, 2
    T = B * L
    NT = T // P
    HH = H0 // 2
    TILES0 = (T * K0 + E0 * (P - 1)) // P
    TILES1 = (T * K1 + E1 * (P - 1)) // P
    CH = 2 * L
    NB = DS * 2
    U = 8
    POOL_CHOICES = ((5,), ())
    MAP_SLOTS = K0 + len(POOL_CHOICES[0])
    R = 4
    assert DC == P and DI == 2 * P and DM == 2 * P and L == 2 * P and B == 4 and H1 == P
    assert TILES0 % U == U - 1 and TILES1 % U == U - 1

    with ExitStack() as stack:
        def sb(name, shape, dt=F32, on=stack):
            return on.enter_context(nc.sbuf_tensor(name, shape, dt))

        def semaphore(name):
            return stack.enter_context(nc.semaphore(name))

        bank = stack.enter_context(nc.psum_tensor("bank", [P, 8, 512], F32))

        xn_rows0 = nc.dram_tensor("xn_rows0", [T, DM], F32, kind="Internal").ap()
        xn_rows1 = nc.dram_tensor("xn_rows1", [T, DM], F32, kind="Internal").ap()
        y_rows0 = nc.dram_tensor("y_rows0", [TILES0 * P, DM], F32, kind="Internal").ap()
        y_rows1 = nc.dram_tensor("y_rows1", [TILES1 * P, DM], F32, kind="Internal").ap()

        ident = sb("ident", [P, P])
        eye3 = sb("eye3", [P, NB], BF16)
        before = sb("before", [P, P], BF16)
        ones16 = sb("ones16", [P, P], BF16)
        iota_i = sb("iota_i", [P, P], I32)
        iota_f = sb("iota_f", [P, P])
        iota_h = sb("iota_h", [P, P], F16)
        count_i = sb("count_i", [P, NT], I32)
        fill_f = sb("fill_f", [P, NT])
        tokid = sb("tokid", [P, NT])
        minus_half = sb("minus_half", [P, NT])
        gates_raw = sb("gates_raw", [P, 4])
        gates = sb("gates", [P, 4])
        xs = sb("xs", [P, NT, DM])
        ctxT = sb("ctxT", [P, B, TAPS - 1 + L])
        hg_moe = sb("hg_moe", [P, 2])
        stats = sb("stats", [P, NT, 6])
        meanvar = sb("meanvar", [P, NT, 2])
        vareps = sb("vareps", [P, NT])
        rstd = sb("rstd", [P, NT])
        std = sb("std", [P, NT])
        eps = sb("eps", [P, 1])
        wq = sb("wq", [P, P])
        wk = sb("wk", [P, P])
        wqkT = sb("wqkT", [P, 2, P])
        bqk = sb("bqk", [P, 2])
        router0 = sb("router0", [P, 2, E0])
        rbias0 = sb("rbias0", [P, E0])
        router1 = sb("router1", [P, 2, E1])
        wr_rows = sb("wr_rows", [E1, DM])
        rbias1 = sb("rbias1", [P, E1])
        sw1 = sb("sw1", [P, NSH * 2, H0])
        sb1 = sb("sb1", [HH, NSH, 2])
        sw2 = sb("sw2", [HH + 1, NSH, 2, DM])
        swg = sb("swg", [P, 2, H1])
        swu = sb("swu", [P, 2, H1])
        swd = sb("swd", [P, DM])

        r1 = ExitStack()
        w1 = sb("w1", [P, E0, 2, H0], on=r1)
        r1.close()
        r1 = ExitStack()
        got = sb("got", [P, 4, K0, DM], on=r1)
        sh_gate = sb("sh_gate", [P, T], on=r1)
        sh_up = sb("sh_up", [P, T], on=r1)
        sh_tanh = sb("sh_tanh", [P, T], on=r1)
        shT1 = sb("shT1", [P, T], on=r1)
        r1.close()
        hold1 = sb("hold1", [P, E0 * 2 * H0])
        r2 = ExitStack()
        w2 = sb("w2", [HH + 1, E0, 2, DM], on=r2)
        r2.close()
        r2 = ExitStack()
        wgu = sb("wgu", [P, E1 * 2, 2, H1], on=r2)
        wd = sb("wd", [P, E1, DM], on=r2)
        r2.close()
        hold2 = sb("hold2", [P, E0 * 2 * DM])
        r3 = ExitStack()
        cu = sb("cu", [P, 2, T], on=r3)
        delta = sb("delta", [P, 2, T], on=r3)
        du = sb("du", [P, 2, T], on=r3)
        sz = sb("sz", [P, NT, DM], on=r3)
        bcp = sb("bcp", [P, T], BF16, on=r3)
        cw = sb("cw", [P, 2, TAPS], on=r3)
        cb = sb("cb", [P, 2], on=r3)
        hcb = sb("hcb", [P, 2], on=r3)
        dtb = sb("dtb", [P, 2], on=r3)
        dsk = sb("dsk", [P, 2], on=r3)
        a_log = sb("a_log", [P, 2, DS], on=r3)
        a_exp = sb("a_exp", [P, 2, DS], on=r3)
        a_neg = sb("a_neg", [P, 2, DS], on=r3)
        dg = sb("dg", [P, 2, P], on=r3)
        hg = sb("hg", [P, 1], on=r3)
        r3a = ExitStack()
        r3f = ExitStack()
        ctx_nat = sb("ctx_nat", [P, NT, DC], on=r3f)
        wcv = sb("wcv", [P, 2, TAPS, DC], on=r3f)
        r3f.close()
        exp_v = sb("exp_v", [P, 4, CH], on=r3a)
        wip = sb("wip", [P, 2, DC], on=r3a)
        wcT = sb("wcT", [P, TAPS, 2, P], on=r3a)
        xpw = sb("xpw", [DR + NB, DI], on=r3a)
        dtw = sb("dtw", [P, 2, DR], on=r3a)
        wxT = sb("wxT", [P, 2, P], on=r3a)
        dtpT = sb("dtpT", [DR, 2, P], on=r3a)
        dtl = sb("dtl", [DR, T], on=r3a)
        th = sb("th", [P, 2, CH], on=r3a)
        part = sb("part", [P, CH], on=r3a)
        part16 = sb("part16", [P, CH], BF16, on=r3a)
        ln_v = sb("ln_v", [P, 4, CH], on=r3a)
        r3a.close()
        r3b = ExitStack()
        b_sb = sb("b_sb", [P, 2, CH], on=r3b)
        decay = sb("decay", [P, 2, 2, 2, L], on=r3b)
        inflow = sb("inflow", [P, 2, 2, CH], on=r3b)
        state = sb("state", [P, 2, CH], on=r3b)
        prod = sb("prod", [P, 2, 2, CH], on=r3b)
        r3b.close()
        r3.close()
        r3 = ExitStack()
        r3g = ExitStack()
        shT_late = sb("shT_late", [HH + 1, NSH * 2, CH], on=r3g)
        r3g.close()
        attT = sb("attT", [P, B, 2, L], on=r3)
        xn = sb("xn", [P, NT, DM], on=r3)
        b1_bc = sb("b1_bc", [P, E0, H0], on=r3)
        logits = sb("logits", [P, NT, E0], on=r3)
        top = sb("top", [P, NT, 8], on=r3)
        topi = sb("topi", [P, NT, 8], U32, on=r3)
        topf = sb("topf", [P, NT, 8], on=r3)
        wexp = sb("wexp", [P, NT, K0], on=r3)
        wsum = sb("wsum", [P, NT], on=r3)
        wall = sb("wall", [P, NT], on=r3)
        wrec = sb("wrec", [P, NT], on=r3)
        wgt = sb("wgt", [P, NT, K0], on=r3)
        wgt_g = sb("wgt_g", [P, NT, K0], on=r3)
        chosen = sb("chosen", [P, NT, E0], BF16, on=r3)
        full = sb("full", [P, E0, NT], on=r3)
        ntiles = sb("ntiles", [P, E0], on=r3)
        tile_end = sb("tile_end", [P, E0], on=r3)
        row0 = sb("row0", [P, E0], on=r3)
        posf = sb("posf", [P, NT, E0], on=r3)
        rowf = sb("rowf", [P, NT, K0], on=r3)
        row_i = sb("row_i", [P, NT, K0], I32, on=r3)
        tile_i = sb("tile_i", [P, NT, K0], I32, on=r3)
        slot_i = sb("slot_i", [P, NT, K0], I32, on=r3)
        tile_f = sb("tile_f", [P, NT, K0], on=r3)
        slot_f = sb("slot_f", [P, NT, K0], on=r3)
        tok_of = sb("tok_of", [P, TILES0 + 1], I32, on=r3)
        ended = sb("ended", [P, E0], on=r3)
        owner = sb("owner", [P, 1], on=r3)
        owner_i = sb("owner_i", [1, P], I32, on=r3)
        r3d = ExitStack()
        att = sb("att", [P, 2, L], on=r3d)
        r3d.close()
        r3d = ExitStack()
        slot_hot = sb("slot_hot", [P, MAP_SLOTS, P], F16, on=r3d)
        r3d.close()
        hold3 = sb("hold3", [P, 2 * L], on=r3)
        att_max = sb("att_max", [P, 2 * B], on=r3)
        att_neg = sb("att_neg", [P, 2 * B], on=r3)
        att_sum = sb("att_sum", [P, 2 * B], on=r3)
        att_rec = sb("att_rec", [P, 2 * B], on=r3)
        xnT = sb("xnT", [P, 2, T], on=r3)
        r3c = ExitStack()
        hot = sb("hot", [P, NT, K0, E0], on=r3c)
        r3e = ExitStack()
        qT = sb("qT", [P, T], on=r3e)
        kT = sb("kT", [P, T], on=r3e)
        r3e.close()
        r3e = ExitStack()
        shT = sb("shT", [HH + 1, NSH * 2, CH], on=r3e)
        r3e.close()
        hold4 = sb("hold4", [P, 2 * T], on=r3c)
        tile_tok = sb("tile_tok", [P, MAP_SLOTS, TILES0], F16, on=r3c)
        r3c.close()
        xg = sb("xg", [P, R, DM], on=r3)
        xgT = sb("xgT", [P, 2, 2, P], on=r3)
        hid = sb("hid", [P, 2, DM], on=r3)
        gate_th = sb("gate_th", [P, 2, H1], on=r3)
        hidT = sb("hidT", [P, 2, 2, P], on=r3)
        yt = sb("yt", [P, R, DM], on=r3)
        r3.close()

        def flat(t, n, start=0):
            ap = t[:]
            if len(ap.shape) > 2:
                names = " ".join("abcde"[:len(ap.shape) - 1])
                ap = ap.rearrange(f"p {names} -> p ({names})")
            return ap[:, start:start + n]

        def cols(p):
            return slice(p * CH, (p + 1) * CH)

        s = MambaSemaphores(semaphore)
        lp = LoopSemaphores(semaphore)
        norm = NormSemaphores(semaphore)
        layers = []
        for i, (E, K, tiles, H) in enumerate(((E0, K0, TILES0, H0), (E1, K1, TILES1, H1))):
            layers.append(Layer(
                i=i, done=(0, TILES0)[i], slot_done=[(0, (TILES0 - 1 - r) // R + 1)[i] for r in range(R)], E=E, K=K, tiles=tiles, last=tiles + 1 - U, s=LayerSemaphores(semaphore, i),
                rows=(xn_rows0, xn_rows1)[i], y_rows=(y_rows0, y_rows1)[i],
                logits=flat(logits, NT * E).rearrange("p (j e) -> p j e", e=E),
                chosen=flat(chosen, NT * E), posf=flat(posf, NT * E).rearrange("p (j e) -> p j e", e=E),
                full=flat(full, E * NT).rearrange("p (e m) -> p e m", m=NT),
                hot=flat(hot, NT * K * E).rearrange("p (j k e) -> p j k e", k=K, e=E),
                wexp=flat(wexp, NT * K).rearrange("p (j k) -> p j k", k=K),
                wgt=flat(wgt, NT * K).rearrange("p (j k) -> p j k", k=K),
                wgt_g=flat(wgt_g, NT * K).rearrange("p (j k) -> p j k", k=K),
                rowf=flat(rowf, NT * K), row_i=flat(row_i, NT * K).rearrange("p (j k) -> p j k", k=K),
                tile_i=flat(tile_i, NT * K), slot_i=flat(slot_i, NT * K),
                tile_f=flat(tile_f, NT * K).rearrange("p (j k) -> p j k", k=K),
                slot_f=flat(slot_f, NT * K).rearrange("p (j k) -> p j k", k=K),
            ))
        a = AttentionSemaphores(semaphore)

        def first_tiles(t0, u, n):
            return isinstance(t0, int) and t0 + u < n

        def at(t0, u, d):
            return (t0 + (u + d) // U * U, (u + d) % U) if (u + d) // U else (t0, u + d)

        def exists(ly, t0, u):
            return not isinstance(t0, int) or 0 <= t0 + u < ly.tiles

        def turns(eng, ly, body):
            for u in range(U):
                body(0, u)
            with eng.Fori(U, ly.last, U) as t0:
                for u in range(U):
                    body(t0, u)
            for u in range(U - 1):
                body(ly.last, u)

        def expert(engine, ly, t0, u):
            return nc.values_load(owner_i[0:1, bass.ds(t0 + u, 1)], engines=(engine,), min_val=0, max_val=ly.E - 1,
                                  skip_runtime_bounds_check_because="VectorE clamped it to the experts")

        def all_added(ly, j):
            return ly.K * (j + 1)

        def slot_count(ly, t0, u, n):
            return t0 * (16 // R) + 16 * (ly.slot_done[u % R] + u // R + n)

        norm_order = [("moe0", j) for j in range(NT)]
        COMBINE_STEPS = NT + 2

        def combine_norms(j):
            return ([("attention", j - 1)] if 1 <= j <= NT else []) + ([("moe1", j - 2)] if j >= 2 else [])

        for j in range(COMBINE_STEPS):
            norm_order += combine_norms(j)

        def norm_count(kind, j):
            return norm_order.index((kind, j)) + 1

        def map_slot(ly, j, k):
            if ly.i == 1:
                return j % 2 * ly.K + k
            pools = POOL_CHOICES[0]
            return ly.K + pools.index(k) if k in pools and j % 2 else k

        def moe_norm(ly, j):
            return norm_count(f"moe{ly.i}", j)

        CONV_BANK = (5, 6, 7, 0)
        Y_BANK = ((5, 6), (7, 0))
        LOGIT_BANK = (5, 0)
        BASE_BANK = ((1, 2, 5, 6), (3, 4, 5, 6))
        EARLY = 5
        OUTS_AHEAD = 3
        N_CONSTS = 19

        block = stack.enter_context(nc.Block())

        @block.sync
        def _(sp):
            sp.dma_start(ctx_nat[:], io["ctx_1024"].rearrange("b (s p) d -> p (b s) d", p=P)).then_inc(s.ctx_in, 16)
            for dst, src in (
                (wip[:], io["L0_xattn_in_proj_w"].rearrange("(h p) d -> p h d", p=P)),
                (cw[:], io["L0_xattn_conv_w"].rearrange("(h p) k -> p h k", p=P)),
                (cb[:], io["L0_xattn_conv_b"].rearrange("(h p) -> p h", p=P)),
                (xpw[:], io["L0_xattn_x_proj_w"]),
                (dtw[:], io["L0_xattn_dt_proj_w"].rearrange("(h p) r -> p h r", p=P)),
                (dtb[:], io["L0_xattn_dt_proj_b"].rearrange("(h p) -> p h", p=P)),
                (dsk[:], io["L0_xattn_D"].rearrange("(h p) -> p h", p=P)),
                (a_log[:], io["L0_xattn_A_log"].rearrange("(h p) n -> p h n", p=P)),
            ):
                sp.dma_start(dst, src, allow_slow_non_contiguous=True).then_inc(s.mamba_in, 16)
            sp.dma_start(xs[:], io["x"].rearrange("b (s p) d -> p (b s) d", p=P)).then_inc(s.x_in, 16)
            for i, name in enumerate(("g_xattn", "g_ffn")):
                sp.dma_start(gates_raw[:, 2 * i:2 * i + 2], io[name].partition_broadcast(P)).then_inc(s.gates_in, 16)
            quarter = E0 // 4
            for q in range(4):
                e = slice(q * quarter, (q + 1) * quarter)
                sp.dma_start(w1[:, e].rearrange("p e k h -> p (e k) h"),
                             io["L0_ffn_rw1"][e].rearrange("e (k p) h -> p (e k) h", p=P)).then_inc(s.w1_in, 16)
                sp.dma_start(w2[0:HH, e].rearrange("p e k d -> p (e k) d"),
                             io["L0_ffn_rw2"][e].rearrange("e (k p) d -> p (e k) d", p=HH)).then_inc(s.w2_in, 16)
            sp.dma_start(w2[HH:HH + 1, :, 1, :], io["L0_ffn_rb2"].unsqueeze(0)).then_inc(s.w2_in, 16)
            for dst, src in (
                (router0[:], io["L0_ffn_router_w"].rearrange("(k p) e -> p k e", p=P)),
                (rbias0[:], io["L0_ffn_router_b"].partition_broadcast(P)),
                (sw1[:], io["L0_ffn_sw1"].rearrange("e (k p) h -> p (e k) h", p=P)),
                (sb1[:], io["L0_ffn_sb1"].rearrange("e (m p) -> p e m", p=HH)),
                (sw2[0:HH].rearrange("p e k d -> p (e k) d"), io["L0_ffn_sw2"].rearrange("e (k p) d -> p (e k) d", p=HH)),
                (sw2[HH:HH + 1, :, 1, :], io["L0_ffn_sb2"].unsqueeze(0)),
            ):
                sp.dma_start(dst, src, allow_slow_non_contiguous=True).then_inc(s.l0_in, 16)
            for dst, src in (
                (wq[:], io["L1_xattn_Wq"]), (wk[:], io["L1_xattn_Wk"]),
                (bqk[:, 0:1], io["L1_xattn_bq"].unsqueeze(1)), (bqk[:, 1:2], io["L1_xattn_bk"].unsqueeze(1)),
            ):
                sp.dma_start(dst, src, allow_slow_non_contiguous=True).then_inc(s.att_in, 16)
            for dst, src in (
                (wr_rows[:], io["L1_ffn_Wr"]), (rbias1[:], io["L1_ffn_bias"].partition_broadcast(P)),
                (swg[:], io["L1_ffn_sWg"].rearrange("(k p) i -> p k i", p=P)),
                (swu[:], io["L1_ffn_sWu"].rearrange("(k p) i -> p k i", p=P)), (swd[:], io["L1_ffn_sWd"]),
            ):
                sp.dma_start(dst, src).then_inc(s.l1_in, 16)
            sp.wait_ge(s.x1_made, 4)
            sp.dma_start(b1_bc[:].rearrange("p e h -> p (e h)"),
                         io["L0_ffn_rb1"].rearrange("e h -> (e h)").partition_broadcast(P)).then_inc(s.b1_in, 16)
            for ly in layers:
                for j in range(NT):
                    sp.wait_ge(norm.normed, moe_norm(ly, j))
                    sp.dma_start(ly.rows[j * P:(j + 1) * P, :], xn[:, j, :]).then_inc(ly.s.xn_out, 16)

                def store(t0, u):
                    sp.wait_ge(lp.y_made, t0 + (ly.done + u + 1))
                    sp.dma_start(ly.y_rows[bass.ds(t0 * P + u * P, P), :], yt[:, u % R, :]).then_inc(lp.y_out[u % R], 16)

                turns(sp, ly, store)
                if ly.i == 0:
                    sp.wait_ge(lp.y_psum, ly.done + ly.tiles)
                    piece = 0
                    for e in (slice(0, E1 // 2), slice(E1 // 2, E1)):
                        for k in range(2):
                            for g, name in enumerate(("L1_ffn_Wg", "L1_ffn_Wu")):
                                sp.wait_ge(ly.s.added, K0 + 4 * piece)
                                piece += 1
                                sp.dma_start(wgu[:].rearrange("p (e k) g i -> p e k g i", k=2)[:, e, k, g, :],
                                             io[name][e].rearrange("e (k p) i -> k p e i", p=P)[k]).then_inc(a.wgu_in, 16)
                        sp.wait_ge(ly.s.added, K0 + 4 * piece)
                        piece += 1
                        sp.dma_start(wd[:, e], io["L1_ffn_Wd"][e].rearrange("e i d -> i e d")).then_inc(a.wgu_in, 16)
            for j in range(NT):
                sp.wait_ge(layers[1].s.added, all_added(layers[1], j))
                sp.dma_start(out[j // 2, j % 2 * P:(j % 2 + 1) * P, :], xs[:, j, :]).then_inc(a.out_done, 16)
            sp.wait_ge(a.out_done, 16 * NT)

        @block.gpsimd
        def _(pool):
            def const(ins):
                ins.then_inc(s.consts, 1)
                made[0] += 1
                pool.wait_ge(s.consts, made[0])

            made = [0]
            const(pool.memset(ident[:], 0.0))
            const(pool.affine_select(out=ident[:], in_=ident[:], compare_op=ALU.not_equal, fill=1.0, base=0,
                                     pattern=[[-1, P]], channel_multiplier=1))
            const(pool.memset(ctxT[:, :, 0:TAPS - 1], 0.0))
            const(pool.memset(minus_half[:], -0.5))
            const(pool.memset(eps[:], EPS_LN))
            const(pool.memset(eye3[:], 0.0))
            const(pool.memset(bcp[0:NB], 0.0))
            for q in range(1, 4):
                const(pool.affine_select(out=eye3[:], in_=eye3[:], compare_op=ALU.not_equal, fill=1.0, base=-NB * q,
                                         pattern=[[-1, NB]], channel_multiplier=1))
            const(pool.memset(ones16[:], 1.0))
            const(pool.affine_select(out=before[:], in_=ones16[:], compare_op=ALU.is_gt, fill=0.0, base=0,
                                     pattern=[[1, P]], channel_multiplier=-1))
            const(pool.iota(iota_i[:], pattern=[[1, P]], base=0, channel_multiplier=0))
            const(pool.tensor_copy(iota_f[:], iota_i[:]))
            const(pool.tensor_copy(iota_h[:], iota_i[:]))
            const(pool.iota(count_i[:], pattern=[[P, NT]], base=0, channel_multiplier=0))
            const(pool.tensor_copy(fill_f[:], count_i[:]))
            const(pool.iota(count_i[:], pattern=[[P, NT]], base=0, channel_multiplier=1))
            const(pool.tensor_copy(tokid[:], count_i[:]))
            assert made[0] == N_CONSTS

            pool.wait_ge(s.var_made, 1)
            pool.tensor_tensor(rstd[:], vareps[:], minus_half[:], ALU.pow).then_inc(s.rstd_made, 1)

            for q in range(4):
                pool.wait_ge(s.w_made_1, q + 1)
                pool.tensor_tensor(th[:, q % 2], exp_v[:, q], th[:, q % 2], ALU.subtract).then_inc(s.low_made, 1)

            def step(p, t, slot):
                for h in range(2):
                    if h == 0:
                        pool.wait_ge(s.b_copied, t + 1)
                    if not (isinstance(t, int) and t < 2):
                        pool.wait_ge(s.scanned, 2 * (t - 2) + h + 1)
                    pool.tensor_tensor(inflow[:, slot, h], du[:, h, cols(p)], b_sb[:, slot],
                                       ALU.mult).then_inc(s.inflow_made, 1)

            for h in range(2):
                pool.wait_ge(s.delta_made, h + 1)
                pool.tensor_tensor(du[:, h, cols(0)], delta[:, h, cols(0)], cu[:, h, cols(0)],
                                   ALU.mult).then_inc(s.du_made, 1)
            pool.wait_ge(s.du_made, 2)
            pool.wait_ge(s.region_free, 1)
            for p in range(2):
                for i in range(2):
                    step(p, p * DS + i, i)
                with pool.Fori(1, DS // 2) as m:
                    for i in range(2):
                        step(p, 2 * m + (p * DS + i), i)

            pool.wait_ge(s.y_summed, 4 * DS)
            pool.memset(shT[64:HH + 1], 1.0).then_inc(a.shT_ones, 1)
            pool.wait_ge(s.x1_made, 4)
            pool.memset(shT_late[64:HH + 1], 1.0).then_inc(a.shT_ones, 1)

            for ly in layers:
                ls = ly.s
                if ly.i == 1:
                    for c in range(2):
                        h = sh_tanh[:, cols(c)]
                        pool.wait_ge(a.sh_gated, c + 1)
                        pool.tensor_tensor(h, h, sh_gate[:, cols(c)], ALU.mult).then_inc(a.sh_half, 1)
                        pool.wait_ge(a.sh_half, 3 * c + 1)
                        pool.tensor_tensor(h, h, sh_gate[:, cols(c)], ALU.add).then_inc(a.sh_half, 1)
                        pool.wait_ge(a.sh_half, 3 * c + 2)
                        pool.tensor_tensor(shT1[:, cols(c)], h, sh_up[:, cols(c)], ALU.mult).then_inc(a.sh_half, 1)
                made_here = 0
                for j in range(NT):
                    for k in POOL_CHOICES[ly.i]:
                        slot = map_slot(ly, j, k)
                        if made_here:
                            pool.wait_ge(ls.pool_hot_made, made_here)
                        else:
                            pool.wait_ge(a.shT_ones, 2)
                            pool.wait_ge(ls.hot_made, 1)
                        if j >= 2:
                            pool.wait_ge(ls.map_used, (j - 2) * ly.K + k + 1)
                        pool.tensor_scalar(slot_hot[:, slot, :], iota_h[:], ly.slot_f[:, j, k:k + 1], None,
                                           ALU.is_equal).then_inc(ls.pool_hot_made, 1)
                        pool.wait_ge(ls.pool_hot_made, made_here + 1)
                        pool.tensor_scalar(tile_tok[:, slot, 0:ly.tiles], iota_h[:, 0:ly.tiles],
                                           ly.tile_f[:, j, k:k + 1], tokid[:, j:j + 1], ALU.is_equal, ALU.mult
                                           ).then_inc(ls.pool_hot_made, 1)
                        made_here += 2
                pool.wait_ge(ls.xn_out, 16 * NT)
                pool.wait_ge(ls.tok_made, 1)

                for t in range(ly.tiles):
                    if t >= R:
                        pool.wait_ge(lp.xgT_psum, ly.done + t - (R - 1))
                    pool.indirect_dma_start(xg[:, t % R, :], None, ly.rows,
                                            bass.IndirectOffsetOnAxis(ap=tok_of[:, t:t + 1], axis=0)
                                            ).then_inc(lp.gathered[t % R], 16)
                for r in range(R):
                    pool.wait_ge(lp.y_out[r], 16 * (ly.slot_done[r] + (ly.tiles - 1 - r) // R + 1))
                for j in range(NT):
                    b = j % 4
                    if j >= 4:
                        pool.wait_ge(ls.added, all_added(ly, j - 4))
                    for k in range(ly.K):
                        pool.indirect_dma_start(got[:, b, k, :], None, ly.y_rows,
                                                bass.IndirectOffsetOnAxis(ap=ly.row_i[:, j, k:k + 1], axis=0)
                                                ).then_inc(ls.last_in[k] if j == NT - 1 else ls.got_in[b], 16)

        @block.scalar
        def _(act):
            for i in range(2):
                if i == 0:
                    act.wait_ge(s.consts, 3)
                act.wait_ge(s.ctxT_psum, i + 1)
                act.copy(ctxT[:, 2 * i:2 * i + 2, TAPS - 1:],
                         bank[:, i].rearrange("p (b l) -> p b l", b=2)).then_inc(s.ctxT_made, 1)
            act.wait_ge(s.wcT_psum, 1)
            act.copy(flat(wcT, CH), bank[:, 2]).then_inc(s.wcT_made, 1)
            act.wait_ge(s.gates_in, 32)
            act.activation(gates[:], gates_raw[:], ACT.Tanh).then_inc(s.gates_made, 1)

            act.wait_ge(s.hcb_made, 1)

            def tanh_u(q):
                h = q % 2
                act.wait_ge(s.conv_psum, q + 1)
                if q >= 2:
                    act.wait_ge(s.u_made, q - 1)
                act.activation(th[:, h], bank[:, CONV_BANK[q]], ACT.Tanh, bias=hcb[:, h:h + 1],
                               scale=0.5).then_inc(s.th_made, 1)

            def tanh_z(i):
                act.wait_ge(s.z_normed, 2 * i + 2)
                act.activation(ln_v[:, i], flat(sz, CH, i * CH), ACT.Tanh, scale=0.5).then_inc(s.z_th, 1)

            tanh_u(0)
            tanh_u(1)
            tanh_z(0)
            tanh_z(1)
            tanh_u(2)
            tanh_z(2)
            tanh_z(3)
            tanh_u(3)
            for p in range(2):
                act.wait_ge(s.xp_psum, p + 1)
                act.copy(dtl[:, cols(p)], bank[0:DR, 1 + p]).then_inc(s.dtl_made, 1)
                if p >= 1:
                    act.wait_ge(s.parts_made, 4 * p)
                act.copy(part16[:], bank[:, 1 + p]).then_inc(s.hi_made, 1)
                act.copy(bcp[NB:2 * NB, cols(p)], bank[NB:2 * NB, 1 + p]).then_inc(s.hi_made, 1)
                for q in (2 * p, 2 * p + 1):
                    h = q % 2
                    act.wait_ge(s.dpre_psum, q + 1)
                    act.activation(exp_v[:, q], bank[:, CONV_BANK[q]], ACT.Abs, bias=dtb[:, h:h + 1]).then_inc(s.abs_made, 1)
                    act.activation(delta[:, h, cols(p)], bank[:, CONV_BANK[q]], ACT.Relu,
                                   bias=dtb[:, h:h + 1]).then_inc(s.abs_made, 1)
                    act.wait_ge(s.abs_made, 2 * q + 2)
                    act.activation(exp_v[:, q], exp_v[:, q], ACT.Exp, scale=-1.0).then_inc(s.exp_made, 1)
            act.wait_ge(s.z_made, 4)
            for q in range(4):
                act.wait_ge(s.exp_made, q + 1)
                act.activation(ln_v[:, q], exp_v[:, q], ACT.Ln, bias=1.0).then_inc(s.ln_made, 1)
            act.wait_ge(s.mamba_in, 128)
            act.activation(a_exp[:], a_log[:], ACT.Exp).then_inc(s.a_made, 1)
            act.wait_ge(s.a_made, 1)
            act.mul(a_neg[:], a_exp[:], -1.0).then_inc(s.a_made, 1)

            a_of = a_neg[:].rearrange("p h (m i) -> p h m i", i=2)

            def step(p, t, m, slot):
                act.wait_ge(s.b_bcast, t + 1)
                first = isinstance(t, int) and t < 2
                if not first:
                    act.wait_ge(s.inflow_made, 2 * (t - 1))
                act.copy(b_sb[:, slot], bank[:, 1 + slot]).then_inc(s.b_copied, 1)
                for h in range(2):
                    if not first:
                        act.wait_ge(s.scanned, 2 * (t - 2) + h + 1)
                    act.activation(decay[:, slot, h, :, 1:],
                                   delta[:, h, cols(p)].rearrange("p (b l) -> p b l", b=2)[:, :, 1:],
                                   ACT.Exp, scale=a_of[:, h, bass.ds(m, 1), slot]).then_inc(s.decay_made, 1)

            act.wait_ge(s.region_free, 1)
            act.wait_ge(s.a_made, 2)
            for p in range(2):
                for i in range(2):
                    step(p, p * DS + i, 0, i)
                with act.Fori(1, DS // 2) as m:
                    for i in range(2):
                        step(p, 2 * m + (p * DS + i), m, i)

            def deviation(n):
                j = norm_order[n - 1][1]
                act.wait_ge(norm.var_found, n)
                act.activation(std[:, j:j + 1], meanvar[:, j, 1:2], ACT.Sqrt, bias=eps[:]).then_inc(norm.std_found, 1)

            def turned(n):
                j = norm_order[n - 1][1]
                act.wait_ge(norm.turned_psum, n)
                act.copy(xnT[:, :, j * P:(j + 1) * P],
                         bank[:, 1 + n % 2, 0:DM].rearrange("p (k t) -> p k t", k=2)).then_inc(norm.turned, 1)

            def shared_copied(c):
                ls = layers[1].s
                for g, dst in enumerate((sh_gate, sh_up)):
                    act.wait_ge(ls.sh_psum, 2 * c + g + 1)
                    act.copy(dst[:, cols(c)], bank[:, 3 + g]).then_inc(a.sh_copied, 1)

            def shared_hidden(n):
                em, c = n % 4, n // 4
                act.wait_ge(layers[0].s.sh_psum, n + 1)
                act.wait_ge(a.shT_ones, c + 1)
                act.activation((shT, shT_late)[c][0:HH, em], bank[0:HH, 3 + n % 2], ACT.Relu,
                               bias=sb1[:, em // 2, em % 2:em % 2 + 1]).then_inc(layers[0].s.sh_made, 1)

            for ly in layers:
                ls = ly.s
                if ly.i == 1:
                    for c in range(4):
                        act.wait_ge(a.qk_psum, c + 1)
                        if c == 2:
                            for r in range(R):
                                act.wait_ge(lp.y_out[r], 16 * layers[1].slot_done[r])
                        act.activation((qT, kT)[c // 2][:, cols(c % 2)], bank[:, (5, 6, 7, 0)[c]], ACT.Identity,
                                       bias=bqk[:, c // 2:c // 2 + 1]).then_inc(a.qk_made, 1)
                    for n in range(2 * B + 1):
                        if n < 2 * B:
                            act.wait_ge(a.neg_made, n + 1)
                            if n >= 2:
                                act.wait_ge(a.attT_psum, n - 1)
                            act.activation(att[:, n % 2], bank[:, 5 + n % 2, 0:L], ACT.Exp, bias=att_neg[:, n:n + 1],
                                           accum_out=att_sum[:, n:n + 1]).then_inc(a.aexp_made, 1)
                        if n >= 1:
                            i = n - 1
                            act.wait_ge(a.attT_psum, i + 1)
                            act.copy(attT[:, i // 2, :, (i % 2) * P:(i % 2 + 1) * P],
                                     bank[:, (7, 0)[i % 2], 0:2 * P].rearrange("p (k r) -> p k r", k=2)
                                     ).then_inc(a.attT_made, 1)
                    for j in range(COMBINE_STEPS):
                        for kind, i in combine_norms(j):
                            deviation(norm_count(kind, i))
                        for kind, i in combine_norms(j):
                            turned(norm_count(kind, i))
                    for c in range(2):
                        shared_copied(c)
                        act.wait_ge(a.sh_copied, 2 * c + 2)
                        act.activation(sh_tanh[:, cols(c)], sh_gate[:, cols(c)], ACT.Tanh, scale=0.5
                                       ).then_inc(a.sh_gated, 1)
                else:
                    for n in range(1, NT + 1, 2):
                        deviation(n)
                        deviation(n + 1)
                        if n == NT - 1:
                            shared_hidden(0)
                        turned(n)
                        turned(n + 1)
                    for n in range(1, EARLY):
                        shared_hidden(n)
                act.wait_ge(ls.shifted, 1)
                act.activation(ly.wexp, ly.wexp, ACT.Exp).then_inc(ls.exped, 1)
                if ly.i == 0:
                    for n in range(EARLY, 2 * NSH * 2):
                        shared_hidden(n)
                if ly.i == 1:
                    all_exp = flat(full, NT * E1, NT * E1)
                    act.activation(all_exp, all_exp, ACT.Exp).then_inc(ls.exped, 1)

                def transpose_out(t0, u):
                    act.wait_ge(lp.xgT_psum, t0 + (ly.done + u + 1))
                    if not first_tiles(t0, u, 2):
                        act.wait_ge(lp.h_psum, t0 + (ly.done + u - 1))
                    act.copy(flat(xgT, 2 * P, (u % 2) * 2 * P), bank[:, u % 2, 0:2 * P]).then_inc(lp.xgT_made, 1)

                def tile(t0, u):
                    if exists(ly, *at(t0, u, 1)):
                        transpose_out(*at(t0, u, 1))
                    if ly.i == 1:
                        act.wait_ge(lp.h_psum, t0 + (ly.done + u + 1))
                        if not first_tiles(t0, u, 2):
                            act.wait_ge(lp.hid_made, t0 + (ly.done + u - 1))
                        act.activation(gate_th[:, u % 2], bank[:, 2 + u % 2, 0:H1], ACT.Tanh,
                                       scale=0.5).then_inc(lp.gate_made, 1)
                    if exists(ly, *at(t0, u, -1)):
                        hidden_out(*at(t0, u, -1))

                def hidden_out(t0, u):
                    act.wait_ge(lp.hidT_psum, t0 + (ly.done + u + 1))
                    if not first_tiles(t0, u, 2):
                        act.wait_ge(lp.y_psum, t0 + (ly.done + u - 1))
                    if ly.i == 0:
                        act.activation(hidT[0:HH, u % 2].rearrange("p k r -> p (k r)"), bank[0:HH, 4 + u % 2, 0:2 * P],
                                       ACT.Relu).then_inc(lp.hidT_made, 1)
                    else:
                        act.copy(hidT[:, u % 2, 0], bank[:, 4 + u % 2, 0:P]).then_inc(lp.hidT_made, 1)

                if ly.i == 0:
                    act.wait_ge(a.hidT_ones, 1)
                transpose_out(0, 0)
                turns(act, ly, tile)
                hidden_out(ly.last, U - 2)

        @block.tensor
        def _(pe):
            pe.wait_ge(s.consts, 2)
            pe.wait_ge(s.ctx_in, 16)
            for j in range(NT):
                mm = pe.transpose(bank[:, j // 4, (j % 4) * P:(j % 4 + 1) * P], ctx_nat[:, j, :], ident[:])
                if j % 4 == 3:
                    mm.then_inc(s.ctxT_psum, 1)
            pe.wait_ge(s.wcv_made, 2 * TAPS)
            for k in range(TAPS):
                for h in range(2):
                    c = (k % 2) * 2 + h
                    mm = pe.transpose(bank[:, 2 + k // 2, c * P:(c + 1) * P], wcv[:, h, k, :], ident[:])
                if k % 2 == 1:
                    mm.then_inc(s.wcT_psum, 1)
            pe.wait_ge(s.mamba_in, 128)
            for h in range(2):
                pe.transpose(bank[:, 4, h * (DR + NB):(h + 1) * (DR + NB)], xpw[:, h * P:(h + 1) * P],
                             ident[0:DR + NB, 0:DR + NB])
                mm = pe.transpose(bank[0:DR, 4, (1 + h) * P:(2 + h) * P], dtw[:, h, :], ident[:])
            mm.then_inc(s.xw_psum, 1)
            pe.wait_ge(s.wcT_made, 2)
            pe.wait_ge(s.ctxT_made, 2)
            for q in range(4):
                p, h = q // 2, q % 2
                for k in range(TAPS):
                    mm = pe.matmul(bank[:, CONV_BANK[q]], wcT[:, k, h, :], ctxT[:, 2 * p:2 * p + 2, k:k + L],
                                   start=k == 0, stop=k == TAPS - 1)
                mm.then_inc(s.conv_psum, 1)
            pe.wait_ge(s.xw_made, 6)
            for p in range(2):
                pe.wait_ge(s.u_made, 2 * p + 2)
                for h in range(2):
                    mm = pe.matmul(bank[:, 1 + p], wxT[:, h, :], cu[:, h, cols(p)], start=h == 0, stop=h == 1)
                mm.then_inc(s.xp_psum, 1)
                pe.wait_ge(s.dtl_made, p + 1)
                for h in range(2):
                    pe.matmul(bank[:, CONV_BANK[2 * p + h]], dtpT[:, h, :], dtl[:, cols(p)],
                              start=True, stop=True).then_inc(s.dpre_psum, 1)

            pick = eye3[:].rearrange("k (m i) -> k m i", i=2)

            def broadcast_b(p, t, m, slot):
                if not (isinstance(t, int) and t < 2):
                    pe.wait_ge(s.b_copied, t - 1)
                pe.matmul(bank[:, 1 + slot], pick[:, bass.ds(m, 1), slot].to_broadcast([P, P]), bcp[:, cols(p)],
                          start=True, stop=True).then_inc(s.b_bcast, 1)

            def broadcast_c(p, t, m, slot):
                if not (isinstance(t, int) and t < 2):
                    pe.wait_ge(s.prod_made, 2 * (t - 1))
                pe.matmul(bank[:, 3 + slot], pick[:, bass.ds(m + DS // 2, 1), slot].to_broadcast([P, P]), bcp[:, cols(p)],
                          start=True, stop=True).then_inc(s.c_bcast, 1)

            def ysum(p, t, slot, stop=False):
                for h in range(2):
                    pe.wait_ge(s.prod_made, 2 * t + h + 1)
                    pe.matmul(bank[:, Y_BANK[p][h]], ident[:], prod[:, slot, h], start=False,
                              stop=stop).then_inc(s.y_summed, 1)

            pe.wait_ge(s.dg_made, 2)
            pe.wait_ge(s.abs_made, 8)
            pe.wait_ge(s.hi_made, 4)
            pe.wait_ge(s.parts_made, 8)
            def start_y(p):
                for h in range(2):
                    pe.matmul(bank[:, Y_BANK[p][h]], dg[:, h, :], cu[:, h, cols(p)], start=True, stop=False)

            def gated_back(p):
                pe.wait_ge(s.gated, 2 * p + 2)
                for b in range(2):
                    for lt in range(2):
                        for h in range(2):
                            mm = pe.transpose(bank[:, Y_BANK[p][b], lt * DM + h * P:lt * DM + (h + 1) * P],
                                              sz[:, 4 * p + 2 * b + h, lt * P:(lt + 1) * P], ident[:])
                    mm.then_inc(s.mix_psum, 1)

            start_y(0)
            broadcast_b(0, 0, 0, 0)
            broadcast_b(0, 1, 0, 1)
            broadcast_c(0, 0, 0, 0)
            for p in range(2):
                t0 = p * DS

                def two_steps(m):
                    for i in range(2):
                        broadcast_b(p, 2 * m + (t0 + 2 + i), m + 1, i)
                        broadcast_c(p, 2 * m + (t0 + 1 + i), m + i, 1 - i)
                        ysum(p, 2 * m + (t0 + i), i)

                two_steps(0)
                if p == 1:
                    gated_back(0)
                with pe.Fori(1, DS // 2 - 1) as m:
                    two_steps(m)
                broadcast_c(p, t0 + DS - 1, DS // 2 - 1, 1)
                if p == 0:
                    broadcast_b(1, DS, 0, 0)
                    broadcast_b(1, DS + 1, 0, 1)
                ysum(p, t0 + DS - 2, 0)
                if p == 0:
                    broadcast_c(1, DS, 0, 0)
                ysum(p, t0 + DS - 1, 1, stop=True)
                if p == 0:
                    start_y(1)
            gated_back(1)

            def turn(n):
                j = norm_order[n - 1][1]
                pe.wait_ge(norm.normed, n)
                if n > 2:
                    pe.wait_ge(norm.turned, n - 2)
                for k in range(2):
                    mm = pe.transpose(bank[:, 1 + n % 2, k * P:(k + 1) * P], xn[:, j, k * P:(k + 1) * P], ident[:])
                mm.then_inc(norm.turned_psum, 1)

            def router_logits(ly, j):
                router = (router0, router1)[ly.i]
                pe.wait_ge(norm.turned, moe_norm(ly, j))
                dst = bank[:, LOGIT_BANK[ly.i], j * ly.E:(j + 1) * ly.E]
                for k in range(2):
                    mm = pe.matmul(dst, xnT[:, k, j * P:(j + 1) * P], router[:, k, :], start=k == 0, stop=k == 1)
                if j == NT - 1:
                    mm.then_inc(ly.s.logits_psum, 1)

            def attend(j):
                pe.wait_ge(norm.turned, norm_count("attention", j))
                if j >= 2:
                    pe.wait_ge(a.x3_made, j - 1)
                for k in range(2):
                    mm = pe.matmul(bank[:, 5 + j % 2, 0:L], xnT[:, k, j * P:(j + 1) * P], attT[:, j // 2, k, :],
                                   start=k == 0, stop=k == 1)
                mm.then_inc(a.att_psum, 1)

            def shared_hidden(n):
                ls = layers[0].s
                em, c = n % 4, n // 4
                if n >= 2:
                    pe.wait_ge(ls.sh_made, n - 1)
                for k in range(2):
                    mm = pe.matmul(bank[0:HH, 3 + n % 2], sw1[:, em // 2 * 2 + k, em % 2 * HH:(em % 2 + 1) * HH],
                                   xnT[:, k, cols(c)], start=k == 0, stop=k == 1)
                mm.then_inc(ls.sh_psum, 1)

            def shared_gate_up(c, g, k):
                if c and k == 0:
                    pe.wait_ge(a.sh_copied, g + 1)
                mm = pe.matmul(bank[:, 3 + g], (swg, swu)[g][:, k, :], xnT[:, k, cols(c)], start=k == 0, stop=k == 1)
                if k == 1:
                    mm.then_inc(layers[1].s.sh_psum, 1)

            def shared_out(ly, j):
                dst = bank[:, BASE_BANK[ly.i][j // 2], j % 2 * DM:(j % 2 + 1) * DM]
                if ly.i == 0:
                    pe.wait_ge(ly.s.sh_made, NSH * 2 * (j // 4 + 1))
                    tok = slice(j % 4 * P, (j % 4 + 1) * P)
                    for em in range(NSH * 2):
                        K = HH + em % 2
                        mm = pe.matmul(dst, (shT, shT_late)[j // 4][0:K, em, tok], sw2[0:K, em // 2, em % 2, :],
                                       start=em == 0, stop=em == NSH * 2 - 1)
                else:
                    mm = pe.matmul(dst, shT1[:, j * P:(j + 1) * P], swd[:], start=True, stop=True)
                mm.then_inc(ly.s.base_psum, 1)

            for ly in layers:
                ls = ly.s
                if ly.i == 0:
                    pe.wait_ge(s.l0_in, 96)
                    turn(1)
                    for j in range(NT):
                        if j == 3:
                            pe.wait_ge(norm.turned, 4)
                            shared_hidden(0)
                        if j == 5:
                            shared_hidden(1)
                        if j < NT - 1:
                            turn(j + 2)
                        router_logits(ly, j)
                    for n in range(2, EARLY):
                        shared_hidden(n)
                else:
                    pe.wait_ge(s.att_in, 64)
                    pe.wait_ge(s.l1_in, 80)
                    pe.wait_ge(lp.y_made, layers[0].tiles)
                    for c, w in enumerate((wq, wk)):
                        pe.transpose(bank[:, 5, c * P:(c + 1) * P], w[:], ident[:])
                    for k in range(2):
                        mm = pe.transpose(bank[:, 5, 2 * P + k * E1:2 * P + (k + 1) * E1], wr_rows[:, k * P:(k + 1) * P],
                                          ident[0:E1, 0:E1])
                    mm.then_inc(a.wqkT_psum, 1)
                    pe.wait_ge(a.wqkT_made, 2)
                    for c in range(4):
                        p = c % 2
                        pe.matmul(bank[:, (5, 6, 7, 0)[c]], wqkT[:, c // 2, :], ctxT[:, 2 * p:2 * p + 2, TAPS - 1:],
                                  start=True, stop=True).then_inc(a.qk_psum, 1)
                    pe.wait_ge(a.qk_made, 4)
                    for n in range(2 * B + 2):
                        if n < 2 * B:
                            b = n // 2
                            if n >= 2:
                                pe.wait_ge(a.aexp_made, n - 1)
                            pe.matmul(bank[:, 5 + n % 2, 0:L], qT[:, n * P:(n + 1) * P], kT[:, b * L:(b + 1) * L],
                                      start=True, stop=True).then_inc(a.e_psum, 1)
                        if n >= 2:
                            i = n - 2
                            pe.wait_ge(a.att_made, i + 1)
                            if i >= 2:
                                pe.wait_ge(a.attT_made, i - 1)
                            for k in range(2):
                                mm = pe.transpose(bank[:, (7, 0)[i % 2], k * P:(k + 1) * P],
                                                  att[:, i % 2, k * P:(k + 1) * P], ident[:])
                            mm.then_inc(a.attT_psum, 1)
                    pe.wait_ge(a.attT_made, 2 * B)
                    for n in range(NT + 1, 3 * NT + 1):
                        kind, j = norm_order[n - 1]
                        turn(n)
                        if kind == "attention":
                            attend(j)
                        else:
                            router_logits(ly, j)
                            if 3 <= j < 7:
                                shared_gate_up(0, (j - 3) // 2, (j - 3) % 2)
                    shared_gate_up(1, 0, 0)
                    shared_gate_up(1, 0, 1)
                pe.wait_ge(ls.chosen_made, 1)
                W = NT * ly.E
                pe.matmul(bank[:, 6, 0:W], before[:], ly.chosen, start=True, stop=False)
                for d in range(1, NT):
                    mm = pe.matmul(bank[:, 6, d * ly.E:W], ones16[:], ly.chosen[:, 0:W - d * ly.E],
                                   start=False, stop=d == NT - 1)
                mm.then_inc(ls.rank_psum, 1)
                for j in range(NT):
                    mm = pe.matmul(bank[:, 7, 0:ly.E], ones16[:], ly.chosen[:, j * ly.E:(j + 1) * ly.E],
                                   start=j == 0, stop=j == NT - 1)
                mm.then_inc(ls.rank_psum, 1)
                if ly.i == 1:
                    shared_gate_up(1, 1, 0)
                    shared_gate_up(1, 1, 1)
                if ly.i == 0:
                    for n in range(EARLY, 2 * NSH * 2):
                        shared_hidden(n)
                    for j in range(OUTS_AHEAD):
                        shared_out(ly, j)
                for j in range(NT):
                    if ly.i == 0 and 1 <= j <= NT - OUTS_AHEAD:
                        shared_out(ly, j + OUTS_AHEAD - 1)
                    for k in range(ly.K):
                        n = j * ly.K + k
                        pools = POOL_CHOICES[ly.i]
                        if k in pools:
                            pe.wait_ge(ls.pool_hot_made, 2 * (j * len(pools) + pools.index(k) + 1))
                        else:
                            own = [c for c in range(ly.K) if c not in pools]
                            pe.wait_ge(ls.hot_made, 2 * (j * len(own) + own.index(k) + 1))
                        slot = map_slot(ly, j, k)
                        pe.matmul(bank[:, 0, 0:ly.tiles], slot_hot[:, slot, :], tile_tok[:, slot, 0:ly.tiles],
                                  start=n == 0, stop=n == NT * ly.K - 1).then_inc(ls.map_used, 1)
                    if ly.i == 1 and j >= 4:
                        pe.wait_ge(a.sh_half, 3)
                        pe.wait_ge(a.sh_copied, 4)
                        shared_out(ly, j - 4)
                pe.wait_ge(ls.owner_made, 1)
                pe.transpose(bank[0:1, 7, 0:P], owner[:], ident[:]).then_inc(ls.owner_psum, 1)
                if ly.i == 1:
                    pe.wait_ge(a.sh_half, 6)
                    for j in range(4, NT):
                        shared_out(ly, j)

                def rows_in(t0, u):
                    pe.wait_ge(lp.gathered[u % R], slot_count(ly, t0, u, 1))
                    if not first_tiles(t0, u, 2):
                        pe.wait_ge(lp.xgT_made, t0 + (ly.done + u - 1))
                    for k in range(2):
                        mm = pe.transpose(bank[:, u % 2, k * P:(k + 1) * P], xg[:, u % R, k * P:(k + 1) * P], ident[:])
                    mm.then_inc(lp.xgT_psum, 1)

                PE = mybir.EngineType.PE
                owners = [None] * U

                def down(t0, u):
                    e = owners[u]
                    pe.wait_ge(lp.hidT_made, t0 + (ly.done + u + 1))
                    if not first_tiles(t0, u, 2):
                        pe.wait_ge(lp.y_made, t0 + (ly.done + u - 1))
                    dst = bank[:, 6 + u % 2, 0:DM]
                    if ly.i == 0:
                        pe.matmul(dst, hidT[0:HH, u % 2, 0], w2[0:HH, bass.ds(e, 1), 0, :], start=True, stop=False)
                        mm = pe.matmul(dst, hidT[0:HH + 1, u % 2, 1], w2[0:HH + 1, bass.ds(e, 1), 1, :],
                                       start=False, stop=True)
                    else:
                        mm = pe.matmul(dst, hidT[:, u % 2, 0], wd[:, bass.ds(e, 1), :], start=True, stop=True)
                    mm.then_inc(lp.y_psum, 1)

                def tile(t0, u):
                    if exists(ly, *at(t0, u, 1)):
                        rows_in(*at(t0, u, 1))
                    if u == 0:
                        owners[0] = expert(PE, ly, t0, 0)
                    e = owners[u]
                    pe.wait_ge(lp.xgT_made, t0 + (ly.done + u + 1))
                    if not first_tiles(t0, u, 2):
                        pe.wait_ge(lp.hid_made, t0 + (ly.done + u - 1))
                    for k in range(2):
                        if ly.i == 0:
                            mm = pe.matmul(bank[:, 2 + u % 2, 0:H0], xgT[:, u % 2, k], w1[:, bass.ds(e, 1), k, :],
                                           start=k == 0, stop=k == 1)
                        else:
                            w = wgu[:].rearrange("p (e k) g i -> p e k (g i)", k=2)
                            mm = pe.matmul(bank[:, 2 + u % 2, 0:2 * H1], xgT[:, u % 2, k], w[:, bass.ds(e, 1), k, :],
                                           start=k == 0, stop=k == 1)
                    mm.then_inc(lp.h_psum, 1)
                    if u == 0 and exists(ly, *at(t0, 0, -1)):
                        for v in (U - 2, U - 1):
                            owners[v] = expert(PE, ly, t0 - U, v)
                    if u < U - 1 and exists(ly, *at(t0, u, 1)):
                        owners[u + 1] = expert(PE, ly, t0, u + 1)
                    if exists(ly, *at(t0, u, -1)):
                        hidden_in(*at(t0, u, -1))
                    if exists(ly, *at(t0, u, -2)):
                        down(*at(t0, u, -2))

                def hidden_in(t0, u):
                    pe.wait_ge(lp.hid_made, t0 + (ly.done + u + 1))
                    if not first_tiles(t0, u, 2):
                        pe.wait_ge(lp.hidT_made, t0 + (ly.done + u - 1))
                    if ly.i == 0:
                        for k in range(2):
                            mm = pe.transpose(bank[0:HH, 4 + u % 2, k * P:(k + 1) * P],
                                              hid[:, u % 2, k * HH:(k + 1) * HH], ident[:])
                    else:
                        mm = pe.transpose(bank[:, 4 + u % 2, 0:P], hid[:, u % 2, 0:H1], ident[:])
                    mm.then_inc(lp.hidT_psum, 1)

                pe.wait_ge(ls.tok_made, 1)
                pe.wait_ge(ls.owner_ready, 1)
                if ly.i == 0:
                    pe.wait_ge(s.w1_in, 64)
                    pe.wait_ge(s.w2_in, 80)
                else:
                    pe.wait_ge(a.wgu_in, 160)
                rows_in(0, 0)
                pe.wait_ge(ls.based, NT)
                turns(pe, ly, tile)
                hidden_in(ly.last, U - 2)
                down(ly.last, U - 3)
                down(ly.last, U - 2)

        @block.vector
        def _(dve):
            def link(ins):
                ins.then_inc(s.dve_step, 1)
                steps[0] += 1
                dve.wait_ge(s.dve_step, steps[0])

            steps = [0]
            dve.wait_ge(s.mamba_in, 128)
            for h in range(2):
                for k in range(TAPS):
                    dve.tensor_scalar(wcv[:, h, k, :], wip[:, h, :], cw[:, h, k:k + 1], None,
                                      ALU.mult).then_inc(s.wcv_made, 1)
            dve.tensor_scalar(hcb[:], cb[:], 0.5, None, ALU.mult).then_inc(s.hcb_made, 1)
            dve.memset(wxT[:, :, DR:NB], 0.0).then_inc(s.xw_made, 1)
            dve.wait_ge(s.wcT_psum, 2)
            dve.tensor_copy(flat(wcT, CH, CH), bank[:, 3]).then_inc(s.wcT_made, 1)
            dve.wait_ge(s.xw_psum, 1)
            xw = bank[:, 4, 0:2 * (DR + NB)].rearrange("p (h c) -> p h c", h=2)
            for r in range(1, 4):
                dve.tensor_copy(wxT[:, :, r * NB:(r + 1) * NB], xw[:, :, DR:]).then_inc(s.xw_made, 1)
            dve.tensor_copy(wxT[:, :, 0:DR], xw[:, :, 0:DR]).then_inc(s.xw_made, 1)
            dve.tensor_copy(dtpT[:], bank[0:DR, 4, P:3 * P].rearrange("p (h c) -> p h c", h=2)).then_inc(s.xw_made, 1)

            dve.wait_ge(s.x_in, 16)
            for j in range(NT):
                ins = dve.bn_stats(stats[:, j, :], xs[:, j, :])
            link(ins)
            for j in range(NT):
                ins = dve.bn_aggr(meanvar[:, j, :], stats[:, j, :])
            link(ins)
            dve.tensor_scalar(vareps[:], meanvar[:, :, 1], EPS_LN, None, ALU.add).then_inc(s.var_made, 1)
            dve.wait_ge(s.consts, 2)
            for h in range(2):
                dve.tensor_scalar(dg[:, h, :], ident[:], dsk[:, h:h + 1], None, ALU.mult).then_inc(s.dg_made, 1)

            dve.wait_ge(s.hcb_made, 1)

            def silu_u(q):
                p, h = q // 2, q % 2
                dve.wait_ge(s.th_made, q + 1)
                link(dve.tensor_scalar(cu[:, h, cols(p)], bank[:, CONV_BANK[q]], 0.5, hcb[:, h:h + 1],
                                       ALU.mult, ALU.add))
                dve.scalar_tensor_tensor(cu[:, h, cols(p)], th[:, h], 1.0, cu[:, h, cols(p)],
                                         ALU.add, ALU.mult).then_inc(s.u_made, 1)

            def silu_z(i):
                dve.wait_ge(s.z_th, i + 1)
                dve.scalar_tensor_tensor(flat(sz, CH, i * CH), ln_v[:, i], 1.0, flat(sz, CH, i * CH),
                                         ALU.add, ALU.mult).then_inc(s.z_made, 1)

            silu_u(0)
            dve.wait_ge(s.rstd_made, 1)
            for j in range(NT):
                dve.tensor_scalar(sz[:, j, :], xs[:, j, :], meanvar[:, j, 0:1], rstd[:, j:j + 1],
                                  ALU.subtract, ALU.mult).then_inc(s.z_normed, 1)
            silu_u(1)
            silu_z(0)
            silu_z(1)
            silu_u(2)
            silu_z(2)
            silu_z(3)
            silu_u(3)
            for p in range(2):
                dve.wait_ge(s.hi_made, 2 * p + 2)
                ps = bank[:, 1 + p]
                second, third = slice(2 * NB, 3 * NB), slice(3 * NB, P)
                dve.tensor_tensor(bcp[second, cols(p)], ps[second], part16[second], ALU.subtract).then_inc(s.parts_made, 1)
                dve.tensor_tensor(part[third], ps[third], part16[third], ALU.subtract).then_inc(s.parts_made, 1)
                dve.wait_ge(s.parts_made, 4 * p + 2)
                dve.tensor_copy(part16[third], part[third]).then_inc(s.parts_made, 1)
                dve.wait_ge(s.parts_made, 4 * p + 3)
                dve.tensor_tensor(bcp[third, cols(p)], part[third], part16[third], ALU.subtract).then_inc(s.parts_made, 1)
            def softplus_part(q):
                return delta[:, q % 2, cols(q // 2)]

            for q in range(5):
                if q < 4:
                    dve.wait_ge(s.exp_made, q + 1)
                    if q >= 2:
                        dve.wait_ge(s.low_added, q - 1)
                    dve.tensor_scalar(th[:, q % 2], exp_v[:, q], 1.0, -1.0, ALU.add, ALU.add).then_inc(s.w_made_1, 1)
                if q >= 1:
                    dve.wait_ge(s.low_made, q)
                    d = softplus_part(q - 1)
                    dve.tensor_tensor(d, d, th[:, (q - 1) % 2], ALU.add).then_inc(s.low_added, 1)
            for q in range(5):
                if q < 4:
                    dve.wait_ge(s.ln_made, q + 1)
                    dve.wait_ge(s.low_added, q + 1)
                    d = softplus_part(q)
                    dve.tensor_tensor(d, d, ln_v[:, q], ALU.add).then_inc(s.delta_made, 1)
                if q >= 3:
                    h, part_of = (q - 1) % 2, cols((q - 1) // 2)
                    dve.wait_ge(s.delta_made, q)
                    dve.tensor_tensor(du[:, h, part_of], delta[:, h, part_of], cu[:, h, part_of],
                                      ALU.mult).then_inc(s.du2_made, 1)
            dve.wait_ge(s.du2_made, 2)
            dve.memset(decay[:, :, :, :, 0:1].rearrange("p a b c o -> p (a b c) o"), 0.0).then_inc(s.region_free, 1)

            def step(p, t, slot):
                for h in range(2):
                    dve.wait_ge(s.decay_made, 2 * t + h + 1)
                    dve.wait_ge(s.inflow_made, 2 * t + h + 1)
                    if not (isinstance(t, int) and t < 1):
                        dve.wait_ge(s.prod_made, 2 * (t - 1) + h + 1)
                    dve.tensor_tensor_scan(state[:, h], decay[:, slot, h].rearrange("p b l -> p (b l)"),
                                           inflow[:, slot, h], 0.0, ALU.mult, ALU.add).then_inc(s.scanned, 1)
                for h in range(2):
                    if h == 0:
                        dve.wait_ge(s.c_bcast, t + 1)
                    dve.wait_ge(s.scanned, 2 * t + h + 1)
                    if not (isinstance(t, int) and t < 2):
                        dve.wait_ge(s.y_summed, 2 * (t - 2) + h + 1)
                    dve.tensor_tensor(prod[:, slot, h], state[:, h], bank[:, 3 + slot],
                                      ALU.mult).then_inc(s.prod_made, 1)

            dve.wait_ge(s.region_free, 1)
            dve.wait_ge(s.gates_made, 1)
            link(dve.tensor_scalar(hg[:], gates[:, 0:1], 0.5, None, ALU.mult))

            def mark(ins):
                ins.then_inc(s.dve_step, 1)
                steps[0] += 1
                return steps[0]

            def norm_stats(j):
                return mark(dve.bn_stats(stats[:, j, :], xs[:, j, :]))

            def norm_var(j, stats_made):
                dve.wait_ge(s.dve_step, stats_made)
                dve.bn_aggr(meanvar[:, j, :], stats[:, j, :]).then_inc(norm.var_found, 1)

            def norm_rstd(kind, j):
                dve.wait_ge(norm.std_found, norm_count(kind, j))
                return mark(dve.reciprocal(rstd[:, j:j + 1], std[:, j:j + 1]))

            def norm_out(j, rstd_made):
                dve.wait_ge(s.dve_step, rstd_made)
                dve.tensor_scalar(xn[:, j, :], xs[:, j, :], meanvar[:, j, 0:1], rstd[:, j:j + 1],
                                  ALU.subtract, ALU.mult).then_inc(norm.normed, 1)

            def normalise(kind, tiles):
                made = [norm_stats(j) for j in tiles]
                for j, m in zip(tiles, made):
                    norm_var(j, m)
                made = [norm_rstd(kind, j) for j in tiles]
                for j, m in zip(tiles, made):
                    norm_out(j, m)

            def gate(p):
                dve.wait_ge(s.y_summed, 2 * (p + 1) * DS)
                dve.wait_ge(s.z_made, 4)
                for h in range(2):
                    z = sz[:, 4 * p + h:4 * p + 4:2, :]
                    dve.tensor_tensor(z, z, bank[:, Y_BANK[p][h]].rearrange("p (b l) -> p b l", b=2),
                                      ALU.mult).then_inc(s.gated, 1)

            def mix(p, b):
                j = 4 * p + 2 * b
                dve.wait_ge(s.mix_psum, 2 * p + b + 1)
                dve.scalar_tensor_tensor(flat(xs, CH, j * DM), bank[:, Y_BANK[p][b]], hg[:, 0:1],
                                         flat(xs, CH, j * DM), ALU.mult, ALU.add).then_inc(s.x1_made, 1)

            for p in range(2):
                t0 = p * DS
                for i in range(2):
                    step(p, t0 + i, i)
                if p == 1:
                    gate(0)
                with dve.Fori(1, DS // 2) as m:
                    for i in range(2):
                        step(p, 2 * m + (t0 + i), i)
            for b in range(2):
                mix(0, b)
            dve.wait_ge(s.x1_made, 2)
            normalise("moe0", (0, 1))
            gate(1)
            normalise("moe0", (2, 3))
            for b in range(2):
                mix(1, b)
                dve.wait_ge(s.x1_made, 3 + b)
                normalise("moe0", (4 + 2 * b, 5 + 2 * b))
            dve.wait_ge(s.x1_made, 4)
            for g in range(2):
                dve.tensor_scalar(hg_moe[:, g:g + 1], gates[:, 2 + g:3 + g], 0.5, None, ALU.mult).then_inc(a.hg_made, 1)

            def add_row(ly, j, k):
                if j == NT - 1:
                    dve.wait_ge(ly.s.last_in[k], 16)
                elif k == 0:
                    dve.wait_ge(ly.s.got_in[j % 4], 16 * ly.K * (j // 4 + 1))
                if k > 0:
                    dve.wait_ge(ly.s.added, all_added(ly, j - 1) + k)
                dve.scalar_tensor_tensor(xs[:, j, :], got[:, j % 4, k, :], ly.wgt_g[:, j, k:k + 1], xs[:, j, :],
                                         ALU.mult, ALU.add).then_inc(ly.s.added, 1)

            def add_attention(i):
                dve.wait_ge(a.att_psum, i + 1)
                dve.scalar_tensor_tensor(xs[:, i, :], bank[:, 5 + i % 2, 0:L], gates[:, 1:2], xs[:, i, :],
                                         ALU.mult, ALU.add).then_inc(a.x3_made, 1)

            def combine_step(j):
                ly, i, prev = layers[0], j - 2, j - 1
                with_prev, with_i, with_rows = 1 <= j <= NT, i >= 0, j < NT
                if with_prev:
                    dve.wait_ge(ly.s.added, all_added(ly, prev))
                    prev_stats = norm_stats(prev)
                if with_i:
                    add_attention(i)
                if with_prev:
                    norm_var(prev, prev_stats)
                if with_i:
                    dve.wait_ge(a.x3_made, i + 1)
                    i_stats = norm_stats(i)
                    norm_var(i, i_stats)
                if with_prev:
                    prev_rstd = norm_rstd("attention", prev)
                    norm_out(prev, prev_rstd)
                if with_rows:
                    add_row(ly, j, 0)
                if with_i:
                    i_rstd = norm_rstd("moe1", i)
                if with_rows:
                    add_row(ly, j, 1)
                if with_i:
                    norm_out(i, i_rstd)
                if with_rows:
                    for k in range(2, ly.K):
                        add_row(ly, j, k)

            for ly in layers:
                ls = ly.s
                if ly.i == 1:
                    dve.wait_ge(a.wqkT_psum, 1)
                    dve.tensor_copy(flat(wqkT, 2 * P), bank[:, 5, 0:2 * P]).then_inc(a.wqkT_made, 1)
                    dve.tensor_copy(flat(router1, 2 * E1), bank[:, 5, 2 * P:2 * P + 2 * E1]).then_inc(a.wqkT_made, 1)
                    for n in range(2 * B + 1):
                        if n < 2 * B:
                            dve.wait_ge(a.e_psum, n + 1)
                            dve.tensor_reduce(att_neg[:, n:n + 1], bank[:, 5 + n % 2, 0:L], AX.X, ALU.max,
                                              negate=True).then_inc(a.neg_made, 1)
                        if n >= 1:
                            i = n - 1
                            dve.wait_ge(a.aexp_made, i + 1)
                            dve.reciprocal(att_rec[:, i:i + 1], att_sum[:, i:i + 1]).then_inc(a.rec_made, 1)
                            dve.wait_ge(a.rec_made, i + 1)
                            dve.tensor_scalar(att[:, i % 2], att[:, i % 2], att_rec[:, i:i + 1], None,
                                              ALU.mult).then_inc(a.att_made, 1)

                    for j in range(COMBINE_STEPS):
                        combine_step(j)

                E, K = ly.E, ly.K
                dve.wait_ge(ls.logits_psum, 1)
                dve.wait_ge((s.l0_in, s.l1_in)[ly.i], (96, 80)[ly.i])
                link(dve.tensor_tensor(ly.logits, bank[:, LOGIT_BANK[ly.i], 0:NT * E].rearrange("p (j e) -> p j e", e=E),
                                       (rbias0, rbias1)[ly.i][:].unsqueeze(1).to_broadcast([P, NT, E]), ALU.add))
                for j in range(NT):
                    ins = dve.max(top[:, j, :], ly.logits[:, j, :])
                link(ins)
                for j in range(NT):
                    ins = dve.max_index(topi[:, j, :], top[:, j, :], ly.logits[:, j, :])
                link(ins)
                largest = top[:, :, 0:1]
                ins = dve.tensor_tensor(ly.wexp, top[:, :, 0:K], largest.to_broadcast([P, NT, K]), ALU.subtract)
                all_exp = flat(full, NT * E1, NT * E1).rearrange("p (j e) -> p j e", e=E1)
                if ly.i == 1:
                    ins = dve.tensor_tensor(all_exp, ly.logits, largest.to_broadcast([P, NT, E]), ALU.subtract)
                ins.then_inc(ls.shifted, 1)
                link(dve.tensor_copy(topf[:], topi[:]))
                link(dve.tensor_tensor(ly.hot, iota_f[:, 0:E].unsqueeze(1).unsqueeze(1).to_broadcast([P, NT, K, E]),
                                       topf[:, :, 0:K].unsqueeze(3).to_broadcast([P, NT, K, E]), ALU.is_equal))
                with nc.allow_low_precision(reason="sums of zeros and one one"):
                    dve.tensor_reduce(ly.chosen.rearrange("p (j e) -> p j e", e=E),
                                      ly.hot.rearrange("p j k e -> p j e k"), AX.X, ALU.add).then_inc(ls.chosen_made, 1)
                dve.wait_ge(ls.rank_psum, 2)
                link(dve.tensor_tensor(ly.full, bank[:, 7, 0:E].unsqueeze(2).to_broadcast([P, E, NT]),
                                       fill_f[:].unsqueeze(1).to_broadcast([P, E, NT]), ALU.is_gt))
                link(dve.tensor_reduce(ntiles[:, 0:E], ly.full, AX.X, ALU.add))
                link(dve.tensor_tensor_scan(tile_end[:, 0:E], ntiles[:, 0:E], ntiles[:, 0:E], 0.0, ALU.add, ALU.max))
                link(dve.tensor_scalar(ended[:, 0:E], tile_end[:, 0:E], tokid[:, 0:1], None, ALU.is_le))
                link(dve.tensor_reduce(owner[:], ended[:, 0:E], AX.X, ALU.add))
                dve.tensor_scalar(owner[:], owner[:], float(E - 1), None, ALU.min).then_inc(ls.owner_made, 1)
                link(dve.tensor_tensor(row0[:, 0:E], tile_end[:, 0:E], ntiles[:, 0:E], ALU.subtract))
                link(dve.tensor_scalar(row0[:, 0:E], row0[:, 0:E], float(P), None, ALU.mult))
                link(dve.tensor_tensor(ly.posf, bank[:, 6, 0:NT * E].rearrange("p (j e) -> p j e", e=E),
                                       row0[:, 0:E].unsqueeze(1).to_broadcast([P, NT, E]), ALU.add))
                link(dve.tensor_tensor(ly.hot, ly.hot, ly.posf.unsqueeze(2).to_broadcast([P, NT, K, E]), ALU.mult))
                link(dve.tensor_reduce(ly.rowf.rearrange("p (j k) -> p j k", k=K), ly.hot, AX.X, ALU.add))
                rows = flat(row_i, NT * K)
                link(dve.tensor_copy(rows, ly.rowf))
                dve.tensor_scalar(ly.tile_i, rows, P.bit_length() - 1, None, ALU.logical_shift_right)
                link(dve.tensor_scalar(ly.slot_i, rows, P - 1, None, ALU.bitwise_and))
                dve.tensor_copy(flat(tile_f, NT * K), ly.tile_i)
                link(dve.tensor_copy(flat(slot_f, NT * K), ly.slot_i))

                group = (2, 4)[ly.i]
                back = (1, 2)[ly.i]

                slot_of = ly.slot_f.rearrange("p (m q) k -> p m q k", q=group)
                tile_of = ly.tile_f.rearrange("p (m q) k -> p m q k", q=group)
                token_of = tokid[:].rearrange("p (m q) -> p m q", q=group)

                def choices(m):
                    turn = bass.ds(m, 1)
                    for q in range(group):
                        for k in range(K):
                            if k in POOL_CHOICES[ly.i]:
                                continue
                            slot = map_slot(ly, q, k)
                            if not (isinstance(m, int) and m == 0 and q < back):
                                dve.wait_ge(ls.map_used, m * (group * K) + ((q - back) * K + k + 1))
                            dve.tensor_scalar(slot_hot[:, slot, :], iota_h[:], slot_of[:, turn, q, k], None,
                                              ALU.is_equal).then_inc(ls.hot_made, 1)
                            dve.tensor_scalar(tile_tok[:, slot, 0:ly.tiles], iota_h[:, 0:ly.tiles],
                                              tile_of[:, turn, q, k], token_of[:, turn, q], ALU.is_equal, ALU.mult
                                              ).then_inc(ls.hot_made, 1)

                choices(0)
                if NT // group > 2:
                    with dve.Fori(1, NT // group) as m:
                        choices(m)
                else:
                    choices(1)
                dve.wait_ge(ls.map_used, NT * K)
                dve.tensor_copy(tok_of[:, 0:ly.tiles], bank[:, 0, 0:ly.tiles]).then_inc(ls.tok_made, 1)
                dve.wait_ge(ls.owner_psum, 1)
                dve.tensor_copy(owner_i[:], bank[0:1, 7, 0:P]).then_inc(ls.owner_ready, 1)

                for j in range(NT):
                    dve.wait_ge(ls.base_psum, j // 2 * 2 + 2)
                    dve.scalar_tensor_tensor(xs[:, j, :], bank[:, BASE_BANK[ly.i][j // 2], j % 2 * DM:(j % 2 + 1) * DM],
                                             hg_moe[:, ly.i:ly.i + 1], xs[:, j, :], ALU.mult, ALU.add
                                             ).then_inc(ls.based, 1)
                if ly.i == 0:
                    dve.wait_ge(s.b1_in, 16)
                    dve.memset(hidT[64:HH + 1], 1.0).then_inc(a.hidT_ones, 1)
                dve.wait_ge(ls.owner_ready, 1)

                def y_out(t0, u):
                    dve.wait_ge(lp.y_psum, t0 + (ly.done + u + 1))
                    if not first_tiles(t0, u, R):
                        dve.wait_ge(lp.y_out[u % R], slot_count(ly, t0, u, 0))
                    dve.tensor_copy(yt[:, u % R, :], bank[:, 6 + u % 2, 0:DM]).then_inc(lp.y_made, 1)

                def tile(t0, u):
                    v = u % 2
                    if not first_tiles(t0, u, 2):
                        dve.wait_ge(lp.hidT_psum, t0 + (ly.done + u - 1))
                    if ly.i == 0:
                        e = expert(mybir.EngineType.DVE, ly, t0, u)
                        dve.wait_ge(lp.h_psum, t0 + (ly.done + u + 1))
                        dve.tensor_tensor(hid[:, v, 0:H0], bank[:, 2 + v, 0:H0], b1_bc[:, bass.ds(e, 1), :].squeeze(1),
                                          ALU.add).then_inc(lp.hid_made, 1)
                    else:
                        dve.wait_ge(lp.gate_made, t0 + (u + 1))
                        dve.scalar_tensor_tensor(hid[:, v, 0:H1], gate_th[:, v], 1.0, bank[:, 2 + v, 0:H1],
                                                 ALU.add, ALU.mult).then_inc(lp.half_made, 1)
                        dve.wait_ge(lp.half_made, t0 + (u + 1))
                        dve.tensor_tensor(hid[:, v, 0:H1], hid[:, v, 0:H1], bank[:, 2 + v, H1:2 * H1],
                                          ALU.mult).then_inc(lp.hid_made, 1)
                    if exists(ly, *at(t0, u, -2)):
                        y_out(*at(t0, u, -2))

                turns(dve, ly, tile)
                y_out(ly.last, U - 3)
                y_out(ly.last, U - 2)
                dve.wait_ge(ls.exped, 1 + ly.i)
                link(dve.tensor_reduce(wsum[:], ly.wexp, AX.X, ALU.add))
                if ly.i == 1:
                    link(dve.tensor_reduce(wall[:], all_exp, AX.X, ALU.add))
                    link(dve.scalar_tensor_tensor(wsum[:], wall[:], 1e-9, wsum[:], ALU.mult, ALU.add))
                link(dve.reciprocal(wrec[:], wsum[:]))
                link(dve.tensor_tensor(ly.wgt, ly.wexp, wrec[:].unsqueeze(2).to_broadcast([P, NT, K]), ALU.mult))
                dve.wait_ge(a.hg_made, 2)
                gate = (gates[:, 2:3], hg_moe[:, 1:2])[ly.i]
                link(dve.tensor_scalar(ly.wgt_g, ly.wgt, gate, None, ALU.mult))
            for j in range(NT):
                for k in range(K1):
                    add_row(layers[1], j, k)


_OUT = ((4, 256, 256), "float32")


def kernel(**inputs):
    import numpy as _np
    import concourse.bacc as _bacc
    from concourse.bass_utils import run_bass_kernel_spmd as _run

    nc = _bacc.Bacc("TRN2", target_bir_lowering=False, num_devices=1)
    arrays, io = {}, {}
    for name, value in inputs.items():
        value = _np.ascontiguousarray(value)
        arrays[f"in_{name}"] = value
        io[name] = nc.dram_tensor(f"in_{name}", value.shape, mybir.dt.from_np(value.dtype), kind="ExternalInput").ap()
    out = nc.dram_tensor("out_x", _OUT[0], F32, kind="ExternalOutput").ap()
    flamingo_two_layer_kernel(nc, io, out)
    result = _run(nc, [arrays], core_ids=[0])
    return result.results[0]["out_x"]
```
